# Optimizing a Trainium2 kernel written in Bass

```python
import numpy as np
import jax
import jax.numpy as jnp

def _softmax(x, axis=-1):
    return jax.nn.softmax(x, axis=axis)

def _gelu(x):
    return jax.nn.gelu(x, approximate=True)

def _silu(x):
    return jax.nn.silu(x)

def _sigmoid(x):
    return jax.nn.sigmoid(x)

def _layernorm(x, axis=-1, eps=1e-05):
    m = jnp.mean(x, axis=axis, keepdims=True)
    v = jnp.var(x, axis=axis, keepdims=True)
    return (x - m) / jnp.sqrt(v + eps)

def _scatter_add(tgt, idx, src, axis=0):
    return tgt.at[idx].add(src)

def _segment_sum(src, seg, n):
    return jax.ops.segment_sum(src, seg, n)
kernel_name = 'mk_gps_d1_gnn_r64_66391e'

def setup_inputs(seed: int=0):
    np.random.seed(seed)
    _w = jnp.asarray

    def _rec_inputs():
        import jax
        import jax.numpy as jnp
        _gk = jax.random.key(seed)
        x = -8.776e-05 + 1 * jax.random.normal(jax.random.fold_in(_gk, 1), (10000, 512), jnp.float32)
        src = jax.random.randint(jax.random.fold_in(_gk, 2), (2500,), 0, 10000, jnp.int32)
        dst = jnp.minimum((10000 * jax.random.uniform(jax.random.fold_in(_gk, 3), (2500,)) ** 2.0).astype(jnp.int32), 9999)
        _o = jnp.argsort(dst, stable=True)
        src = src[_o]
        dst = dst[_o]
        return (x, src, dst)
    x, src, dst = _rec_inputs()

    def _L0_gnn_setup():
        import jax, jax.numpy as jnp
        import numpy as np
        key = jax.random.key(seed)
        k1, k2, k3 = jax.random.split(key, 3)
        N, E, D = (10000, 2500, 512)
        x = jax.random.normal(k1, (N, D), dtype=jnp.float32)
        edge_index = jax.random.randint(k2, (2, E), 0, N, dtype=jnp.int64)
        W = jax.random.normal(k3, (D, D), dtype=jnp.float32) * (1.0 / np.sqrt(D))
        b = jnp.zeros((D,), dtype=jnp.float32)
        return {'x': x, 'edge_index': edge_index, 'W': W, 'b': b}
    _L0_gnn_all = _L0_gnn_setup()
    _L0_gnn_in = {k: v for k, v in _L0_gnn_all.items() if k in ('W', 'b')}
    del _L0_gnn_all

    def _L0_mix_setup():
        import jax, jax.numpy as jnp
        import numpy as np
        DIM = 512
        HEADS = 8
        DIM_HEAD = 64
        SLICE = 32
        INNER = HEADS * DIM_HEAD
        key = jax.random.key(seed)
        ks = jax.random.split(key, 8)
        B, N = (8, 128)
        s = 0.02
        return {'x': jax.random.normal(ks[0], (B, N, DIM), dtype=jnp.float32), 'W_in': jax.random.normal(ks[1], (DIM, INNER), dtype=jnp.float32) * s, 'b_in': jnp.zeros((INNER,), dtype=jnp.float32), 'Wq': jax.random.normal(ks[2], (DIM_HEAD, SLICE), dtype=jnp.float32) * s, 'Wk': jax.random.normal(ks[3], (DIM_HEAD, SLICE), dtype=jnp.float32) * s, 'Wv': jax.random.normal(ks[4], (DIM_HEAD, DIM_HEAD), dtype=jnp.float32) * s, 'W_out': jax.random.normal(ks[5], (INNER, DIM), dtype=jnp.float32) * s, 'b_out': jnp.zeros((DIM,), dtype=jnp.float32)}
    _L0_mix_all = _L0_mix_setup()
    _L0_mix_in = {k: v for k, v in _L0_mix_all.items() if k in ('W_in', 'b_in', 'Wq', 'Wk', 'Wv', 'W_out', 'b_out')}
    del _L0_mix_all

    def _L0_ffn_setup():
        import jax, jax.numpy as jnp
        import numpy as np
        EPS = 1e-05
        TOP_K = 2

        def layer_norm(x, g, b):
            m = x.mean(-1, keepdims=True)
            v = ((x - m) ** 2).mean(-1, keepdims=True)
            return (x - m) / jnp.sqrt(v + EPS) * g + b
        key = jax.random.key(seed)
        ks = jax.random.split(key, 8)
        B, S, D, E, H = (8, 512, 512, 8, 32)
        x = jax.random.normal(ks[0], (B, S, D), dtype=jnp.float32)
        Wg = jax.random.normal(ks[1], (D, E), dtype=jnp.float32) * 0.02
        W1 = jax.random.normal(ks[2], (E, D, H), dtype=jnp.float32) * 0.02
        b1 = jnp.zeros((E, H), dtype=jnp.float32)
        W2 = jax.random.normal(ks[3], (E, H, D), dtype=jnp.float32) * 0.02
        b2 = jnp.zeros((E, D), dtype=jnp.float32)
        ln_g = jnp.ones((D,), dtype=jnp.float32)
        ln_b = jnp.zeros((D,), dtype=jnp.float32)
        out_g = jnp.ones((D,), dtype=jnp.float32)
        out_b = jnp.zeros((D,), dtype=jnp.float32)
        return {'x': x, 'Wg': Wg, 'W1': W1, 'b1': b1, 'W2': W2, 'b2': b2, 'ln_g': ln_g, 'ln_b': ln_b, 'out_g': out_g, 'out_b': out_b}
    _L0_ffn_all = _L0_ffn_setup()
    _L0_ffn_in = {k: v for k, v in _L0_ffn_all.items() if k in ('Wg', 'W1', 'b1', 'W2', 'b2', 'ln_g', 'ln_b', 'out_g', 'out_b')}
    del _L0_ffn_all
    return {'x': x, 'src': src, 'dst': dst, 'L0_gnn_W': _L0_gnn_in['W'], 'L0_gnn_b': _L0_gnn_in['b'], 'L0_mix_W_in': _L0_mix_in['W_in'], 'L0_mix_b_in': _L0_mix_in['b_in'], 'L0_mix_Wq': _L0_mix_in['Wq'], 'L0_mix_Wk': _L0_mix_in['Wk'], 'L0_mix_Wv': _L0_mix_in['Wv'], 'L0_mix_W_out': _L0_mix_in['W_out'], 'L0_mix_b_out': _L0_mix_in['b_out'], 'L0_ffn_Wg': _L0_ffn_in['Wg'], 'L0_ffn_W1': _L0_ffn_in['W1'], 'L0_ffn_b1': _L0_ffn_in['b1'], 'L0_ffn_W2': _L0_ffn_in['W2'], 'L0_ffn_b2': _L0_ffn_in['b2'], 'L0_ffn_ln_g': _L0_ffn_in['ln_g'], 'L0_ffn_ln_b': _L0_ffn_in['ln_b'], 'L0_ffn_out_g': _L0_ffn_in['out_g'], 'L0_ffn_out_b': _L0_ffn_in['out_b']}

def reference(x, src, dst, L0_gnn_W, L0_gnn_b, L0_mix_W_in, L0_mix_b_in, L0_mix_Wq, L0_mix_Wk, L0_mix_Wv, L0_mix_W_out, L0_mix_b_out, L0_ffn_Wg, L0_ffn_W1, L0_ffn_b1, L0_ffn_W2, L0_ffn_b2, L0_ffn_ln_g, L0_ffn_ln_b, L0_ffn_out_g, L0_ffn_out_b):
    import jax
    import jax.numpy as jnp

    def _L0_gnn_ref(x, edge_index, W, b):
        import jax, jax.numpy as jnp
        import numpy as np
        N = x.shape[0]
        loop = jnp.arange(N, dtype=edge_index.dtype)
        src = jnp.concatenate([edge_index[0], loop])
        dst = jnp.concatenate([edge_index[1], loop])
        deg = jax.ops.segment_sum(jnp.ones(src.shape, dtype=x.dtype), dst, num_segments=N)
        deg_inv_sqrt = jnp.where(deg > 0, jax.lax.rsqrt(deg), 0.0)
        norm = deg_inv_sqrt[src] * deg_inv_sqrt[dst]
        h = x @ W
        msg = h[src] * norm[:, None]
        out = jax.ops.segment_sum(msg, dst, num_segments=N) + b
        return out

    def _L0_mix_ref(x, W_in, b_in, Wq, Wk, Wv, W_out, b_out):
        import jax, jax.numpy as jnp
        import numpy as np
        DIM = 512
        HEADS = 8
        DIM_HEAD = 64
        SLICE = 32
        INNER = HEADS * DIM_HEAD
        B, N, C = x.shape
        x_mid = (x @ W_in + b_in).reshape(B, N, HEADS, DIM_HEAD).transpose(0, 2, 1, 3)
        q = x_mid @ Wq
        k = x_mid @ Wk
        v = x_mid @ Wv
        q = jax.nn.softmax(q, axis=-1)
        k = jax.nn.softmax(k, axis=-2)
        kv = jnp.einsum('bhns,bhnc->bhsc', k, v)
        qkv = jnp.einsum('bhns,bhsc->bhnc', q, kv)
        qkv = qkv.transpose(0, 2, 1, 3).reshape(B, N, INNER)
        return qkv @ W_out + b_out

    def _L0_ffn_ref(x, Wg, W1, b1, W2, b2, ln_g, ln_b, out_g, out_b):
        import jax, jax.numpy as jnp
        import numpy as np
        EPS = 1e-05
        TOP_K = 2

        def layer_norm(x, g, b):
            m = x.mean(-1, keepdims=True)
            v = ((x - m) ** 2).mean(-1, keepdims=True)
            return (x - m) / jnp.sqrt(v + EPS) * g + b
        xn = layer_norm(x, ln_g, ln_b)
        logits = jnp.einsum('bsd,de->bse', xn, Wg)
        probs = jax.nn.softmax(logits, axis=-1)
        top_p, top_i = jax.lax.top_k(probs, TOP_K)
        conf = top_p / top_p.sum(-1, keepdims=True)
        h = jax.nn.gelu(jnp.einsum('bsd,edh->bseh', xn, W1) + b1)
        o = jnp.einsum('bseh,ehd->bsed', h, W2) + b2
        sel = jnp.take_along_axis(o, top_i[..., None], axis=2)
        combined = jnp.einsum('bskd,bsk->bsd', sel, conf)
        return layer_norm(x + combined, out_g, out_b)
    edge_index = jnp.stack([src, dst])
    xn = _layernorm(x, axis=-1)
    x = x + _L0_gnn_ref(xn, edge_index, L0_gnn_W, L0_gnn_b) + _L0_mix_ref(xn[None], L0_mix_W_in, L0_mix_b_in, L0_mix_Wq, L0_mix_Wk, L0_mix_Wv, L0_mix_W_out, L0_mix_b_out)[0]
    x = x + _L0_ffn_ref(_layernorm(x, axis=-1)[None], L0_ffn_Wg, L0_ffn_W1, L0_ffn_b1, L0_ffn_W2, L0_ffn_b2, L0_ffn_ln_g, L0_ffn_ln_b, L0_ffn_out_g, L0_ffn_out_b)[0]
    return x

_drawn_inputs = setup_inputs


def setup_inputs(seed=0):
    import zlib

    import numpy as np

    out = dict(_drawn_inputs(seed))
    spreads = {'L0_gnn_b': (0.0, 0.552),
     'L0_mix_b_in': (0.0, 0.8),
     'L0_mix_b_out': (0.0, 0.614),
     'L0_ffn_b1': (0.0, 2.0),
     'L0_ffn_b2': (0.0, 0.8),
     'L0_ffn_ln_g': (1.0, 0.6),
     'L0_ffn_ln_b': (0.0, 0.777),
     'L0_ffn_out_g': (1.0, 0.6),
     'L0_ffn_out_b': (0.0, 0.792)}
    factors = {'L0_mix_W_in': 8.0,
     'L0_mix_Wq': 8.0,
     'L0_mix_Wk': 8.0,
     'L0_mix_Wv': 8.0,
     'L0_mix_W_out': 8.0,
     'L0_ffn_W1': 6.218,
     'L0_ffn_W2': 5.845}
    for name, (base, spread) in spreads.items():
        noise = np.random.default_rng([zlib.crc32(name.encode()), seed]).standard_normal(out[name].shape)
        drawn = base * np.exp(spread * noise) if base else spread * noise
        out[name] = jnp.asarray(drawn.astype(out[name].dtype))
    for name, factor in factors.items():
        out[name] = (out[name] * factor).astype(out[name].dtype)
    return out
```

```python
from contextlib import ExitStack

import concourse.bass as bass
from concourse import mybir

ALU = mybir.AluOpType
ACT = mybir.ActivationFunctionType
AX = mybir.AxisListType
F32 = mybir.dt.float32
F16 = mybir.dt.float16
I32 = mybir.dt.int32
U32 = mybir.dt.uint32
ROP = bass.bass_isa.ReduceOp

P = 128
N, D = 10000, 512
EDGES = 2500
HEADS, HEAD, SLICE = 8, 64, 32
QC = HEADS * SLICE
EXPERTS, HID = 8, 32
HC = EXPERTS * HID
ZC = HC + EXPERTS
KD = D // P
PAIRS = HEADS // 2
TILES = -(-N // P)
TAIL = N - (TILES - 1) * P
ETILES = -(-EDGES // P)
ETAIL = EDGES - (ETILES - 1) * P
EPS = 1e-5
ACT_SCALE = 1024.0
W_TOP = 2.0 ** 14
EXP_MASK = 0x7F800000
SPARE = P


class Tile:

    def __init__(self, base, unroll=1, j=None):
        self.base, self.unroll, self.j = base, unroll, j
        self.n = base if j is None else j * unroll + base

    def slot(self, ring):
        return self.base % ring

    def uses(self, ring):
        if self.j is None:
            return self.base // ring
        return self.j * (self.unroll // ring) + self.base // ring

    def rows(self):
        return TAIL if self.j is None and self.base == TILES - 1 else P


def over_tiles(eng, unroll, stages):
    ahead, behind = max(o for o, _ in stages), min(o for o, _ in stages)
    start = unroll * -(-(unroll - behind) // unroll)
    count = (TILES - 1 - ahead - start) // unroll

    def peeled(lo, hi):
        for s in range(lo, hi):
            for o, body in stages:
                if 0 <= s + o < TILES:
                    body(Tile(s + o))

    peeled(-ahead, start)
    with eng.Fori(0, count) as j:
        for c in range(unroll):
            for o, body in stages:
                body(Tile(start + c + o, unroll, j))
    peeled(start + count * unroll, TILES - behind)


def stand_alone(eng):
    eng.nop(nofuse=True)


class Mem:

    def __init__(self, nc, stack, lasting):
        self.nc, self.stack, self.lasting, self.own = nc, stack, lasting, []

    def sb(self, name, shape, dt=F32):
        return self.stack.enter_context(self.nc.sbuf_tensor(name, shape, dt))

    def ps(self, name, shape, dt=F32):
        return self.stack.enter_context(self.nc.psum_tensor(name, shape, dt))

    def sem(self, name):
        handle = self.lasting.enter_context(self.nc.semaphore(name))
        self.own.append(handle)
        return handle

    def clear_sems(self):
        for handle in self.own:
            self.nc.gpsimd.sem_clear(handle)
        self.nc.all_engine_barrier()

    def sems(self, name, n):
        return [self.sem(f"{name}{i}") for i in range(n)]


class Arena(Mem):

    def __init__(self, nc, stack, lasting, tensor):
        super().__init__(nc, stack, lasting)
        self.flat, self.at = tensor[:].rearrange("p a b -> p (a b)"), 0

    def sb(self, name, shape, dt=F32):
        count = 1
        for n in shape[1:]:
            count *= n
        words = -(-count * (2 if dt == F16 else 4) // 4)
        view = self.flat[0:shape[0], self.at:self.at + words]
        self.at += words
        if dt != F32:
            view = view.bitcast(dt)
        if len(shape) == 3:
            view = view.rearrange("p (a b) -> p a b", a=shape[1])
        if len(shape) == 4:
            view = view.rearrange("p (a b c) -> p a b c", a=shape[1], b=shape[2])
        return view


class Chain:

    def __init__(self, eng, sem):
        self.eng, self.sem, self.n = eng, sem, 0

    def do(self, ins):
        self.n += 1
        return ins.then_inc(self.sem, 1)

    def settle(self):
        self.eng.wait_ge(self.sem, self.n)


def split(own, nc, jobs):
    for hi, lo, value, scale in jobs:
        own.do(nc.vector.tensor_scalar(hi, value, scale, None, ALU.mult))
    own.settle()
    for hi, lo, value, scale in jobs:
        own.do(nc.vector.scalar_tensor_tensor(lo, value, scale, hi, ALU.mult, ALU.subtract))


def power_of_two(nc, out, value):
    return nc.vector.tensor_scalar(out.bitcast(I32), value.bitcast(I32), EXP_MASK, None, ALU.bitwise_and)


def prepare(nc, keep, src, dst, W_gnn, W_in, b_in, Wq, Wk, dinv_table, y_table):
    with ExitStack() as st:
        m = Arena(nc, st, st, keep.k)
        win = m.sb("p_win", [P, KD, D])
        wg = m.sb("p_wg", [P, KD, D])
        winT = m.sb("p_winT", [P, PAIRS, D])
        wqk = m.sb("p_wqk", [P, KD, D])
        bd = m.sb("p_bd", [P, 2, 2, SLICE])
        bcol = m.sb("p_bcol", [P, PAIRS])
        bcolB = m.sb("p_bcolB", [P, PAIRS, 64])
        brow = m.sb("p_brow", [64, D])
        brow_hi = m.sb("p_brow_hi", [64, D], F16)
        peak = m.sb("p_peak", [P, 2])
        peakb = m.sb("p_peakb", [P, 1])
        peak_all = m.sb("p_peak_all", [P, 2])
        pow2 = m.sb("p_pow2", [P, 2])
        wscale = m.sb("p_wscale", [P, 2])
        dstrow = m.sb("p_dstrow", [P, ETILES * P], I32)
        iota_i = m.sb("p_iota_i", [P, P], I32)
        iota = m.sb("p_iota", [P, P])
        spare_i = m.sb("p_spare_i", [P, 1], I32)
        spare = m.sb("p_spare", [P, 1])
        earlier = m.sb("p_earlier", [P, P])
        junk = m.sb("p_junk", [P, P])
        part = m.sb("p_part", [P, 2, ETILES], I32)
        partf = m.sb("p_partf", [P, 2, ETILES])
        hot_lo = m.sb("p_hot_lo", [P, ETILES, P], F16)
        hot_hi = m.sb("p_hot_hi", [P, ETILES, TILES], F16)
        deg = m.sb("p_deg", [P, TILES])
        mhalf = m.sb("p_mhalf", [P, TILES])
        dinvT = m.sb("p_dinvT", [TILES, P])
        prev = m.sb("p_prev", [P, ETILES])
        move = m.sb("p_move", [P, ETILES])
        zero = m.sb("p_zero", [P, D])
        ps_t = m.ps("pp_t", [P, 2, D])
        ps_w = m.ps("pp_w", [P, 2, D])
        ps_b = m.ps("pp_b", [64, D])
        ps_d = m.ps("pp_d", [P, D])
        ps_i = m.ps("pp_i", [P, D])

        (win_in, wg_in, bd_in, bcol_in, edges_in, dstrow_in, dinv_out, spare_out) = (
            m.sem("p_" + n) for n in ("win_in", "wg_in", "bd_in", "bcol_in", "edges_in", "dstrow_in",
                                      "dinv_out", "spare_out"))
        (filled, ident_ok, earlier_ok, iota_ok, pool_own, peaks_ok, peak_all_ok, deg_ok, dinv_ok, dve_own,
         winT_ps, winT_ok, wqk_ps, wqk_ok, bcolB_ok, brow_ps, hot_ok, deg_ps, dinvT_ps, dinvT_ok,
         act_own) = (
            m.sem("p_" + n) for n in (
                "filled", "ident_ok", "earlier_ok", "iota_ok", "pool_own", "peaks_ok", "peak_all_ok", "deg_ok",
                "dinv_ok", "dve_own", "winT_ps", "winT_ok", "wqk_ps", "wqk_ok", "bcolB_ok", "brow_ps", "hot_ok",
                "deg_ps", "dinvT_ps", "dinvT_ok", "act_own"))

        with nc.Block() as block:
            @block.gpsimd
            def _(pool):
                own = Chain(pool, pool_own)
                own.do(nc.gpsimd.memset(keep.ident[:], 0.0))
                own.do(nc.gpsimd.memset(earlier[:], 1.0))
                nc.gpsimd.memset(bd[:], 0.0).then_inc(filled, 1)
                nc.gpsimd.memset(keep.src[:], 0).then_inc(filled, 1)
                nc.gpsimd.memset(keep.dst[:], N).then_inc(filled, 1)
                nc.gpsimd.memset(dstrow[:], N).then_inc(filled, 1)
                nc.gpsimd.memset(zero[:], 0.0).then_inc(filled, 1)
                own.do(nc.gpsimd.memset(keep.mhalf[:], -0.5))
                own.do(nc.gpsimd.memset(mhalf[:], -0.5))
                own.settle()
                nc.gpsimd.affine_select(out=keep.ident[:], in_=keep.ident[:], compare_op=ALU.not_equal,
                                        fill=1.0, base=0, pattern=[[-1, P]],
                                        channel_multiplier=1).then_inc(ident_ok, 1)
                nc.gpsimd.affine_select(out=earlier[:], in_=earlier[:], compare_op=ALU.is_gt, fill=0.0, base=0,
                                        pattern=[[-1, P]], channel_multiplier=1).then_inc(earlier_ok, 1)
                nc.gpsimd.iota(iota_i[:], [[1, P]], base=0, channel_multiplier=0).then_inc(iota_ok, 1)
                nc.gpsimd.iota(spare_i[:], [[1, 1]], base=N, channel_multiplier=1).then_inc(iota_ok, 1)
                pool.wait_ge(deg_ok, 1)
                nc.gpsimd.tensor_tensor(keep.dinv[:], deg[:], mhalf[:], ALU.pow).then_inc(dinv_ok, 1)
                pool.wait_ge(peaks_ok, 3)
                nc.gpsimd.partition_all_reduce(peak_all[:], peak[:], P, ROP.max).then_inc(peak_all_ok, 1)

            @block.sync
            def _(sp):
                sp.dma_start(win[:], W_in.rearrange("(k p) n -> p k n", p=P)).then_inc(win_in, 16)
                sp.dma_start(wg[:], W_gnn.rearrange("(k p) n -> p k n", p=P)).then_inc(wg_in, 16)
                sp.wait_ge(filled, 5)
                for h in range(2):
                    rows = slice(h * HEAD, (h + 1) * HEAD)
                    sp.dma_start(bd[rows, 0, h, :], Wq).then_inc(bd_in, 16)
                    sp.dma_start(bd[rows, 1, h, :], Wk).then_inc(bd_in, 16)
                sp.dma_start(y_table[N:N + SPARE, :], zero[:]).then_inc(spare_out, 16)
                sp.wait_ge(dinvT_ok, 1)
                sp.dma_start(dinv_table.rearrange("(t p) o -> t (p o)", p=P), dinvT[:]).then_inc(dinv_out, 16)
                sp.wait_ge(dinv_out, 16)
                sp.wait_ge(spare_out, 16)

            @block.scalar
            def _(act):
                act.wait_ge(filled, 5)
                full = (ETILES - 1) * P
                for vec, tile in ((src, keep.src), (dst, keep.dst)):
                    act.dma_start(tile[:, 0:ETILES - 1],
                                  vec[0:full].rearrange("(j p) -> p j", p=P),
                                  allow_slow_non_contiguous=True).then_inc(edges_in, 16)
                    act.dma_start(tile[0:ETAIL, ETILES - 1:ETILES],
                                  vec[full:EDGES].rearrange("(p o) -> p o", o=1)).then_inc(edges_in, 16)
                act.dma_start(dstrow[:, 0:EDGES],
                              dst.rearrange("(a e) -> a e", a=1).to_broadcast([P, EDGES])).then_inc(dstrow_in, 16)
                act.dma_start(bcol[:], b_in.rearrange("(j p) -> p j", p=P),
                              allow_slow_non_contiguous=True).then_inc(bcol_in, 16)
                for j in range(PAIRS):
                    act.wait_ge(winT_ps, j + 1)
                    nc.scalar.activation(winT[:, j, :], ps_t[:, j % 2, :], ACT.Copy).then_inc(winT_ok, 1)
                for k in range(KD):
                    act.wait_ge(wqk_ps, k + 1)
                    for qk in range(2):
                        nc.scalar.activation(
                            wqk[:, k, qk * QC:(qk + 1) * QC].rearrange("p (j c) -> p j c", j=PAIRS),
                            ps_w[:, k % 2, :].rearrange("p (j q c) -> p q j c", j=PAIRS, q=2)[:, qk],
                            ACT.Copy).then_inc(wqk_ok, 1)
                act.wait_ge(dinvT_ps, 1)
                nc.scalar.activation(dinvT[:], ps_i[0:TILES, 0:P], ACT.Copy).then_inc(dinvT_ok, 1)

            @block.tensor
            def _(pe):
                pe.wait_ge(ident_ok, 1)
                pe.wait_ge(win_in, 16)
                for j in range(PAIRS):
                    if j >= 2:
                        pe.wait_ge(winT_ok, j - 1)
                    for k in range(KD):
                        last = nc.tensor.transpose(ps_t[:, j % 2, k * P:(k + 1) * P],
                                                   win[:, k, j * P:(j + 1) * P], keep.ident[:])
                    last.then_inc(winT_ps, 1)
                pe.wait_ge(winT_ok, PAIRS)
                pe.wait_ge(bd_in, 64)
                for k in range(KD):
                    if k >= 2:
                        pe.wait_ge(wqk_ok, 2 * (k - 1))
                    for j in range(PAIRS):
                        last = nc.tensor.matmul(ps_w[:, k % 2, j * P:(j + 1) * P],
                                                winT[:, j, k * P:(k + 1) * P],
                                                bd[:].rearrange("p q h s -> p (q h s)"), start=True, stop=True)
                    last.then_inc(wqk_ps, 1)
                pe.wait_ge(bcolB_ok, 1)
                for j in range(PAIRS):
                    last = nc.tensor.matmul(ps_b[:, j * P:(j + 1) * P], bcolB[:, j, :],
                                            bd[:].rearrange("p q h s -> p (q h s)"), start=True, stop=True)
                last.then_inc(brow_ps, 1)
                pe.wait_ge(hot_ok, 2 * ETILES)
                for j in range(ETILES):
                    last = nc.tensor.matmul(ps_d[:, 0:TILES], hot_lo[:, j, :], hot_hi[:, j, :],
                                            start=(j == 0), stop=(j == ETILES - 1))
                last.then_inc(deg_ps, 1)
                pe.wait_ge(dinv_ok, 1)
                nc.tensor.transpose(ps_i[0:TILES, 0:P], keep.dinv[:], keep.ident[:]).then_inc(dinvT_ps, 1)

            @block.vector
            def _(dve):
                own = Chain(dve, dve_own)
                own.do(nc.vector.memset(keep.bias16[:], 0.0))
                own.do(nc.vector.memset(keep.ones_b[:], ACT_SCALE))
                own.do(nc.vector.memset(keep.one[:], 1.0))
                dve.wait_ge(edges_in, 64)
                dve.wait_ge(iota_ok, 2)
                own.do(nc.vector.tensor_scalar(part[:, 0, :], keep.dst[:], P - 1, None, ALU.bitwise_and))
                own.do(nc.vector.tensor_scalar(part[:, 1, :], keep.dst[:], 7, None, ALU.logical_shift_right))
                own.do(nc.vector.tensor_copy(iota[:], iota_i[:]))
                own.do(nc.vector.tensor_copy(spare[:], spare_i[:]))
                own.do(nc.vector.tensor_copy(keep.dstf[:], keep.dst[:]))
                own.settle()
                own.do(nc.vector.tensor_copy(partf[:], part[:]))
                own.settle()
                for j in range(ETILES):
                    nc.vector.tensor_scalar(hot_lo[:, j, :], iota[:], partf[:, 0, j:j + 1], None,
                                            ALU.is_equal).then_inc(hot_ok, 1)
                    nc.vector.tensor_scalar(hot_hi[:, j, :], iota[:, 0:TILES], partf[:, 1, j:j + 1], None,
                                            ALU.is_equal).then_inc(hot_ok, 1)
                dve.wait_ge(bcol_in, 16)
                nc.vector.tensor_copy(bcolB[:], bcol[:].unsqueeze(2).to_broadcast([P, PAIRS, 64])
                                      ).then_inc(bcolB_ok, 1)
                dve.wait_ge(deg_ps, 1)
                nc.vector.tensor_scalar(deg[:], ps_d[:, 0:TILES], 1.0, None, ALU.add).then_inc(deg_ok, 1)
                dve.wait_ge(dstrow_in, 16)
                dve.wait_ge(earlier_ok, 1)
                for j in range(ETILES):
                    own.do(nc.vector.scalar_tensor_tensor(junk[:], dstrow[:, j * P:(j + 1) * P],
                                                          keep.dstf[:, j:j + 1], earlier[:], ALU.is_equal,
                                                          ALU.mult, accum_out=prev[:, j:j + 1]))
                    own.settle()
                own.do(nc.vector.tensor_scalar(prev[:], prev[:], 0.0, None, ALU.is_gt))
                own.do(nc.vector.tensor_scalar(move[:], keep.dstf[:], -1.0, spare[:], ALU.mult, ALU.add))
                own.settle()
                own.do(nc.vector.tensor_tensor(move[:], move[:], prev[:], ALU.mult))
                own.settle()
                own.do(nc.vector.tensor_tensor(move[:], move[:], keep.dstf[:], ALU.add))
                own.settle()
                own.do(nc.vector.tensor_copy(keep.target[:], move[:]))
                dve.wait_ge(wg_in, 16)
                nc.vector.tensor_reduce(peak[:, 1:2], wg[:], AX.XY, ALU.max,
                                        apply_absolute_value=True).then_inc(peaks_ok, 1)
                dve.wait_ge(brow_ps, 1)
                for qk in range(2):
                    own.do(nc.vector.tensor_copy(
                        brow[:, qk * QC:(qk + 1) * QC].rearrange("p (j c) -> p j c", j=PAIRS),
                        ps_b[:].rearrange("p (j q c) -> p q j c", j=PAIRS, q=2)[:, qk]))
                own.do(nc.vector.memset(peakb[:], 1e-30))
                own.settle()
                own.do(nc.vector.tensor_reduce(peakb[0:64], brow[:], AX.X, ALU.max, apply_absolute_value=True))
                dve.wait_ge(wqk_ok, 2 * KD)
                own.do(nc.vector.tensor_reduce(peak[:, 0:1], wqk[:], AX.XY, ALU.max, apply_absolute_value=True))
                own.settle()
                nc.vector.tensor_tensor(peak[:, 0:1], peak[:, 0:1], peakb[:], ALU.max).then_inc(peaks_ok, 1)
                dve.wait_ge(peaks_ok, 2)
                nc.vector.tensor_scalar(peak[:, 1:2], peak[:, 1:2], 1e-30, None, ALU.max).then_inc(peaks_ok, 1)
                dve.wait_ge(peak_all_ok, 1)
                own.do(power_of_two(nc, pow2[:], peak_all[:]))
                own.settle()
                own.do(nc.vector.reciprocal(wscale[:], pow2[:]))
                own.settle()
                own.do(nc.vector.tensor_scalar(wscale[:], wscale[:], W_TOP, None, ALU.mult))
                own.do(nc.vector.tensor_scalar(keep.unscale[:], pow2[:], 1.0 / (W_TOP * ACT_SCALE), None, ALU.mult))
                dve.wait_ge(dinv_ok, 1)
                own.settle()
                own.do(nc.vector.tensor_scalar(keep.hcoef[:], keep.dinv[:], keep.unscale[:, 1:2], None, ALU.mult))
                split(own, nc, [(keep.w_hi[:, k, col:col + D], keep.w_lo[:, k, col:col + D], w[:, k, :],
                                 wscale[:, c:c + 1])
                                for w, col, c in ((wqk, 0, 0), (wg, D, 1)) for k in range(KD)])
                own.do(nc.vector.tensor_scalar(brow_hi[:], brow[:], wscale[0:64, 0:1], None, ALU.mult))
                own.settle()
                own.do(nc.vector.tensor_copy(keep.bias16[0:1, :], brow_hi[0:1, :]))
                own.do(nc.vector.scalar_tensor_tensor(keep.bias16[32:33, :], brow[32:33, :], wscale[32:33, 0:1],
                                                      brow_hi[32:33, :], ALU.mult, ALU.subtract))
                own.settle()
        m.clear_sems()


def first_pass(nc, keep, x, h_table, y_table):
    with ExitStack() as st:
        m = Mem(nc, st, keep.lasting)
        X, R = 4, 2
        xb = m.sb("a_x", [P, X, D])
        xn = m.sb("a_xn", [P, R, D])
        xT_hi = m.sb("a_xT_hi", [P, R, D], F16)
        xT_lo = m.sb("a_xT_lo", [P, R, D], F16)
        hb = m.sb("a_h", [P, R, D])
        qb = m.sb("a_q", [P, R, QC])
        stats = m.sb("a_stats", [P, R, 6])
        mv = m.sb("a_mv", [P, R, 2])
        var = m.sb("a_var", [P, R, 1])
        top = m.sb("a_top", [P, R, HEADS])
        total = m.sb("a_total", [P, R, HEADS])
        ps_x = m.ps("ap_x", [P, R, D])
        ps_qk = m.ps("ap_qk", [P, R, D])
        ps_h = m.ps("ap_h", [P, R, D])
        ps_q = m.ps("ap_q", [P, R, D])

        x_in = m.sems("a_x_in", X)
        y_out = m.sems("a_y_out", X)
        h_out = m.sems("a_h_out", R)
        (stats_ok, mv_ok, var_ok, rstd_ok, mean_ok, xn_ok, xT_ps, xT_hi_ok, xT_lo_ok, qk_ps, h_ps, k_ok, kmax_ok,
         top_ok, less_ok, exp_ok, total_ok, recip_ok, q_ok, q_ps, qT_hi_ok, qT_lo_ok, h_ok, y_ok) = (
            m.sem("a_" + n) for n in (
                "stats_ok", "mv_ok", "var_ok", "rstd_ok", "mean_ok", "xn_ok", "xT_ps", "xT_hi_ok", "xT_lo_ok",
                "qk_ps", "h_ps", "k_ok", "kmax_ok", "top_ok", "less_ok", "exp_ok", "total_ok", "recip_ok", "q_ok",
                "q_ps", "qT_hi_ok", "qT_lo_ok", "h_ok", "y_ok"))

        def heads(ap):
            return ap.rearrange("p (h s) -> p h s", h=HEADS)

        with nc.Block() as block:
            @block.sync
            def _(sp):
                def load(t):
                    if t.base >= X:
                        sp.wait_ge(y_out[t.slot(X)], 16 * t.uses(X))
                    r = t.rows()
                    sp.dma_start(xb[0:r, t.slot(X), :], x[bass.ds(t.n * P, r), :]).then_inc(x_in[t.slot(X)], 16)

                def store(t):
                    r = t.rows()
                    sp.wait_ge(h_ok, t.n + 1)
                    sp.dma_start(h_table[bass.ds(t.n * P, r), :], hb[0:r, t.slot(R), :]
                                 ).then_inc(h_out[t.slot(R)], 16)
                    sp.wait_ge(y_ok, t.n + 1)
                    sp.dma_start(y_table[bass.ds(t.n * P, r), :], xb[0:r, t.slot(X), :]
                                 ).then_inc(y_out[t.slot(X)], 16)

                over_tiles(sp, X, [(3, load), (0, store)])
                for q in range(X):
                    sp.wait_ge(y_out[q], 16 * len(range(q, TILES, X)))
                for q in range(R):
                    sp.wait_ge(h_out[q], 16 * len(range(q, TILES, R)))

            @block.gpsimd
            def _(pool):
                def rstd(t):
                    b = t.slot(R)
                    pool.wait_ge(mv_ok, t.n + 1)
                    stand_alone(pool)
                    nc.gpsimd.tensor_scalar(var[:, b], mv[:, b, 1:2], EPS, ACT_SCALE ** -2, ALU.add, ALU.mult
                                            ).then_inc(var_ok, 1)
                    nc.gpsimd.tensor_copy(keep.mean[:, bass.ds(t.n, 1)], mv[:, b, 0:1]).then_inc(mean_ok, 1)
                    pool.wait_ge(var_ok, t.n + 1)
                    nc.gpsimd.tensor_tensor(keep.rstd[:, bass.ds(t.n, 1)], var[:, b], keep.mhalf[:], ALU.pow
                                            ).then_inc(rstd_ok, 1)

                over_tiles(pool, X, [(2, rstd)])

            @block.vector
            def _(dve):
                def norm(t):
                    dve.wait_ge(rstd_ok, t.n + 1)
                    dve.wait_ge(mean_ok, t.n + 1)
                    if t.base >= R:
                        dve.wait_ge(xT_ps, t.n + 1 - R)
                    nc.vector.tensor_scalar(xn[:, t.slot(R), :], xb[:, t.slot(X), :],
                                            keep.mean[:, bass.ds(t.n, 1)], keep.rstd[:, bass.ds(t.n, 1)],
                                            ALU.subtract, ALU.mult).then_inc(xn_ok, 1)

                def statistics(t):
                    dve.wait_ge(x_in[t.slot(X)], 16 * (t.uses(X) + 1))
                    nc.vector.bn_stats(stats[:, t.slot(R), :], xb[:, t.slot(X), :]).then_inc(stats_ok, 1)

                def aggregate(t):
                    dve.wait_ge(stats_ok, t.n + 1)
                    if t.base >= R:
                        dve.wait_ge(mean_ok, t.n + 1 - R)
                    stand_alone(dve)
                    nc.vector.bn_aggr(mv[:, t.slot(R), :], stats[:, t.slot(R), :]).then_inc(mv_ok, 1)

                def low_half(t):
                    dve.wait_ge(xT_hi_ok, t.n + 1)
                    b = t.slot(R)
                    nc.vector.tensor_tensor(xT_lo[:, b, :], ps_x[:, b, :], xT_hi[:, b, :], ALU.subtract
                                            ).then_inc(xT_lo_ok, 1)

                def row_max(t):
                    dve.wait_ge(qk_ps, t.n + 1)
                    nc.vector.tensor_reduce(top[:, t.slot(R), :], heads(ps_qk[:, t.slot(R), 0:QC]), AX.X, ALU.max
                                            ).then_inc(top_ok, 1)

                def column_max(t):
                    dve.wait_ge(k_ok, t.n + 1)
                    if t.base == 0 and t.j is None:
                        nc.vector.tensor_copy(keep.kmax[:], keep.k[:, 0, :]).then_inc(kmax_ok, 1)
                    else:
                        dve.wait_ge(kmax_ok, t.n)
                        r = t.rows()
                        nc.vector.tensor_tensor(keep.kmax[0:r], keep.kmax[0:r], keep.k[0:r, t.n, :], ALU.max
                                                ).then_inc(kmax_ok, 1)

                def less_max(t):
                    b = t.slot(R)
                    dve.wait_ge(top_ok, t.n + 1)
                    if t.base >= R:
                        dve.wait_ge(q_ps, t.n + 1 - R)
                    nc.vector.tensor_tensor(heads(qb[:, b, :]), heads(ps_qk[:, b, 0:QC]),
                                            top[:, b, :].unsqueeze(2).to_broadcast([P, HEADS, SLICE]),
                                            ALU.subtract).then_inc(less_ok, 1)

                def totals(t):
                    dve.wait_ge(exp_ok, t.n + 1)
                    nc.vector.tensor_reduce(total[:, t.slot(R), :], heads(qb[:, t.slot(R), :]), AX.X, ALU.add
                                            ).then_inc(total_ok, 1)

                def reciprocals(t):
                    dve.wait_ge(total_ok, t.n + 1)
                    nc.vector.reciprocal(total[:, t.slot(R), :], total[:, t.slot(R), :]).then_inc(recip_ok, 1)

                def normalise_q(t):
                    b = t.slot(R)
                    dve.wait_ge(recip_ok, t.n + 1)
                    nc.vector.tensor_tensor(heads(qb[:, b, :]), heads(qb[:, b, :]),
                                            total[:, b, :].unsqueeze(2).to_broadcast([P, HEADS, SLICE]),
                                            ALU.mult).then_inc(q_ok, 1)

                def low_q(t):
                    dve.wait_ge(qT_hi_ok, t.n + 1)
                    nc.vector.scalar_tensor_tensor(keep.qT_lo[:, t.n, :], ps_q[:, t.slot(R), 0:QC], ACT_SCALE,
                                                   keep.qT_hi[:, t.n, :], ALU.mult, ALU.subtract
                                                   ).then_inc(qT_lo_ok, 1)

                def self_loop(t):
                    dve.wait_ge(h_ok, t.n + 1)
                    nc.vector.scalar_tensor_tensor(xb[:, t.slot(X), :], hb[:, t.slot(R), :],
                                                   keep.dinv[:, bass.ds(t.n, 1)], xb[:, t.slot(X), :],
                                                   ALU.mult, ALU.add).then_inc(y_ok, 1)

                over_tiles(dve, X, [(1, norm), (-1, row_max), (-1, less_max), (2, statistics), (-1, column_max),
                                    (2, aggregate), (0, self_loop), (-1, totals), (-1, reciprocals),
                                    (1, low_half), (-1, normalise_q), (-2, low_q)])

            @block.scalar
            def _(act):
                def high_half(t):
                    b = t.slot(R)
                    act.wait_ge(xT_ps, t.n + 1)
                    if t.base >= R:
                        act.wait_ge(qk_ps, t.n + 1 - R)
                    nc.scalar.activation(xT_hi[:, b, :], ps_x[:, b, :], ACT.Copy).then_inc(xT_hi_ok, 1)

                def keep_k(t):
                    act.wait_ge(less_ok, t.n + 1)
                    nc.scalar.activation(keep.k[:, t.n, :], ps_qk[:, t.slot(R), QC:2 * QC], ACT.Identity,
                                         scale=keep.unscale[:, 0:1]).then_inc(k_ok, 1)

                def exponent(t):
                    b = t.slot(R)
                    act.wait_ge(less_ok, t.n + 1)
                    nc.scalar.activation(qb[:, b, :], qb[:, b, :], ACT.Exp, scale=keep.unscale[:, 0:1]
                                         ).then_inc(exp_ok, 1)

                def high_q(t):
                    act.wait_ge(q_ps, t.n + 1)
                    nc.scalar.activation(keep.qT_hi[:, t.n, :], ps_q[:, t.slot(R), 0:QC], ACT.Copy,
                                         scale=ACT_SCALE).then_inc(qT_hi_ok, 1)

                def h_rows(t):
                    b = t.slot(R)
                    act.wait_ge(h_ps, t.n + 1)
                    if t.base >= R:
                        act.wait_ge(h_out[b], 16 * t.uses(R))
                        act.wait_ge(y_ok, t.n + 1 - R)
                    nc.scalar.activation(hb[:, b, :], ps_h[:, b, :], ACT.Identity,
                                         scale=keep.hcoef[:, bass.ds(t.n, 1)]).then_inc(h_ok, 1)

                over_tiles(act, X, [(-1, keep_k), (-1, exponent), (0, h_rows), (1, high_half), (-2, high_q)])

            @block.tensor
            def _(pe):
                def parts(b):
                    return ((xT_hi, keep.w_hi), (xT_lo, keep.w_hi), (xT_hi, keep.w_lo))

                def h_product(t):
                    b = t.slot(R)
                    pe.wait_ge(xT_lo_ok, t.n + 1)
                    if t.base >= R:
                        pe.wait_ge(h_ok, t.n + 1 - R)
                    for k in range(KD):
                        for n, (xs, ws) in enumerate(parts(b)):
                            last = nc.tensor.matmul(ps_h[:, b, :], xs[:, b, k * P:(k + 1) * P], ws[:, k, D:2 * D],
                                                    start=(k == 0 and n == 0), stop=(k == KD - 1 and n == 2))
                    last.then_inc(h_ps, 1)

                def transposes(t):
                    b = t.slot(R)
                    pe.wait_ge(xn_ok, t.n + 1)
                    if t.base >= R:
                        pe.wait_ge(xT_lo_ok, t.n + 1 - R)
                    for k in range(KD):
                        last = nc.tensor.transpose(ps_x[:, b, k * P:(k + 1) * P], xn[:, b, k * P:(k + 1) * P],
                                                   keep.ident[:])
                    last.then_inc(xT_ps, 1)

                def qk_product(t):
                    b = t.slot(R)
                    if t.base >= R:
                        pe.wait_ge(less_ok, t.n + 1 - R)
                        pe.wait_ge(k_ok, t.n + 1 - R)
                    nc.tensor.matmul(ps_qk[:, b, :], keep.ones_b[:], keep.bias16[:], start=True, stop=False)
                    for k in range(KD):
                        for n, (xs, ws) in enumerate(parts(b)):
                            last = nc.tensor.matmul(ps_qk[:, b, :], xs[:, b, k * P:(k + 1) * P], ws[:, k, 0:D],
                                                    start=False, stop=(k == KD - 1 and n == 2))
                    last.then_inc(qk_ps, 1)

                def q_transposes(t):
                    b = t.slot(R)
                    pe.wait_ge(q_ok, t.n + 1)
                    if t.base >= R:
                        pe.wait_ge(qT_lo_ok, t.n + 1 - R)
                    for c in range(2):
                        last = nc.tensor.transpose(ps_q[:, b, c * P:(c + 1) * P], qb[:, b, c * P:(c + 1) * P],
                                                   keep.ident[:])
                    last.then_inc(q_ps, 1)

                over_tiles(pe, X, [(0, h_product), (1, transposes), (0, qk_product), (-1, q_transposes)])


def second_pass(nc, keep, x, dst, h_table, y_table, dinv_table):
    with ExitStack() as st:
        m = Mem(nc, st, keep.lasting)
        X, R = 4, 2
        kmax_all = m.sb("b_kmax_all", [P, QC])
        kacc = m.sb("b_kacc", [P, QC])
        xb = m.sb("b_x", [P, X, D])
        xs_hi = m.sb("b_x_hi", [P, R, D], F16)
        xs_lo = m.sb("b_x_lo", [P, R, D], F16)
        kb = m.sb("b_k", [P, R, QC])
        k_hi = m.sb("b_k_hi", [P, R, QC], F16)
        k_lo = m.sb("b_k_lo", [P, R, QC], F16)
        ln_act = m.sb("b_ln_act", [P, 1])
        dstrow = m.sb("b_dstrow", [P, ETILES * P], I32)
        same = m.sb("b_same", [P, P])
        hsrc = m.sb("b_hsrc", [P, D])
        msg = m.sb("b_msg", [P, D])
        dst_dinv = m.sb("b_dst_dinv", [P, 1])
        index = m.sb("b_index", [P, 3], I32)
        ps_g = m.ps("bp_g", [P, 2, D])
        ps_e = m.ps("bp_e", [P, D])
        ps_s = m.ps("bp_s", [P, D])

        x_in = m.sems("b_x_in", X)
        (kmax_in, dstrow_in, kmax_ready, ln_ok, xn_ok, less_ok, exp_ok, x_hi_ok, x_lo_ok, k_hi_ok, k_lo_ok, g_ps,
         kacc_ok, same_ok, hsrc_in, dinv_in, sum_ps, msg_ok, added, ksum_ps, g_ok, rk_ok, fill_ok, index_ok, target_ok) = (
            m.sem("b_" + n) for n in (
                "kmax_in", "dstrow_in", "kmax_ready", "ln_ok", "xn_ok", "less_ok", "exp_ok", "x_hi_ok", "x_lo_ok",
                "k_hi_ok", "k_lo_ok", "g_ps", "kacc_ok", "same_ok", "hsrc_in", "dinv_in", "sum_ps", "msg_ok",
                "added", "ksum_ps", "g_ok", "rk_ok", "fill_ok", "index_ok", "target_ok"))

        def has_edges(t):
            return t.base % X == 0

        def etile(t):
            return t.uses(X)

        with nc.Block() as block:
            @block.sync
            def _(sp):
                sp.wait_ge(fill_ok, 1)
                sp.dma_start(dstrow[:, 0:EDGES],
                             dst.rearrange("(a e) -> a e", a=1).to_broadcast([P, EDGES])).then_inc(dstrow_in, 16)

                def load(t):
                    if t.base >= X:
                        sp.wait_ge(x_lo_ok, t.n + 1 - X)
                    r = t.rows()
                    sp.dma_start(xb[0:r, t.slot(X), :], x[bass.ds(t.n * P, r), :]).then_inc(x_in[t.slot(X)], 16)

                over_tiles(sp, X, [(3, load)])

            @block.gpsimd
            def _(pool):
                nc.gpsimd.memset(dstrow[:], N).then_inc(fill_ok, 1)
                nc.gpsimd.memset(kacc[:], 0.0).then_inc(kacc_ok, 1)
                nc.gpsimd.partition_all_reduce(kmax_all[:], keep.kmax[:], P, ROP.max).then_inc(kmax_ready, 1)

                def gather(t):
                    if not has_edges(t):
                        return
                    j = etile(t)
                    if t.base >= X:
                        pool.wait_ge(sum_ps, j)
                        pool.wait_ge(msg_ok, j)
                    for n, table in enumerate((keep.src, keep.dst)):
                        nc.gpsimd.tensor_copy(index[:, n:n + 1], table[:, bass.ds(j, 1)]).then_inc(index_ok, 1)
                    pool.wait_ge(index_ok, j * 2 + 2)
                    stand_alone(pool)
                    pool.indirect_dma_start(hsrc[:], None, h_table, bass.IndirectOffsetOnAxis(
                        index[:, 0:1], 0)).then_inc(hsrc_in, 16)
                    stand_alone(pool)
                    pool.indirect_dma_start(dst_dinv[:], None, dinv_table, bass.IndirectOffsetOnAxis(
                        index[:, 1:2], 0)).then_inc(dinv_in, 16)

                def scatter(t):
                    if not has_edges(t):
                        return
                    j = etile(t)
                    pool.wait_ge(msg_ok, j + 1)
                    if t.base >= X:
                        pool.wait_ge(added, 16 * j)
                    nc.gpsimd.tensor_copy(index[:, 2:3], keep.target[:, bass.ds(j, 1)]).then_inc(target_ok, 1)
                    pool.wait_ge(target_ok, j + 1)
                    stand_alone(pool)
                    pool.indirect_dma_start(y_table, bass.IndirectOffsetOnAxis(index[:, 2:3], 0), msg[:], None,
                                            compute_op=ALU.add).then_inc(added, 16)

                def add_up(t):
                    pool.wait_ge(exp_ok, t.n + 1)
                    pool.wait_ge(kacc_ok, t.n + 1)
                    r = t.rows()
                    nc.gpsimd.tensor_tensor(kacc[0:r, :], kacc[0:r, :], kb[0:r, t.slot(R), :], ALU.add
                                            ).then_inc(kacc_ok, 1)

                over_tiles(pool, X, [(2, gather), (0, add_up), (-2, scatter)])
                pool.wait_ge(added, 16 * ETILES)

            @block.vector
            def _(dve):
                nc.vector.memset(ln_act[:], 8.317766166719343).then_inc(ln_ok, 1)
                dve.wait_ge(kmax_ready, 1)

                def norm(t):
                    dve.wait_ge(x_in[t.slot(X)], 16 * (t.uses(X) + 1))
                    r = t.rows()
                    nc.vector.tensor_scalar(xb[0:r, t.slot(X), :], xb[0:r, t.slot(X), :],
                                            keep.mean[0:r, bass.ds(t.n, 1)], keep.rstd[0:r, bass.ds(t.n, 1)],
                                            ALU.subtract, ALU.mult).then_inc(xn_ok, 1)

                def less_max(t):
                    if t.base >= R:
                        dve.wait_ge(kacc_ok, t.n + 2 - R)
                        dve.wait_ge(k_lo_ok, t.n + 1 - R)
                    r = t.rows()
                    nc.vector.tensor_tensor(kb[0:r, t.slot(R), :], keep.k[0:r, t.n, :], kmax_all[0:r], ALU.subtract
                                            ).then_inc(less_ok, 1)

                def low_x(t):
                    b = t.slot(R)
                    dve.wait_ge(x_hi_ok, t.n + 1)
                    r = t.rows()
                    nc.vector.tensor_tensor(xs_lo[0:r, b, :], xb[0:r, t.slot(X), :], xs_hi[0:r, b, :], ALU.subtract
                                            ).then_inc(x_lo_ok, 1)

                def high_k(t):
                    b = t.slot(R)
                    dve.wait_ge(exp_ok, t.n + 1)
                    if t.base >= R:
                        dve.wait_ge(g_ps, t.n + 1 - R)
                    r = t.rows()
                    nc.vector.tensor_copy(k_hi[0:r, b, :], kb[0:r, b, :]).then_inc(k_hi_ok, 1)

                def low_k(t):
                    b = t.slot(R)
                    dve.wait_ge(k_hi_ok, t.n + 1)
                    r = t.rows()
                    nc.vector.tensor_tensor(k_lo[0:r, b, :], kb[0:r, b, :], k_hi[0:r, b, :], ALU.subtract
                                            ).then_inc(k_lo_ok, 1)

                def same_target(t):
                    if not has_edges(t):
                        return
                    j = etile(t)
                    if t.base == 0:
                        dve.wait_ge(dstrow_in, 16)
                    else:
                        dve.wait_ge(sum_ps, j)
                    nc.vector.tensor_scalar(same[:], dstrow[:, bass.ds(j * P, P)], keep.dstf[:, bass.ds(j, 1)],
                                            None, ALU.is_equal).then_inc(same_ok, 1)

                over_tiles(dve, X, [(1, less_max), (1, norm), (1, same_target), (0, high_k), (0, low_x),
                                    (0, low_k)])
                dve.wait_ge(ksum_ps, 1)
                nc.vector.tensor_scalar(keep.rk[:], ps_s[:, 0:2], ACT_SCALE, None, ALU.mult).then_inc(rk_ok, 1)
                dve.wait_ge(rk_ok, 1)
                nc.vector.reciprocal(keep.rk[:], keep.rk[:]).then_inc(rk_ok, 1)
                dve.wait_ge(rk_ok, 2)
                dve.wait_ge(g_ps, TILES)
                for c in range(2):
                    nc.vector.tensor_scalar(keep.g[:, c, :], ps_g[:, c, :], keep.rk[:, c:c + 1], None, ALU.mult
                                            ).then_inc(g_ok, 1)
                dve.wait_ge(g_ok, 2)

            @block.scalar
            def _(act):
                act.wait_ge(ln_ok, 1)

                def exponent(t):
                    b = t.slot(R)
                    act.wait_ge(less_ok, t.n + 1)
                    r = t.rows()
                    nc.scalar.activation(kb[0:r, b, :], kb[0:r, b, :], ACT.Exp, bias=ln_act[0:r]).then_inc(exp_ok, 1)

                def high_x(t):
                    b = t.slot(R)
                    act.wait_ge(xn_ok, t.n + 1)
                    if t.base >= R:
                        act.wait_ge(g_ps, t.n + 1 - R)
                    r = t.rows()
                    nc.scalar.activation(xs_hi[0:r, b, :], xb[0:r, t.slot(X), :], ACT.Copy).then_inc(x_hi_ok, 1)

                def message(t):
                    if not has_edges(t):
                        return
                    j = etile(t)
                    act.wait_ge(sum_ps, j + 1)
                    act.wait_ge(dinv_in, 16 * (j + 1))
                    if t.base >= X:
                        act.wait_ge(added, 16 * j)
                    nc.scalar.activation(msg[:], ps_e[:], ACT.Identity, scale=dst_dinv[:]).then_inc(msg_ok, 1)

                over_tiles(act, X, [(1, exponent), (1, high_x), (-1, message)])

            @block.tensor
            def _(pe):
                def products(t):
                    b, r = t.slot(R), t.rows()
                    pe.wait_ge(x_lo_ok, t.n + 1)
                    pe.wait_ge(k_lo_ok, t.n + 1)
                    for c in range(2):
                        cols = slice(c * P, (c + 1) * P)
                        for n, (ks, xs) in enumerate(((k_hi, xs_hi), (k_hi, xs_lo), (k_lo, xs_hi))):
                            last = nc.tensor.matmul(ps_g[:, c, :], ks[0:r, b, cols], xs[0:r, b, :],
                                                    start=(t.j is None and t.base == 0 and n == 0),
                                                    stop=(t.j is None and t.base == TILES - 1 and n == 2))
                    last.then_inc(g_ps, 1)

                def sum_edges(t):
                    if not has_edges(t):
                        return
                    j = etile(t)
                    pe.wait_ge(same_ok, j + 1)
                    pe.wait_ge(hsrc_in, 16 * (j + 1))
                    if t.base >= X:
                        pe.wait_ge(msg_ok, j)
                    nc.tensor.matmul(ps_e[:], same[:], hsrc[:], start=True, stop=True).then_inc(sum_ps, 1)

                over_tiles(pe, X, [(0, products), (0, sum_edges)])
                pe.wait_ge(kacc_ok, TILES + 1)
                for c in range(2):
                    last = nc.tensor.matmul(ps_s[:, c:c + 1], kacc[:, c * P:(c + 1) * P], keep.one[:],
                                            start=True, stop=True)
                last.then_inc(ksum_ps, 1)


def fold(nc, keep, f, W_in, b_in, Wv, W_out, b_out, gnn_b, Wg, W1, b1, W2, b2, ln_g, ln_b, out_g, out_b):
    with ExitStack() as st:
        m = Mem(nc, st, st)
        win = m.sb("f_win", [P, KD, D])
        wout = m.sb("f_wout", [P, PAIRS, D])
        wv = m.sb("f_wv", [P, 2, HEAD])
        wvT = m.sb("f_wvT", [P, P])
        wvo = m.sb("f_wvo", [P, PAIRS, D])
        bcol = m.sb("f_bcol", [P, PAIRS])
        gT = m.sb("f_gT", [P, KD, QC])
        u = m.sb("f_u", [P, PAIRS, P])
        mm = m.sb("f_m", [P, 2, D])
        row = m.sb("f_row", [SLICE, 2, D])
        w1 = m.sb("f_w1", [P, KD, ZC])
        w1g = m.sb("f_w1g", [P, KD, ZC])
        w2 = m.sb("f_w2", [P, 2, D])
        gcol = m.sb("f_gcol", [P, KD])
        lbcol = m.sb("f_lbcol", [P, KD])
        lbB = m.sb("f_lbB", [P, KD, P])
        b2t = m.sb("f_b2t", [EXPERTS, D])
        b2_hi = m.sb("f_b2_hi", [EXPERTS, D], F16)
        b2_lo = m.sb("f_b2_lo", [EXPERTS, D], F16)
        peak = m.sb("f_peak", [P, 5])
        peak_all = m.sb("f_peak_all", [P, 5])
        bound = m.sb("f_bound", [P, 4])
        pow2 = m.sb("f_pow2", [P, 4])
        scale = m.sb("f_scale", [P, 4])
        b2scale = m.sb("f_b2scale", [P, 1])
        iota_i = m.sb("f_iota_i", [P, EXPERTS], I32)
        ps_t = m.ps("fp_t", [P, 2, D])
        ps_u = m.ps("fp_u", [P, D])
        ps_m = m.ps("fp_m", [P, 2, D])
        ps_v = m.ps("fp_v", [P, D])
        ps_z = m.ps("fp_z", [P, D])
        ps_w = m.ps("fp_w", [P, D])
        names = ("win_in", "wout_in", "wv_in", "col_in", "row_in", "w1_in", "w2_in", "b2_in", "b1_in", "out_in",
                 "b2_copied", "filled", "iota_ok", "wv_filled", "wvT_ps", "wvT_ok", "wvo_ps", "wvo_ok", "gT_ps", "gT_ok",
                 "u_ps", "u_ok", "m_ps", "m_ok", "lbB_ok", "z_ps", "peaks_ok", "peak_all_ok", "b2_ok", "own",
                 "ident_ok")
        sem = {n: m.sem("f_" + n) for n in names}

        with nc.Block() as block:
            @block.sync
            def _(sp):
                sp.dma_start(win[:], W_in.rearrange("(k p) n -> p k n", p=P)).then_inc(sem["win_in"], 16)
                sp.dma_start(wout[:], W_out.rearrange("(j p) n -> p j n", p=P)).then_inc(sem["wout_in"], 16)
                sp.wait_ge(sem["wv_filled"], 1)
                for h in range(2):
                    sp.dma_start(wv[h * HEAD:(h + 1) * HEAD, h, :], Wv).then_inc(sem["wv_in"], 16)
                for k in range(KD):
                    sp.dma_start(w1[:, k, 0:HC].rearrange("p (e j) -> p e j", e=EXPERTS),
                                 W1[:, k * P:(k + 1) * P, :].rearrange("e p j -> p e j")).then_inc(sem["w1_in"], 16)
                sp.dma_start(w1[:, :, HC:ZC], Wg.rearrange("(k p) e -> p k e", p=P)).then_inc(sem["w1_in"], 16)
                sp.wait_ge(sem["b2_ok"], 2)
                for n, part in enumerate((b2_hi, b2_hi, b2_lo)):
                    sp.dma_start(f.b2s[n * EXPERTS:(n + 1) * EXPERTS, :], part[:]).then_inc(sem["b2_copied"], 16)
                sp.wait_ge(sem["b2_copied"], 48)

            @block.scalar
            def _(act):
                act.dma_start(bcol[:], b_in.rearrange("(j p) -> p j", p=P),
                              allow_slow_non_contiguous=True).then_inc(sem["col_in"], 16)
                act.dma_start(gcol[:], ln_g.rearrange("(k p) -> p k", p=P),
                              allow_slow_non_contiguous=True).then_inc(sem["col_in"], 16)
                act.dma_start(lbcol[:], ln_b.rearrange("(k p) -> p k", p=P),
                              allow_slow_non_contiguous=True).then_inc(sem["col_in"], 16)
                for n, v in enumerate((gnn_b, b_out)):
                    act.dma_start(row[:, n, :], v.rearrange("(a n) -> a n", a=1).to_broadcast([SLICE, D])
                                  ).then_inc(sem["row_in"], 16)
                act.dma_start(w2[:], W2.rearrange("e j n -> (e j) n").rearrange("(c p) n -> p c n", p=P)
                              ).then_inc(sem["w2_in"], 16)
                act.dma_start(b2t[:], b2).then_inc(sem["b2_in"], 16)
                act.wait_ge(sem["filled"], 1)
                act.dma_start(f.zbias[:, 0:HC], b1.rearrange("e j -> (e j)").rearrange("(a n) -> a n", a=1)
                              .to_broadcast([P, HC])).then_inc(sem["b1_in"], 16)
                for v, tile in ((out_g, f.gain), (out_b, f.offset)):
                    act.dma_start(tile[:], v.rearrange("(a n) -> a n", a=1).to_broadcast([P, D])
                                  ).then_inc(sem["out_in"], 16)
                act.wait_ge(sem["wvT_ps"], 1)
                nc.scalar.activation(wvT[:], ps_v[:, 0:P], ACT.Copy).then_inc(sem["wvT_ok"], 1)
                for j in range(PAIRS):
                    act.wait_ge(sem["wvo_ps"], j + 1)
                    nc.scalar.activation(wvo[:, j, :], ps_w[:], ACT.Copy).then_inc(sem["wvo_ok"], 1)
                for c in range(2):
                    for k in range(0, KD, 2):
                        act.wait_ge(sem["gT_ps"], c * 2 + k // 2 + 1)
                        for kk in (k, k + 1):
                            nc.scalar.activation(gT[:, kk, c * P:(c + 1) * P],
                                                 ps_t[:, k // 2, (kk - k) * P:(kk - k + 1) * P],
                                                 ACT.Copy).then_inc(sem["gT_ok"], 1)
                act.wait_ge(sem["out_in"], 32)

            @block.gpsimd
            def _(pool):
                nc.gpsimd.memset(wv[:], 0.0).then_inc(sem["wv_filled"], 1)
                nc.gpsimd.memset(f.zbias[:], 0.0).then_inc(sem["filled"], 1)
                nc.gpsimd.iota(iota_i[:], [[1, EXPERTS]], base=0, channel_multiplier=0).then_inc(sem["iota_ok"], 1)
                nc.gpsimd.memset(f.ident16[:], 0.0).then_inc(sem["ident_ok"], 1)
                pool.wait_ge(sem["ident_ok"], 1)
                nc.gpsimd.affine_select(out=f.ident16[:], in_=f.ident16[:], compare_op=ALU.not_equal, fill=1.0,
                                        base=0, pattern=[[-1, P]], channel_multiplier=1
                                        ).then_inc(sem["ident_ok"], 1)
                pool.wait_ge(sem["peaks_ok"], 6)
                nc.gpsimd.partition_all_reduce(peak_all[:], peak[:], P, ROP.max).then_inc(sem["peak_all_ok"], 1)

            @block.tensor
            def _(pe):
                pe.wait_ge(sem["wv_in"], 32)
                nc.tensor.transpose(ps_v[:, 0:P], wv[:].rearrange("p h c -> p (h c)"), keep.ident[:]
                                    ).then_inc(sem["wvT_ps"], 1)
                pe.wait_ge(sem["wvT_ok"], 1)
                pe.wait_ge(sem["wout_in"], 16)
                for j in range(PAIRS):
                    if j:
                        pe.wait_ge(sem["wvo_ok"], j)
                    nc.tensor.matmul(ps_w[:], wvT[:], wout[:, j, :], start=True, stop=True
                                     ).then_inc(sem["wvo_ps"], 1)
                for c in range(2):
                    for k in range(0, KD, 2):
                        if c:
                            pe.wait_ge(sem["gT_ok"], k + 2)
                        for kk in (k, k + 1):
                            last = nc.tensor.transpose(ps_t[:, k // 2, (kk - k) * P:(kk - k + 1) * P],
                                                       keep.g[:, c, kk * P:(kk + 1) * P], keep.ident[:])
                        last.then_inc(sem["gT_ps"], 1)
                pe.wait_ge(sem["lbB_ok"], 1)
                pe.wait_ge(sem["w1_in"], 16 * (KD + 1))
                for k in range(KD):
                    last = nc.tensor.matmul(ps_z[:, 0:ZC], lbB[:, k, :], w1[:, k, :], start=(k == 0),
                                            stop=(k == KD - 1))
                last.then_inc(sem["z_ps"], 1)
                pe.wait_ge(sem["gT_ok"], 2 * KD)
                pe.wait_ge(sem["win_in"], 16)
                for j in range(PAIRS):
                    for k in range(KD):
                        last = nc.tensor.matmul(ps_u[:, j * 2 * SLICE:(j + 1) * 2 * SLICE],
                                                win[:, k, j * P:(j + 1) * P],
                                                gT[:, k, j * 2 * SLICE:(j + 1) * 2 * SLICE],
                                                start=(k == 0), stop=(k == KD - 1))
                last.then_inc(sem["u_ps"], 1)
                pe.wait_ge(sem["u_ok"], 2 * PAIRS + 1)
                pe.wait_ge(sem["wvo_ok"], PAIRS)
                for c in range(2):
                    for j in (2 * c, 2 * c + 1):
                        last = nc.tensor.matmul(ps_m[:, c, :], u[:, j, :], wvo[:, j, :], start=(j % 2 == 0),
                                                stop=(j % 2 == 1))
                last.then_inc(sem["m_ps"], 1)

            @block.vector
            def _(dve):
                own = Chain(dve, sem["own"])
                nc.vector.memset(u[:], 0.0).then_inc(sem["u_ok"], 1)
                own.do(nc.vector.memset(f.mhalf2[:], -0.5))
                own.do(nc.vector.memset(peak[:], 0.0))
                dve.wait_ge(sem["col_in"], 48)
                nc.vector.tensor_copy(lbB[:], lbcol[:].unsqueeze(2).to_broadcast([P, KD, P])
                                      ).then_inc(sem["lbB_ok"], 1)
                dve.wait_ge(sem["w1_in"], 16 * (KD + 1))
                for k in range(KD):
                    own.do(nc.vector.tensor_scalar(w1g[:, k, :], w1[:, k, :], gcol[:, k:k + 1], None, ALU.mult))
                dve.wait_ge(sem["iota_ok"], 1)
                own.do(nc.vector.tensor_copy(f.iota[:], iota_i[:]))
                dve.wait_ge(sem["w2_in"], 16)
                dve.wait_ge(sem["b2_in"], 16)
                own.settle()
                nc.vector.tensor_reduce(peak[:, 2:3], w2[:], AX.XY, ALU.max, apply_absolute_value=True
                                        ).then_inc(sem["peaks_ok"], 1)
                nc.vector.tensor_reduce(peak[0:EXPERTS, 3:4], b2t[:], AX.X, ALU.max, apply_absolute_value=True
                                        ).then_inc(sem["peaks_ok"], 1)
                nc.vector.tensor_reduce(peak[:, 1:2], w1g[:], AX.XY, ALU.max, apply_absolute_value=True
                                        ).then_inc(sem["peaks_ok"], 1)
                dve.wait_ge(sem["z_ps"], 1)
                dve.wait_ge(sem["b1_in"], 16)
                own.do(nc.vector.tensor_tensor(f.zbias[:], ps_z[:, 0:ZC], f.zbias[:], ALU.add))
                own.settle()
                nc.vector.tensor_reduce(peak[:, 4:5], f.zbias[:], AX.X, ALU.max, apply_absolute_value=True
                                        ).then_inc(sem["peaks_ok"], 1)
                dve.wait_ge(sem["u_ps"], 1)
                dve.wait_ge(sem["u_ok"], 1)
                for j in range(PAIRS):
                    for h in range(2):
                        rows = slice(h * HEAD, (h + 1) * HEAD)
                        at = (2 * (j % 2) + h) * SLICE
                        src_at = (2 * j + h) * SLICE
                        nc.vector.tensor_scalar(u[rows, j, at:at + SLICE], ps_u[rows, src_at:src_at + SLICE],
                                                bcol[rows, j:j + 1], None, ALU.add).then_inc(sem["u_ok"], 1)
                dve.wait_ge(sem["row_in"], 32)
                own.do(nc.vector.tensor_tensor(row[:, 0, :], row[:, 0, :], row[:, 1, :], ALU.add))
                dve.wait_ge(sem["m_ps"], 1)
                own.do(nc.vector.tensor_copy(mm[:], ps_m[:]))
                own.settle()
                own.do(nc.vector.tensor_tensor(mm[0:SLICE, 0, :], mm[0:SLICE, 0, :], row[:, 0, :], ALU.add))
                own.settle()
                nc.vector.tensor_reduce(peak[:, 0:1], mm[:], AX.XY, ALU.max, apply_absolute_value=True
                                        ).then_inc(sem["peaks_ok"], 1)
                dve.wait_ge(sem["peaks_ok"], 5)
                nc.vector.tensor_scalar(peak[:], peak[:], 1e-25, None, ALU.max).then_inc(sem["peaks_ok"], 1)
                dve.wait_ge(sem["peak_all_ok"], 1)
                own.do(nc.vector.tensor_copy(bound[:, 0:2], peak_all[:, 0:2]))
                own.do(nc.vector.scalar_tensor_tensor(bound[:, 2:3], peak_all[:, 1:2], float(D), peak_all[:, 4:5],
                                                      ALU.mult, ALU.add))
                own.settle()
                own.do(power_of_two(nc, pow2[:, 0:3], bound[:, 0:3]))
                own.settle()
                own.do(nc.vector.reciprocal(scale[:, 0:3], pow2[:, 0:3]))
                own.settle()
                own.do(nc.vector.tensor_scalar(scale[:, 0:3], scale[:, 0:3], W_TOP, None, ALU.mult))
                own.settle()
                own.do(nc.vector.tensor_scalar(bound[:, 3:4], peak_all[:, 3:4], scale[:, 2:3], 1.0 / ACT_SCALE,
                                               ALU.mult, ALU.mult))
                own.settle()
                own.do(nc.vector.tensor_tensor(bound[:, 3:4], bound[:, 3:4], peak_all[:, 2:3], ALU.max))
                own.settle()
                own.do(power_of_two(nc, pow2[:, 3:4], bound[:, 3:4]))
                own.settle()
                own.do(nc.vector.reciprocal(scale[:, 3:4], pow2[:, 3:4]))
                own.settle()
                own.do(nc.vector.tensor_scalar(scale[:, 3:4], scale[:, 3:4], W_TOP, None, ALU.mult))
                own.settle()
                own.do(nc.vector.tensor_scalar(b2scale[:], scale[:, 3:4], scale[:, 2:3], 1.0 / ACT_SCALE,
                                               ALU.mult, ALU.mult))
                own.do(nc.vector.tensor_scalar(f.hscale[:], scale[:, 2:3], 1.0 / ACT_SCALE, None, ALU.mult))
                own.do(nc.vector.tensor_scalar(f.m_unscale[:], pow2[:, 0:1], 1.0 / (W_TOP * ACT_SCALE), None,
                                               ALU.mult))
                own.do(nc.vector.tensor_scalar(f.z_unscale[:], pow2[:, 1:2], 1.0 / (W_TOP * ACT_SCALE), None,
                                               ALU.mult))
                own.do(nc.vector.tensor_scalar(f.o_unscale[:], pow2[:, 2:3], pow2[:, 3:4],
                                               ACT_SCALE / (W_TOP * W_TOP), ALU.mult, ALU.mult))
                own.settle()
                split(own, nc, [(f.m_hi[:, c, :], f.m_lo[:, c, :], mm[:, c, :], scale[:, 0:1]) for c in range(2)]
                      + [(f.w1_hi[:, k, :], f.w1_lo[:, k, :], w1g[:, k, :], scale[:, 1:2]) for k in range(KD)]
                      + [(f.w2_hi[:, c, :], f.w2_lo[:, c, :], w2[:, c, :], scale[:, 3:4]) for c in range(2)])
                own.settle()
                nc.vector.tensor_scalar(b2_hi[:], b2t[:], b2scale[0:EXPERTS], None, ALU.mult
                                        ).then_inc(sem["b2_ok"], 1)
                dve.wait_ge(sem["b2_ok"], 1)
                nc.vector.scalar_tensor_tensor(b2_lo[:], b2t[:], b2scale[0:EXPERTS], b2_hi[:], ALU.mult,
                                               ALU.subtract).then_inc(sem["b2_ok"], 1)
                dve.wait_ge(sem["b2_ok"], 2)
        m.clear_sems()


def third_pass(nc, keep, f, y_table, out):
    with ExitStack() as st:
        m = Mem(nc, st, keep.lasting)
        X, R = 6, 2
        yb = m.sb("c_y", [P, X, D])
        x1 = m.sb("c_x1", [P, X, D])
        x2 = m.sb("c_x2", [P, X, D])
        ob = m.sb("c_o", [P, R, D])
        nb = m.sb("c_n", [P, R, D])
        square = m.sb("c_square", [P, D])
        xT_hi = m.sb("c_xT_hi", [P, R, D], F16)
        xT_lo = m.sb("c_xT_lo", [P, R, D], F16)
        zb = m.sb("c_z", [P, R, ZC])
        hb = m.sb("c_h", [P, R, HC])
        hT_hi = m.sb("c_hT_hi", [P, R, HC], F16)
        hT_lo = m.sb("c_hT_lo", [P, R, HC], F16)
        conf3 = m.sb("c_conf3", [P, R, 3, EXPERTS], F16)
        confT = m.sb("c_confT", [3 * EXPERTS, R, P], F16)
        sum1 = m.sb("c_sum1", [P, R, 1])
        sum2 = m.sb("c_sum2", [P, R, 1])
        mean1 = m.sb("c_mean1", [P, R, 1])
        mean2 = m.sb("c_mean2", [P, R, 1])
        ssq1 = m.sb("c_ssq1", [P, R, 1])
        ssq2 = m.sb("c_ssq2", [P, R, 1])
        var1 = m.sb("c_var1", [P, R, 2])
        var2 = m.sb("c_var2", [P, R, 1])
        rs1 = m.sb("c_rs1", [P, R, 2])
        rs2 = m.sb("c_rs2", [P, R, 1])
        shift1 = m.sb("c_shift1", [P, R, 1])
        shift2 = m.sb("c_shift2", [P, R, 1])
        ratio = m.sb("c_ratio", [P, R, 1])
        rz = m.sb("c_rz", [P, R, 1])
        best = m.sb("c_best", [P, R, 8])
        best_at = m.sb("c_best_at", [P, R, 8], U32)
        gate = m.sb("c_gate", [P, R, 8])
        conf = m.sb("c_conf", [P, R, 3, EXPERTS])
        hconf = m.sb("c_hconf", [P, R, EXPERTS])
        ps_a = m.ps("cp_a", [P, R, D])
        ps_x = m.ps("cp_x", [P, D])
        ps_z = m.ps("cp_z", [P, D])
        ps_h = m.ps("cp_h", [P, D])
        ps_c = m.ps("cp_c", [3 * EXPERTS, 2 * D], F16)
        ps_o = m.ps("cp_o", [P, R, D])

        y_in = m.sems("c_y_in", X)
        out_done = m.sems("c_out", R)
        names = ("a_ps", "x1_ok", "mean1_ok", "ssq1_ok", "var1_ok", "rs1_ok", "shift1_ok", "ratio_ok", "rz_ok",
                 "x2_ok", "xT_ps", "xT_hi_ok", "xT_lo_ok", "z_ps", "z_ok", "best_ok", "best_at_ok", "gelu_ok",
                 "gap_ok", "tanh_ok", "share_ok", "picked_ok", "conf_ok", "hconf_ok", "conf_hi_ok", "conf3_ok",
                 "h_ok", "hT_ps", "hT_hi_ok", "hT_lo_ok", "confT_ok", "o_ps", "t_ok", "mean2_ok", "ssq2_ok",
                 "var2_ok", "rs2_ok", "shift2_ok", "n_ok", "gained_ok", "offset_ok", "o_ok")
        sem = {n: m.sem("c_" + n) for n in names}

        with nc.Block() as block:
            @block.sync
            def _(sp):
                def load(t):
                    if t.base >= X:
                        sp.wait_ge(sem["x1_ok"], t.n + 1 - X)
                    r = t.rows()
                    sp.dma_start(yb[0:r, t.slot(X), :], y_table[bass.ds(t.n * P, r), :]
                                 ).then_inc(y_in[t.slot(X)], 16)

                def store(t):
                    r = t.rows()
                    sp.wait_ge(sem["o_ok"], t.n + 1)
                    sp.dma_start(out[bass.ds(t.n * P, r), :], ob[0:r, t.slot(R), :]
                                 ).then_inc(out_done[t.slot(R)], 16)

                over_tiles(sp, X, [(5, load), (-3, store)])
                for q in range(R):
                    sp.wait_ge(out_done[q], 16 * len(range(q, TILES, R)))

            @block.tensor
            def _(pe):
                def attention(t):
                    b = t.slot(R)
                    if t.base >= R:
                        pe.wait_ge(sem["x1_ok"], t.n + 1 - R)
                    for c in range(2):
                        for n, (qs, ms) in enumerate(((keep.qT_hi, f.m_hi), (keep.qT_lo, f.m_hi),
                                                      (keep.qT_hi, f.m_lo))):
                            last = nc.tensor.matmul(ps_a[:, b, :], qs[:, t.n, c * P:(c + 1) * P], ms[:, c, :],
                                                    start=(c == 0 and n == 0), stop=(c == 1 and n == 2))
                    last.then_inc(sem["a_ps"], 1)

                def x2_transposes(t):
                    pe.wait_ge(sem["x2_ok"], t.n + 1)
                    if t.base >= 1:
                        pe.wait_ge(sem["xT_lo_ok"], t.n)
                    for k in range(KD):
                        last = nc.tensor.transpose(ps_x[:, k * P:(k + 1) * P],
                                                   x2[:, t.slot(X), k * P:(k + 1) * P], keep.ident[:])
                    last.then_inc(sem["xT_ps"], 1)

                def first_layer(t):
                    b = t.slot(R)
                    pe.wait_ge(sem["xT_lo_ok"], t.n + 1)
                    if t.base >= 1:
                        pe.wait_ge(sem["z_ok"], t.n)
                    for k in range(KD):
                        for n, (xs, ws) in enumerate(((xT_hi, f.w1_hi), (xT_lo, f.w1_hi), (xT_hi, f.w1_lo))):
                            last = nc.tensor.matmul(ps_z[:, 0:ZC], xs[:, b, k * P:(k + 1) * P], ws[:, k, :],
                                                    start=(k == 0 and n == 0), stop=(k == KD - 1 and n == 2))
                    last.then_inc(sem["z_ps"], 1)

                def h_transposes(t):
                    b = t.slot(R)
                    pe.wait_ge(sem["conf3_ok"], t.n + 1)
                    if t.base >= 1:
                        pe.wait_ge(sem["hT_lo_ok"], t.n)
                        pe.wait_ge(sem["confT_ok"], t.n)
                    nc.tensor.transpose(ps_c[:, 0:P], conf3[:, b].rearrange("p a e -> p (a e)"), f.ident16[:])
                    pe.wait_ge(sem["h_ok"], t.n + 1)
                    for c in range(2):
                        last = nc.tensor.transpose(ps_h[:, c * P:(c + 1) * P], hb[:, b, c * P:(c + 1) * P],
                                                   keep.ident[:])
                    last.then_inc(sem["hT_ps"], 1)

                def second_layer(t):
                    b = t.slot(R)
                    pe.wait_ge(sem["hT_lo_ok"], t.n + 1)
                    pe.wait_ge(sem["confT_ok"], t.n + 1)
                    if t.base >= R:
                        pe.wait_ge(sem["t_ok"], t.n + 1 - R)
                    nc.tensor.matmul(ps_o[:, b, :], confT[:, b, :], f.b2s[:], start=True, stop=False)
                    for c in range(2):
                        for n, (hs, ws) in enumerate(((hT_hi, f.w2_hi), (hT_lo, f.w2_hi), (hT_hi, f.w2_lo))):
                            last = nc.tensor.matmul(ps_o[:, b, :], hs[:, b, c * P:(c + 1) * P], ws[:, c, :],
                                                    start=False, stop=(c == 1 and n == 2))
                    last.then_inc(sem["o_ps"], 1)

                over_tiles(pe, X, [(0, first_layer), (1, x2_transposes), (2, attention), (-1, second_layer),
                                   (0, h_transposes)])

            @block.vector
            def _(dve):
                def add_attention(t):
                    q, b = t.slot(X), t.slot(R)
                    dve.wait_ge(sem["a_ps"], t.n + 1)
                    dve.wait_ge(y_in[q], 16 * (t.uses(X) + 1))
                    if t.base >= X:
                        dve.wait_ge(sem["o_ok"], t.n + 1 - X)
                    nc.vector.scalar_tensor_tensor(x1[:, q, :], ps_a[:, b, :], f.m_unscale[:], yb[:, q, :],
                                                   ALU.mult, ALU.add, accum_out=sum1[:, b]
                                                   ).then_inc(sem["x1_ok"], 1)

                def low_x2(t):
                    b = t.slot(R)
                    dve.wait_ge(sem["xT_hi_ok"], t.n + 1)
                    nc.vector.tensor_tensor(xT_lo[:, b, :], ps_x[:], xT_hi[:, b, :], ALU.subtract
                                            ).then_inc(sem["xT_lo_ok"], 1)

                def hidden(t):
                    b = t.slot(R)
                    dve.wait_ge(sem["z_ps"], t.n + 1)
                    dve.wait_ge(sem["rz_ok"], t.n + 1)
                    if t.base >= R:
                        dve.wait_ge(sem["gelu_ok"], t.n + 1 - R)
                    nc.vector.scalar_tensor_tensor(zb[:, b, :], ps_z[:, 0:ZC], rz[:, b], f.zbias[:], ALU.mult,
                                                   ALU.add).then_inc(sem["z_ok"], 1)

                def two_best(t):
                    b = t.slot(R)
                    dve.wait_ge(sem["z_ok"], t.n + 1)
                    stand_alone(dve)
                    nc.vector.max(best[:, b, :], zb[:, b, HC:ZC]).then_inc(sem["best_ok"], 1)
                    dve.wait_ge(sem["best_ok"], t.n + 1)
                    stand_alone(dve)
                    nc.vector.max_index(best_at[:, b, :], best[:, b, :], zb[:, b, HC:ZC]
                                        ).then_inc(sem["best_at_ok"], 1)

                def confidence(t):
                    b = t.slot(R)
                    dve.wait_ge(sem["share_ok"], t.n * 3 + 3)
                    for n in range(2):
                        nc.vector.tensor_scalar(conf[:, b, n, :], f.iota[:], gate[:, b, n:n + 1],
                                                gate[:, b, 4 + n:5 + n], ALU.is_equal, ALU.mult
                                                ).then_inc(sem["picked_ok"], 1)
                    dve.wait_ge(sem["picked_ok"], t.n * 2 + 2)
                    nc.vector.tensor_tensor(conf[:, b, 2, :], conf[:, b, 0, :], conf[:, b, 1, :], ALU.add
                                            ).then_inc(sem["conf_ok"], 1)
                    dve.wait_ge(sem["conf_ok"], t.n + 1)
                    nc.vector.tensor_scalar(hconf[:, b, :], conf[:, b, 2, :], f.hscale[:], None, ALU.mult
                                            ).then_inc(sem["hconf_ok"], 1)
                    if t.base >= R:
                        dve.wait_ge(sem["hT_ps"], t.n + 1 - R)
                    nc.vector.tensor_copy(conf3[:, b, 0:3:2, :],
                                          conf[:, b, 2, :].unsqueeze(1).to_broadcast([P, 2, EXPERTS])
                                          ).then_inc(sem["conf_hi_ok"], 1)
                    dve.wait_ge(sem["conf_hi_ok"], t.n + 1)
                    nc.vector.tensor_tensor(conf3[:, b, 1, :], conf[:, b, 2, :], conf3[:, b, 0, :], ALU.subtract
                                            ).then_inc(sem["conf3_ok"], 1)

                def weigh(t):
                    b = t.slot(R)
                    dve.wait_ge(sem["gelu_ok"], t.n + 1)
                    dve.wait_ge(sem["hconf_ok"], t.n + 1)
                    nc.vector.tensor_tensor(hb[:, b, :].rearrange("p (e j) -> p e j", e=EXPERTS),
                                            hb[:, b, :].rearrange("p (e j) -> p e j", e=EXPERTS),
                                            hconf[:, b, :].unsqueeze(2).to_broadcast([P, EXPERTS, HID]),
                                            ALU.mult).then_inc(sem["h_ok"], 1)

                def low_h(t):
                    b = t.slot(R)
                    dve.wait_ge(sem["hT_hi_ok"], t.n + 1)
                    nc.vector.tensor_tensor(hT_lo[:, b, :], ps_h[:, 0:HC], hT_hi[:, b, :], ALU.subtract
                                            ).then_inc(sem["hT_lo_ok"], 1)

                def add_experts(t):
                    q, b = t.slot(X), t.slot(R)
                    dve.wait_ge(sem["o_ps"], t.n + 1)
                    nc.vector.scalar_tensor_tensor(x2[:, q, :], ps_o[:, b, :], f.o_unscale[:], x2[:, q, :],
                                                   ALU.mult, ALU.add, accum_out=sum2[:, b]
                                                   ).then_inc(sem["t_ok"], 1)

                def gain(t):
                    b = t.slot(R)
                    dve.wait_ge(sem["n_ok"], t.n + 1)
                    nc.vector.tensor_tensor(nb[:, b, :], nb[:, b, :], f.gain[:], ALU.mult
                                            ).then_inc(sem["gained_ok"], 1)

                def finish(t):
                    b, q = t.slot(R), t.slot(X)
                    dve.wait_ge(sem["gained_ok"], t.n + 1)
                    dve.wait_ge(sem["offset_ok"], t.n + 1)
                    if t.base >= R:
                        dve.wait_ge(out_done[b], 16 * t.uses(R))
                    nc.vector.tensor_tensor(ob[:, b, :], x1[:, q, :], nb[:, b, :], ALU.add
                                            ).then_inc(sem["o_ok"], 1)

                over_tiles(dve, X, [(-1, low_h), (-2, add_experts), (0, hidden), (0, two_best), (-3, gain),
                                    (0, confidence), (0, weigh), (2, add_attention), (1, low_x2), (-3, finish)])

            @block.scalar
            def _(act):
                def norm1(t):
                    b, q = t.slot(R), t.slot(X)
                    act.wait_ge(sem["shift1_ok"], t.n + 1)
                    if t.base >= X:
                        act.wait_ge(sem["n_ok"], t.n + 1 - X)
                    nc.scalar.activation(x2[:, q, :], x1[:, q, :], ACT.Identity, bias=shift1[:, b],
                                         scale=rs1[:, b, 0:1]).then_inc(sem["x2_ok"], 1)

                def norm2(t):
                    b, q = t.slot(R), t.slot(X)
                    act.wait_ge(sem["shift2_ok"], t.n + 1)
                    if t.base >= R:
                        act.wait_ge(sem["o_ok"], t.n + 1 - R)
                    nc.scalar.activation(nb[:, b, :], x2[:, q, :], ACT.Identity, bias=shift2[:, b],
                                         scale=rs2[:, b]).then_inc(sem["n_ok"], 1)

                def square1(t):
                    b, q = t.slot(R), t.slot(X)
                    act.wait_ge(sem["mean1_ok"], t.n + 1)
                    nc.scalar.activation(square[:], x1[:, q, :], ACT.Square, bias=mean1[:, b],
                                         accum_out=ssq1[:, b]).then_inc(sem["ssq1_ok"], 1)

                def square2(t):
                    b, q = t.slot(R), t.slot(X)
                    act.wait_ge(sem["mean2_ok"], t.n + 1)
                    nc.scalar.activation(square[:], x2[:, q, :], ACT.Square, bias=mean2[:, b],
                                         accum_out=ssq2[:, b]).then_inc(sem["ssq2_ok"], 1)

                def high_x2(t):
                    b = t.slot(R)
                    act.wait_ge(sem["xT_ps"], t.n + 1)
                    if t.base >= R:
                        act.wait_ge(sem["z_ps"], t.n + 1 - R)
                    nc.scalar.activation(xT_hi[:, b, :], ps_x[:], ACT.Copy).then_inc(sem["xT_hi_ok"], 1)

                def gelu(t):
                    b = t.slot(R)
                    act.wait_ge(sem["z_ok"], t.n + 1)
                    if t.base >= R:
                        act.wait_ge(sem["hT_ps"], t.n + 1 - R)
                    nc.scalar.activation(hb[:, b, :], zb[:, b, 0:HC], ACT.Gelu_apprx_tanh
                                         ).then_inc(sem["gelu_ok"], 1)

                def tanh(t):
                    b = t.slot(R)
                    act.wait_ge(sem["gap_ok"], t.n + 1)
                    nc.scalar.activation(gate[:, b, 3:4], gate[:, b, 2:3], ACT.Tanh, scale=0.5
                                         ).then_inc(sem["tanh_ok"], 1)

                def high_h(t):
                    b = t.slot(R)
                    act.wait_ge(sem["hT_ps"], t.n + 1)
                    if t.base >= R:
                        act.wait_ge(sem["o_ps"], t.n + 1 - R)
                    nc.scalar.activation(hT_hi[:, b, :], ps_h[:, 0:HC], ACT.Copy).then_inc(sem["hT_hi_ok"], 1)
                    nc.scalar.activation(confT[:, b, :], ps_c[:, 0:P], ACT.Copy).then_inc(sem["confT_ok"], 1)

                over_tiles(act, X, [(-1, high_h), (1, norm1), (-3, norm2), (0, gelu), (0, tanh), (-2, square2),
                                    (1, high_x2), (2, square1)])

            @block.gpsimd
            def _(pool):
                def mean_1(t):
                    b = t.slot(R)
                    pool.wait_ge(sem["x1_ok"], t.n + 1)
                    if t.base >= R:
                        pool.wait_ge(sem["ssq1_ok"], t.n + 1 - R)
                    stand_alone(pool)
                    nc.gpsimd.tensor_scalar(mean1[:, b], sum1[:, b], -1.0 / D, 0.0, ALU.mult, ALU.add
                                            ).then_inc(sem["mean1_ok"], 1)

                def rstd1(t):
                    b = t.slot(R)
                    pool.wait_ge(sem["ssq1_ok"], t.n + 1)
                    if t.base >= R:
                        pool.wait_ge(sem["x2_ok"], t.n + 1 - R)
                        pool.wait_ge(sem["z_ok"], t.n + 1 - R)
                    stand_alone(pool)
                    small = ACT_SCALE ** -2
                    nc.gpsimd.tensor_scalar(var1[:, b, 0:1], ssq1[:, b], small / D, EPS * small, ALU.mult, ALU.add
                                            ).then_inc(sem["var1_ok"], 1)
                    nc.gpsimd.tensor_scalar(var1[:, b, 1:2], ssq1[:, b], (1 + EPS) * small / D, EPS * EPS * small,
                                            ALU.mult, ALU.add).then_inc(sem["var1_ok"], 1)
                    pool.wait_ge(sem["var1_ok"], t.n * 2 + 2)
                    nc.gpsimd.tensor_tensor(rs1[:, b, :], var1[:, b, :], f.mhalf2[:], ALU.pow
                                            ).then_inc(sem["rs1_ok"], 1)
                    pool.wait_ge(sem["rs1_ok"], t.n + 1)
                    nc.gpsimd.tensor_tensor(shift1[:, b], mean1[:, b], rs1[:, b, 0:1], ALU.mult
                                            ).then_inc(sem["shift1_ok"], 1)
                    nc.gpsimd.tensor_scalar(ratio[:, b], rs1[:, b, 1:2], rs1[:, b, 0:1], var1[:, b, 0:1],
                                            ALU.mult, ALU.mult).then_inc(sem["ratio_ok"], 1)
                    pool.wait_ge(sem["ratio_ok"], t.n + 1)
                    nc.gpsimd.tensor_tensor(rz[:, b], ratio[:, b], f.z_unscale[:], ALU.mult
                                            ).then_inc(sem["rz_ok"], 1)

                def shares(t):
                    b = t.slot(R)
                    g = gate[:, b, :]
                    pool.wait_ge(sem["best_ok"], t.n + 1)
                    nc.gpsimd.tensor_tensor(g[:, 2:3], best[:, b, 0:1], best[:, b, 1:2], ALU.subtract
                                            ).then_inc(sem["gap_ok"], 1)
                    pool.wait_ge(sem["best_at_ok"], t.n + 1)
                    stand_alone(pool)
                    nc.gpsimd.tensor_copy(g[:, 0:2], best_at[:, b, 0:2]).then_inc(sem["share_ok"], 1)
                    pool.wait_ge(sem["tanh_ok"], t.n + 1)
                    half = ACT_SCALE / 2
                    stand_alone(pool)
                    nc.gpsimd.tensor_scalar(g[:, 4:5], g[:, 3:4], half, half, ALU.mult, ALU.add
                                            ).then_inc(sem["share_ok"], 1)
                    nc.gpsimd.tensor_scalar(g[:, 5:6], g[:, 3:4], -half, half, ALU.mult, ALU.add
                                            ).then_inc(sem["share_ok"], 1)

                def mean_2(t):
                    b = t.slot(R)
                    pool.wait_ge(sem["t_ok"], t.n + 1)
                    if t.base >= R:
                        pool.wait_ge(sem["ssq2_ok"], t.n + 1 - R)
                    stand_alone(pool)
                    nc.gpsimd.tensor_scalar(mean2[:, b], sum2[:, b], -1.0 / D, 0.0, ALU.mult, ALU.add
                                            ).then_inc(sem["mean2_ok"], 1)

                def rstd2(t):
                    b = t.slot(R)
                    pool.wait_ge(sem["ssq2_ok"], t.n + 1)
                    if t.base >= R:
                        pool.wait_ge(sem["n_ok"], t.n + 1 - R)
                    stand_alone(pool)
                    nc.gpsimd.tensor_scalar(var2[:, b], ssq2[:, b], 1.0 / D, EPS * ACT_SCALE ** 2, ALU.mult,
                                            ALU.add).then_inc(sem["var2_ok"], 1)
                    pool.wait_ge(sem["var2_ok"], t.n + 1)
                    nc.gpsimd.tensor_tensor(rs2[:, b], var2[:, b], keep.mhalf[:], ALU.pow
                                            ).then_inc(sem["rs2_ok"], 1)
                    pool.wait_ge(sem["rs2_ok"], t.n + 1)
                    nc.gpsimd.tensor_tensor(shift2[:, b], mean2[:, b], rs2[:, b], ALU.mult
                                            ).then_inc(sem["shift2_ok"], 1)

                def offset(t):
                    q = t.slot(X)
                    pool.wait_ge(sem["x2_ok"], t.n + 1)
                    nc.gpsimd.tensor_tensor(x1[:, q, :], x1[:, q, :], f.offset[:], ALU.add
                                            ).then_inc(sem["offset_ok"], 1)

                over_tiles(pool, X, [(-2, mean_2), (-1, offset), (0, shares), (-2, rstd2), (2, mean_1),
                                     (2, rstd1)])


class Namespace:
    pass


def program(nc, x, src, dst, gnn_W, gnn_b, W_in, b_in, Wq, Wk, Wv, W_out, b_out, Wg, W1, b1, W2, b2, ln_g, ln_b,
            out_g, out_b, out):
    h_table = nc.dram_tensor("h_table", [N, D], F32).ap()
    y_table = nc.dram_tensor("y_table", [N + SPARE, D], F32).ap()
    dinv_table = nc.dram_tensor("dinv_table", [TILES * P, 1], F32).ap()
    keep, f = Namespace(), Namespace()
    with ExitStack() as st:
        keep.lasting = st.enter_context(ExitStack())
        m = Mem(nc, st, keep.lasting)
        keep.ident = m.sb("ident", [P, P])
        keep.mhalf = m.sb("mhalf", [P, 1])
        keep.one = m.sb("one", [P, 1])
        keep.src = m.sb("src_t", [P, ETILES], I32)
        keep.dst = m.sb("dst_t", [P, ETILES], I32)
        keep.dstf = m.sb("dst_f", [P, ETILES])
        keep.target = m.sb("target", [P, ETILES], I32)
        keep.mean = m.sb("mean", [P, TILES])
        keep.rstd = m.sb("rstd", [P, TILES])
        keep.dinv = m.sb("dinv", [P, TILES])
        keep.hcoef = m.sb("hcoef", [P, TILES])
        keep.unscale = m.sb("unscale", [P, 2])
        keep.kmax = m.sb("kmax", [P, QC])
        keep.rk = m.sb("rk", [P, 2])
        keep.qT_hi = m.sb("qT_hi", [P, TILES, QC], F16)
        keep.qT_lo = m.sb("qT_lo", [P, TILES, QC], F16)
        keep.g = m.sb("g", [P, 2, D])
        with ExitStack() as st2:
            keep.k = Mem(nc, st2, keep.lasting).sb("k_logits", [P, TILES, QC])
            with ExitStack() as st3:
                w3 = Mem(nc, st3, keep.lasting)
                keep.w_hi = w3.sb("w_hi", [P, KD, 2 * D], F16)
                keep.w_lo = w3.sb("w_lo", [P, KD, 2 * D], F16)
                keep.ones_b = w3.sb("ones_b", [64, P], F16)
                keep.bias16 = w3.sb("bias16", [64, D], F16)
                prepare(nc, keep, src, dst, gnn_W, W_in, b_in, Wq, Wk, dinv_table, y_table)
                first_pass(nc, keep, x, h_table, y_table)
            second_pass(nc, keep, x, dst, h_table, y_table, dinv_table)
        f.zbias = m.sb("zbias", [P, ZC])
        f.gain = m.sb("gain", [P, D])
        f.offset = m.sb("offset", [P, D])
        f.b2s = m.sb("b2s", [3 * EXPERTS, D], F16)
        f.ident16 = m.sb("ident16", [P, P], F16)
        f.iota = m.sb("iota8", [P, EXPERTS])
        f.hscale = m.sb("hscale", [P, 1])
        f.mhalf2 = m.sb("mhalf2", [P, 2])
        f.m_unscale = m.sb("m_unscale", [P, 1])
        f.z_unscale = m.sb("z_unscale", [P, 1])
        f.o_unscale = m.sb("o_unscale", [P, 1])
        f.m_hi = m.sb("m_hi", [P, 2, D], F16)
        f.m_lo = m.sb("m_lo", [P, 2, D], F16)
        f.w1_hi = m.sb("w1_hi", [P, KD, ZC], F16)
        f.w1_lo = m.sb("w1_lo", [P, KD, ZC], F16)
        f.w2_hi = m.sb("w2_hi", [P, 2, D], F16)
        f.w2_lo = m.sb("w2_lo", [P, 2, D], F16)
        fold(nc, keep, f, W_in, b_in, Wv, W_out, b_out, gnn_b, Wg, W1, b1, W2, b2, ln_g, ln_b, out_g, out_b)
        third_pass(nc, keep, f, y_table, out)


_INS = ["x", "src", "dst", "L0_gnn_W", "L0_gnn_b", "L0_mix_W_in", "L0_mix_b_in", "L0_mix_Wq", "L0_mix_Wk",
        "L0_mix_Wv", "L0_mix_W_out", "L0_mix_b_out", "L0_ffn_Wg", "L0_ffn_W1", "L0_ffn_b1", "L0_ffn_W2",
        "L0_ffn_b2", "L0_ffn_ln_g", "L0_ffn_ln_b", "L0_ffn_out_g", "L0_ffn_out_b"]


def kernel(**inputs):
    import numpy as np
    import concourse.bacc as bacc
    from concourse.bass_utils import run_bass_kernel_spmd

    nc = bacc.Bacc("TRN2", target_bir_lowering=False, num_devices=1)
    arrays, args = {}, []
    for name in _INS:
        array = np.ascontiguousarray(inputs[name])
        arrays[f"in_{name}"] = array
        args.append(nc.dram_tensor(f"in_{name}", array.shape, mybir.dt.from_np(array.dtype),
                                   kind="ExternalInput").ap())
    out = nc.dram_tensor("out_x", (N, D), F32, kind="ExternalOutput").ap()
    program(nc, *args, out)
    result = run_bass_kernel_spmd(nc, [arrays], core_ids=[0])
    return result.results[0]["out_x"]
```

```python
from contextlib import ExitStack

import concourse.bass as bass
from concourse import mybir

ALU = mybir.AluOpType
ACT = mybir.ActivationFunctionType
AX = mybir.AxisListType
F32 = mybir.dt.float32
F16 = mybir.dt.float16
I32 = mybir.dt.int32
U32 = mybir.dt.uint32
ROP = bass.bass_isa.ReduceOp

P = 128
N, D = 10000, 512
EDGES = 2500
HEADS, HEAD, SLICE = 8, 64, 32
QC = HEADS * SLICE
EXPERTS, HID = 8, 32
HC = EXPERTS * HID
ZC = HC + EXPERTS
KD = D // P
PAIRS = HEADS // 2
TILES = -(-N // P)
TAIL = N - (TILES - 1) * P
ETILES = -(-EDGES // P)
ETAIL = EDGES - (ETILES - 1) * P
EPS = 1e-5
ACT_SCALE = 1024.0
W_TOP = 2.0 ** 14
EXP_MASK = 0x7F800000
SPARE = P


class Tile:

    def __init__(self, base, unroll=1, j=None):
        self.base, self.unroll, self.j = base, unroll, j
        self.n = base if j is None else j * unroll + base

    def slot(self, ring):
        return self.base % ring

    def uses(self, ring):
        if self.j is None:
            return self.base // ring
        return self.j * (self.unroll // ring) + self.base // ring

    def rows(self):
        return TAIL if self.j is None and self.base == TILES - 1 else P


def over_tiles(eng, unroll, stages):
    ahead, behind = max(o for o, _ in stages), min(o for o, _ in stages)
    start = unroll * -(-(unroll - behind) // unroll)
    count = (TILES - 1 - ahead - start) // unroll

    def peeled(lo, hi):
        for s in range(lo, hi):
            for o, body in stages:
                if 0 <= s + o < TILES:
                    body(Tile(s + o))

    peeled(-ahead, start)
    with eng.Fori(0, count) as j:
        for c in range(unroll):
            for o, body in stages:
                body(Tile(start + c + o, unroll, j))
    peeled(start + count * unroll, TILES - behind)


def stand_alone(eng):
    eng.nop(nofuse=True)


class Mem:

    def __init__(self, nc, stack, lasting):
        self.nc, self.stack, self.lasting, self.own = nc, stack, lasting, []

    def sb(self, name, shape, dt=F32):
        return self.stack.enter_context(self.nc.sbuf_tensor(name, shape, dt))

    def ps(self, name, shape, dt=F32):
        return self.stack.enter_context(self.nc.psum_tensor(name, shape, dt))

    def sem(self, name):
        handle = self.lasting.enter_context(self.nc.semaphore(name))
        self.own.append(handle)
        return handle

    def clear_sems(self):
        for handle in self.own:
            self.nc.gpsimd.sem_clear(handle)
        self.nc.all_engine_barrier()

    def sems(self, name, n):
        return [self.sem(f"{name}{i}") for i in range(n)]


class Arena(Mem):

    def __init__(self, nc, stack, lasting, tensor):
        super().__init__(nc, stack, lasting)
        self.flat, self.at = tensor[:].rearrange("p a b -> p (a b)"), 0

    def sb(self, name, shape, dt=F32):
        count = 1
        for n in shape[1:]:
            count *= n
        words = -(-count * (2 if dt == F16 else 4) // 4)
        view = self.flat[0:shape[0], self.at:self.at + words]
        self.at += words
        if dt != F32:
            view = view.bitcast(dt)
        if len(shape) == 3:
            view = view.rearrange("p (a b) -> p a b", a=shape[1])
        if len(shape) == 4:
            view = view.rearrange("p (a b c) -> p a b c", a=shape[1], b=shape[2])
        return view


class Chain:

    def __init__(self, eng, sem):
        self.eng, self.sem, self.n = eng, sem, 0

    def do(self, ins):
        self.n += 1
        return ins.then_inc(self.sem, 1)

    def settle(self):
        self.eng.wait_ge(self.sem, self.n)


def split(own, nc, jobs):
    for hi, lo, value, scale in jobs:
        own.do(nc.vector.tensor_scalar(hi, value, scale, None, ALU.mult))
    own.settle()
    for hi, lo, value, scale in jobs:
        own.do(nc.vector.scalar_tensor_tensor(lo, value, scale, hi, ALU.mult, ALU.subtract))


def power_of_two(nc, out, value):
    return nc.vector.tensor_scalar(out.bitcast(I32), value.bitcast(I32), EXP_MASK, None, ALU.bitwise_and)


def prepare(nc, keep, src, dst, W_gnn, W_in, b_in, Wq, Wk, dinv_table, y_table):
    with ExitStack() as st:
        m = Arena(nc, st, st, keep.k)
        win = m.sb("p_win", [P, KD, D])
        wg = m.sb("p_wg", [P, KD, D])
        winT = m.sb("p_winT", [P, PAIRS, D])
        wqk = m.sb("p_wqk", [P, KD, D])
        bd = m.sb("p_bd", [P, 2, 2, SLICE])
        bcol = m.sb("p_bcol", [P, PAIRS])
        bcolB = m.sb("p_bcolB", [P, PAIRS, 64])
        brow = m.sb("p_brow", [64, D])
        brow_hi = m.sb("p_brow_hi", [64, D], F16)
        peak = m.sb("p_peak", [P, 2])
        peakb = m.sb("p_peakb", [P, 1])
        peak_all = m.sb("p_peak_all", [P, 2])
        pow2 = m.sb("p_pow2", [P, 2])
        wscale = m.sb("p_wscale", [P, 2])
        dstrow = m.sb("p_dstrow", [P, ETILES * P], I32)
        iota_i = m.sb("p_iota_i", [P, P], I32)
        iota = m.sb("p_iota", [P, P])
        spare_i = m.sb("p_spare_i", [P, 1], I32)
        spare = m.sb("p_spare", [P, 1])
        earlier = m.sb("p_earlier", [P, P])
        junk = m.sb("p_junk", [P, P])
        part = m.sb("p_part", [P, 2, ETILES], I32)
        partf = m.sb("p_partf", [P, 2, ETILES])
        hot_lo = m.sb("p_hot_lo", [P, ETILES, P], F16)
        hot_hi = m.sb("p_hot_hi", [P, ETILES, TILES], F16)
        deg = m.sb("p_deg", [P, TILES])
        mhalf = m.sb("p_mhalf", [P, TILES])
        dinvT = m.sb("p_dinvT", [TILES, P])
        prev = m.sb("p_prev", [P, ETILES])
        move = m.sb("p_move", [P, ETILES])
        zero = m.sb("p_zero", [P, D])
        ps_t = m.ps("pp_t", [P, 2, D])
        ps_w = m.ps("pp_w", [P, 2, D])
        ps_b = m.ps("pp_b", [64, D])
        ps_d = m.ps("pp_d", [P, D])
        ps_i = m.ps("pp_i", [P, D])

        (win_in, wg_in, bd_in, bcol_in, edges_in, dstrow_in, dinv_out, spare_out) = (
            m.sem("p_" + n) for n in ("win_in", "wg_in", "bd_in", "bcol_in", "edges_in", "dstrow_in",
                                      "dinv_out", "spare_out"))
        (filled, ident_ok, earlier_ok, iota_ok, pool_own, peaks_ok, peak_all_ok, deg_ok, dinv_ok, dve_own,
         winT_ps, winT_ok, wqk_ps, wqk_ok, bcolB_ok, brow_ps, hot_ok, deg_ps, dinvT_ps, dinvT_ok,
         act_own) = (
            m.sem("p_" + n) for n in (
                "filled", "ident_ok", "earlier_ok", "iota_ok", "pool_own", "peaks_ok", "peak_all_ok", "deg_ok",
                "dinv_ok", "dve_own", "winT_ps", "winT_ok", "wqk_ps", "wqk_ok", "bcolB_ok", "brow_ps", "hot_ok",
                "deg_ps", "dinvT_ps", "dinvT_ok", "act_own"))

        with nc.Block() as block:
            @block.gpsimd
            def _(pool):
                own = Chain(pool, pool_own)
                own.do(nc.gpsimd.memset(keep.ident[:], 0.0))
                own.do(nc.gpsimd.memset(earlier[:], 1.0))
                nc.gpsimd.memset(bd[:], 0.0).then_inc(filled, 1)
                nc.gpsimd.memset(keep.src[:], 0).then_inc(filled, 1)
                nc.gpsimd.memset(keep.dst[:], N).then_inc(filled, 1)
                nc.gpsimd.memset(dstrow[:], N).then_inc(filled, 1)
                nc.gpsimd.memset(zero[:], 0.0).then_inc(filled, 1)
                own.do(nc.gpsimd.memset(keep.mhalf[:], -0.5))
                own.do(nc.gpsimd.memset(mhalf[:], -0.5))
                own.settle()
                nc.gpsimd.affine_select(out=keep.ident[:], in_=keep.ident[:], compare_op=ALU.not_equal,
                                        fill=1.0, base=0, pattern=[[-1, P]],
                                        channel_multiplier=1).then_inc(ident_ok, 1)
                nc.gpsimd.affine_select(out=earlier[:], in_=earlier[:], compare_op=ALU.is_gt, fill=0.0, base=0,
                                        pattern=[[-1, P]], channel_multiplier=1).then_inc(earlier_ok, 1)
                nc.gpsimd.iota(iota_i[:], [[1, P]], base=0, channel_multiplier=0).then_inc(iota_ok, 1)
                nc.gpsimd.iota(spare_i[:], [[1, 1]], base=N, channel_multiplier=1).then_inc(iota_ok, 1)
                pool.wait_ge(deg_ok, 1)
                nc.gpsimd.tensor_tensor(keep.dinv[:], deg[:], mhalf[:], ALU.pow).then_inc(dinv_ok, 1)
                pool.wait_ge(peaks_ok, 3)
                nc.gpsimd.partition_all_reduce(peak_all[:], peak[:], P, ROP.max).then_inc(peak_all_ok, 1)

            @block.sync
            def _(sp):
                sp.dma_start(win[:], W_in.rearrange("(k p) n -> p k n", p=P)).then_inc(win_in, 16)
                sp.dma_start(wg[:], W_gnn.rearrange("(k p) n -> p k n", p=P)).then_inc(wg_in, 16)
                sp.wait_ge(filled, 5)
                for h in range(2):
                    rows = slice(h * HEAD, (h + 1) * HEAD)
                    sp.dma_start(bd[rows, 0, h, :], Wq).then_inc(bd_in, 16)
                    sp.dma_start(bd[rows, 1, h, :], Wk).then_inc(bd_in, 16)
                sp.dma_start(y_table[N:N + SPARE, :], zero[:]).then_inc(spare_out, 16)
                sp.wait_ge(dinvT_ok, 1)
                sp.dma_start(dinv_table.rearrange("(t p) o -> t (p o)", p=P), dinvT[:]).then_inc(dinv_out, 16)
                sp.wait_ge(dinv_out, 16)
                sp.wait_ge(spare_out, 16)

            @block.scalar
            def _(act):
                act.wait_ge(filled, 5)
                full = (ETILES - 1) * P
                for vec, tile in ((src, keep.src), (dst, keep.dst)):
                    act.dma_start(tile[:, 0:ETILES - 1],
                                  vec[0:full].rearrange("(j p) -> p j", p=P),
                                  allow_slow_non_contiguous=True).then_inc(edges_in, 16)
                    act.dma_start(tile[0:ETAIL, ETILES - 1:ETILES],
                                  vec[full:EDGES].rearrange("(p o) -> p o", o=1)).then_inc(edges_in, 16)
                act.dma_start(dstrow[:, 0:EDGES],
                              dst.rearrange("(a e) -> a e", a=1).to_broadcast([P, EDGES])).then_inc(dstrow_in, 16)
                act.dma_start(bcol[:], b_in.rearrange("(j p) -> p j", p=P),
                              allow_slow_non_contiguous=True).then_inc(bcol_in, 16)
                for j in range(PAIRS):
                    act.wait_ge(winT_ps, j + 1)
                    nc.scalar.activation(winT[:, j, :], ps_t[:, j % 2, :], ACT.Copy).then_inc(winT_ok, 1)
                for k in range(KD):
                    act.wait_ge(wqk_ps, k + 1)
                    for qk in range(2):
                        nc.scalar.activation(
                            wqk[:, k, qk * QC:(qk + 1) * QC].rearrange("p (j c) -> p j c", j=PAIRS),
                            ps_w[:, k % 2, :].rearrange("p (j q c) -> p q j c", j=PAIRS, q=2)[:, qk],
                            ACT.Copy).then_inc(wqk_ok, 1)
                act.wait_ge(dinvT_ps, 1)
                nc.scalar.activation(dinvT[:], ps_i[0:TILES, 0:P], ACT.Copy).then_inc(dinvT_ok, 1)

            @block.tensor
            def _(pe):
                pe.wait_ge(ident_ok, 1)
                pe.wait_ge(win_in, 16)
                for j in range(PAIRS):
                    if j >= 2:
                        pe.wait_ge(winT_ok, j - 1)
                    for k in range(KD):
                        last = nc.tensor.transpose(ps_t[:, j % 2, k * P:(k + 1) * P],
                                                   win[:, k, j * P:(j + 1) * P], keep.ident[:])
                    last.then_inc(winT_ps, 1)
                pe.wait_ge(winT_ok, PAIRS)
                pe.wait_ge(bd_in, 64)
                for k in range(KD):
                    if k >= 2:
                        pe.wait_ge(wqk_ok, 2 * (k - 1))
                    for j in range(PAIRS):
                        last = nc.tensor.matmul(ps_w[:, k % 2, j * P:(j + 1) * P],
                                                winT[:, j, k * P:(k + 1) * P],
                                                bd[:].rearrange("p q h s -> p (q h s)"), start=True, stop=True)
                    last.then_inc(wqk_ps, 1)
                pe.wait_ge(bcolB_ok, 1)
                for j in range(PAIRS):
                    last = nc.tensor.matmul(ps_b[:, j * P:(j + 1) * P], bcolB[:, j, :],
                                            bd[:].rearrange("p q h s -> p (q h s)"), start=True, stop=True)
                last.then_inc(brow_ps, 1)
                pe.wait_ge(hot_ok, 2 * ETILES)
                for j in range(ETILES):
                    last = nc.tensor.matmul(ps_d[:, 0:TILES], hot_lo[:, j, :], hot_hi[:, j, :],
                                            start=(j == 0), stop=(j == ETILES - 1))
                last.then_inc(deg_ps, 1)
                pe.wait_ge(dinv_ok, 1)
                nc.tensor.transpose(ps_i[0:TILES, 0:P], keep.dinv[:], keep.ident[:]).then_inc(dinvT_ps, 1)

            @block.vector
            def _(dve):
                own = Chain(dve, dve_own)
                own.do(nc.vector.memset(keep.bias16[:], 0.0))
                own.do(nc.vector.memset(keep.ones_b[:], ACT_SCALE))
                own.do(nc.vector.memset(keep.one[:], 1.0))
                dve.wait_ge(edges_in, 64)
                dve.wait_ge(iota_ok, 2)
                own.do(nc.vector.tensor_scalar(part[:, 0, :], keep.dst[:], P - 1, None, ALU.bitwise_and))
                own.do(nc.vector.tensor_scalar(part[:, 1, :], keep.dst[:], 7, None, ALU.logical_shift_right))
                own.do(nc.vector.tensor_copy(iota[:], iota_i[:]))
                own.do(nc.vector.tensor_copy(spare[:], spare_i[:]))
                own.do(nc.vector.tensor_copy(keep.dstf[:], keep.dst[:]))
                own.settle()
                own.do(nc.vector.tensor_copy(partf[:], part[:]))
                own.settle()
                for j in range(ETILES):
                    nc.vector.tensor_scalar(hot_lo[:, j, :], iota[:], partf[:, 0, j:j + 1], None,
                                            ALU.is_equal).then_inc(hot_ok, 1)
                    nc.vector.tensor_scalar(hot_hi[:, j, :], iota[:, 0:TILES], partf[:, 1, j:j + 1], None,
                                            ALU.is_equal).then_inc(hot_ok, 1)
                dve.wait_ge(bcol_in, 16)
                nc.vector.tensor_copy(bcolB[:], bcol[:].unsqueeze(2).to_broadcast([P, PAIRS, 64])
                                      ).then_inc(bcolB_ok, 1)
                dve.wait_ge(deg_ps, 1)
                nc.vector.tensor_scalar(deg[:], ps_d[:, 0:TILES], 1.0, None, ALU.add).then_inc(deg_ok, 1)
                dve.wait_ge(dstrow_in, 16)
                dve.wait_ge(earlier_ok, 1)
                for j in range(ETILES):
                    own.do(nc.vector.scalar_tensor_tensor(junk[:], dstrow[:, j * P:(j + 1) * P],
                                                          keep.dstf[:, j:j + 1], earlier[:], ALU.is_equal,
                                                          ALU.mult, accum_out=prev[:, j:j + 1]))
                    own.settle()
                own.do(nc.vector.tensor_scalar(prev[:], prev[:], 0.0, None, ALU.is_gt))
                own.do(nc.vector.tensor_scalar(move[:], keep.dstf[:], -1.0, spare[:], ALU.mult, ALU.add))
                own.settle()
                own.do(nc.vector.tensor_tensor(move[:], move[:], prev[:], ALU.mult))
                own.settle()
                own.do(nc.vector.tensor_tensor(move[:], move[:], keep.dstf[:], ALU.add))
                own.settle()
                own.do(nc.vector.tensor_copy(keep.target[:], move[:]))
                dve.wait_ge(wg_in, 16)
                nc.vector.tensor_reduce(peak[:, 1:2], wg[:], AX.XY, ALU.max,
                                        apply_absolute_value=True).then_inc(peaks_ok, 1)
                dve.wait_ge(brow_ps, 1)
                for qk in range(2):
                    own.do(nc.vector.tensor_copy(
                        brow[:, qk * QC:(qk + 1) * QC].rearrange("p (j c) -> p j c", j=PAIRS),
                        ps_b[:].rearrange("p (j q c) -> p q j c", j=PAIRS, q=2)[:, qk]))
                own.do(nc.vector.memset(peakb[:], 1e-30))
                own.settle()
                own.do(nc.vector.tensor_reduce(peakb[0:64], brow[:], AX.X, ALU.max, apply_absolute_value=True))
                dve.wait_ge(wqk_ok, 2 * KD)
                own.do(nc.vector.tensor_reduce(peak[:, 0:1], wqk[:], AX.XY, ALU.max, apply_absolute_value=True))
                own.settle()
                nc.vector.tensor_tensor(peak[:, 0:1], peak[:, 0:1], peakb[:], ALU.max).then_inc(peaks_ok, 1)
                dve.wait_ge(peaks_ok, 2)
                nc.vector.tensor_scalar(peak[:, 1:2], peak[:, 1:2], 1e-30, None, ALU.max).then_inc(peaks_ok, 1)
                dve.wait_ge(peak_all_ok, 1)
                own.do(power_of_two(nc, pow2[:], peak_all[:]))
                own.settle()
                own.do(nc.vector.reciprocal(wscale[:], pow2[:]))
                own.settle()
                own.do(nc.vector.tensor_scalar(wscale[:], wscale[:], W_TOP, None, ALU.mult))
                own.do(nc.vector.tensor_scalar(keep.unscale[:], pow2[:], 1.0 / (W_TOP * ACT_SCALE), None, ALU.mult))
                dve.wait_ge(dinv_ok, 1)
                own.settle()
                own.do(nc.vector.tensor_scalar(keep.hcoef[:], keep.dinv[:], keep.unscale[:, 1:2], None, ALU.mult))
                split(own, nc, [(keep.w_hi[:, k, col:col + D], keep.w_lo[:, k, col:col + D], w[:, k, :],
                                 wscale[:, c:c + 1])
                                for w, col, c in ((wqk, 0, 0), (wg, D, 1)) for k in range(KD)])
                own.do(nc.vector.tensor_scalar(brow_hi[:], brow[:], wscale[0:64, 0:1], None, ALU.mult))
                own.settle()
                own.do(nc.vector.tensor_copy(keep.bias16[0:1, :], brow_hi[0:1, :]))
                own.do(nc.vector.scalar_tensor_tensor(keep.bias16[32:33, :], brow[32:33, :], wscale[32:33, 0:1],
                                                      brow_hi[32:33, :], ALU.mult, ALU.subtract))
                own.settle()
        m.clear_sems()


def first_pass(nc, keep, x, h_table, y_table):
    with ExitStack() as st:
        m = Mem(nc, st, keep.lasting)
        X, R = 4, 2
        xb = m.sb("a_x", [P, X, D])
        xn = m.sb("a_xn", [P, R, D])
        xT_hi = m.sb("a_xT_hi", [P, R, D], F16)
        xT_lo = m.sb("a_xT_lo", [P, R, D], F16)
        hb = m.sb("a_h", [P, R, D])
        qb = m.sb("a_q", [P, X, QC])
        bias = keep.g[:, 0, :]
        stats = m.sb("a_stats", [P, R, 6])
        mv = m.sb("a_mv", [P, R, 2])
        var = m.sb("a_var", [P, R, 1])
        top = m.sb("a_top", [P, R, HEADS])
        total = m.sb("a_total", [P, R, HEADS])
        ps_x = m.ps("ap_x", [P, R, D])
        ps_qk = m.ps("ap_qk", [P, R, D])
        ps_h = m.ps("ap_h", [P, R, D])
        ps_q = m.ps("ap_q", [P, R, D])

        x_in = m.sems("a_x_in", X)
        y_out = m.sems("a_y_out", X)
        h_out = m.sems("a_h_out", R)
        (stats_ok, mv_ok, var_ok, rstd_ok, mean_ok, xn_ok, xT_ps, xT_hi_ok, xT_lo_ok, qk_ps, h_ps, k_ok, kmax_ok,
         q_in_ok, bias_ps, bias_ok, top_ok, less_ok, exp_ok, total_ok, recip_ok, q_ok, q_ps, qT_hi_ok, qT_lo_ok, h_ok, y_ok) = (
            m.sem("a_" + n) for n in (
                "stats_ok", "mv_ok", "var_ok", "rstd_ok", "mean_ok", "xn_ok", "xT_ps", "xT_hi_ok", "xT_lo_ok",
                "qk_ps", "h_ps", "k_ok", "kmax_ok", "q_in_ok", "bias_ps", "bias_ok", "top_ok", "less_ok", "exp_ok", "total_ok", "recip_ok", "q_ok",
                "q_ps", "qT_hi_ok", "qT_lo_ok", "h_ok", "y_ok"))

        def heads(ap):
            return ap.rearrange("p (h s) -> p h s", h=HEADS)

        with nc.Block() as block:
            @block.sync
            def _(sp):
                def load(t):
                    if t.base >= X:
                        sp.wait_ge(y_out[t.slot(X)], 16 * t.uses(X))
                    r = t.rows()
                    sp.dma_start(xb[0:r, t.slot(X), :], x[bass.ds(t.n * P, r), :]).then_inc(x_in[t.slot(X)], 16)

                def store(t):
                    r = t.rows()
                    sp.wait_ge(h_ok, t.n + 1)
                    sp.dma_start(h_table[bass.ds(t.n * P, r), :], hb[0:r, t.slot(R), :]
                                 ).then_inc(h_out[t.slot(R)], 16)
                    sp.wait_ge(y_ok, t.n + 1)
                    sp.dma_start(y_table[bass.ds(t.n * P, r), :], xb[0:r, t.slot(X), :]
                                 ).then_inc(y_out[t.slot(X)], 16)

                over_tiles(sp, X, [(3, load), (0, store)])
                for q in range(X):
                    sp.wait_ge(y_out[q], 16 * len(range(q, TILES, X)))
                for q in range(R):
                    sp.wait_ge(h_out[q], 16 * len(range(q, TILES, R)))

            @block.gpsimd
            def _(pool):
                def rstd(t):
                    b = t.slot(R)
                    pool.wait_ge(mv_ok, t.n + 1)
                    stand_alone(pool)
                    nc.gpsimd.tensor_scalar(var[:, b], mv[:, b, 1:2], EPS, ACT_SCALE ** -2, ALU.add, ALU.mult
                                            ).then_inc(var_ok, 1)
                    nc.gpsimd.tensor_copy(keep.mean[:, bass.ds(t.n, 1)], mv[:, b, 0:1]).then_inc(mean_ok, 1)
                    pool.wait_ge(var_ok, t.n + 1)
                    nc.gpsimd.tensor_tensor(keep.rstd[:, bass.ds(t.n, 1)], var[:, b], keep.mhalf[:], ALU.pow
                                            ).then_inc(rstd_ok, 1)

                def normalise_q(t):
                    q = t.slot(X)
                    pool.wait_ge(recip_ok, t.n + 1)
                    nc.gpsimd.tensor_tensor(heads(qb[:, q, :]), heads(qb[:, q, :]),
                                            total[:, t.slot(R), :].unsqueeze(2).to_broadcast([P, HEADS, SLICE]),
                                            ALU.mult).then_inc(q_ok, 1)

                over_tiles(pool, X, [(-2, normalise_q), (2, rstd)])

            @block.vector
            def _(dve):
                def norm(t):
                    dve.wait_ge(rstd_ok, t.n + 1)
                    dve.wait_ge(mean_ok, t.n + 1)
                    if t.base >= R:
                        dve.wait_ge(xT_ps, t.n + 1 - R)
                    nc.vector.tensor_scalar(xn[:, t.slot(R), :], xb[:, t.slot(X), :],
                                            keep.mean[:, bass.ds(t.n, 1)], keep.rstd[:, bass.ds(t.n, 1)],
                                            ALU.subtract, ALU.mult).then_inc(xn_ok, 1)

                def statistics(t):
                    dve.wait_ge(x_in[t.slot(X)], 16 * (t.uses(X) + 1))
                    nc.vector.bn_stats(stats[:, t.slot(R), :], xb[:, t.slot(X), :]).then_inc(stats_ok, 1)

                def aggregate(t):
                    dve.wait_ge(stats_ok, t.n + 1)
                    if t.base >= R:
                        dve.wait_ge(mean_ok, t.n + 1 - R)
                    stand_alone(dve)
                    nc.vector.bn_aggr(mv[:, t.slot(R), :], stats[:, t.slot(R), :]).then_inc(mv_ok, 1)

                def low_half(t):
                    dve.wait_ge(xT_hi_ok, t.n + 1)
                    b = t.slot(R)
                    nc.vector.tensor_tensor(xT_lo[:, b, :], ps_x[:, b, :], xT_hi[:, b, :], ALU.subtract
                                            ).then_inc(xT_lo_ok, 1)

                def bias_q(t):
                    b, q = t.slot(R), t.slot(X)
                    dve.wait_ge(qk_ps, t.n + 1)
                    if t.base >= X:
                        dve.wait_ge(q_ps, t.n + 1 - X)
                    nc.vector.tensor_tensor(qb[:, q, :], ps_qk[:, b, 0:QC], bias[:, 0:QC], ALU.add
                                            ).then_inc(q_in_ok, 1)

                def bias_k(t):
                    nc.vector.scalar_tensor_tensor(keep.k[:, t.n, :], ps_qk[:, t.slot(R), QC:2 * QC],
                                                   keep.unscale[:, 0:1], bias[:, QC:2 * QC], ALU.mult, ALU.add
                                                   ).then_inc(k_ok, 1)

                def row_max(t):
                    dve.wait_ge(q_in_ok, t.n + 1)
                    nc.vector.tensor_reduce(top[:, t.slot(R), :], heads(qb[:, t.slot(X), :]), AX.X, ALU.max
                                            ).then_inc(top_ok, 1)

                def column_max(t):
                    dve.wait_ge(k_ok, t.n + 1)
                    if t.base == 0 and t.j is None:
                        nc.vector.tensor_copy(keep.kmax[:], keep.k[:, 0, :]).then_inc(kmax_ok, 1)
                    else:
                        dve.wait_ge(kmax_ok, t.n)
                        r = t.rows()
                        nc.vector.tensor_tensor(keep.kmax[0:r], keep.kmax[0:r], keep.k[0:r, t.n, :], ALU.max
                                                ).then_inc(kmax_ok, 1)

                def less_max(t):
                    q = t.slot(X)
                    dve.wait_ge(top_ok, t.n + 1)
                    nc.vector.tensor_tensor(heads(qb[:, q, :]), heads(qb[:, q, :]),
                                            top[:, t.slot(R), :].unsqueeze(2).to_broadcast([P, HEADS, SLICE]),
                                            ALU.subtract).then_inc(less_ok, 1)

                def totals(t):
                    dve.wait_ge(exp_ok, t.n + 1)
                    if t.base >= R:
                        dve.wait_ge(q_ok, t.n + 1 - R)
                    nc.vector.tensor_reduce(total[:, t.slot(R), :], heads(qb[:, t.slot(X), :]), AX.X, ALU.add
                                            ).then_inc(total_ok, 1)

                def reciprocals(t):
                    dve.wait_ge(total_ok, t.n + 1)
                    nc.vector.reciprocal(total[:, t.slot(R), :], total[:, t.slot(R), :]).then_inc(recip_ok, 1)

                def low_q(t):
                    dve.wait_ge(qT_hi_ok, t.n + 1)
                    nc.vector.scalar_tensor_tensor(keep.qT_lo[:, t.n, :], ps_q[:, t.slot(R), 0:QC], ACT_SCALE,
                                                   keep.qT_hi[:, t.n, :], ALU.mult, ALU.subtract
                                                   ).then_inc(qT_lo_ok, 1)

                def self_loop(t):
                    dve.wait_ge(h_ok, t.n + 1)
                    nc.vector.scalar_tensor_tensor(xb[:, t.slot(X), :], hb[:, t.slot(R), :],
                                                   keep.dinv[:, bass.ds(t.n, 1)], xb[:, t.slot(X), :],
                                                   ALU.mult, ALU.add).then_inc(y_ok, 1)

                dve.wait_ge(bias_ps, 1)
                nc.vector.tensor_copy(bias[:, 0:QC], ps_q[:, 0, 0:QC]).then_inc(bias_ok, 1)
                nc.vector.tensor_scalar(bias[:, QC:2 * QC], ps_q[:, 0, QC:2 * QC], keep.unscale[:, 0:1], None,
                                        ALU.mult).then_inc(bias_ok, 1)
                dve.wait_ge(bias_ok, 2)
                over_tiles(dve, X, [(1, norm), (-2, totals), (-1, bias_q), (-2, reciprocals), (-1, bias_k),
                                    (-1, row_max), (2, statistics), (-1, less_max), (-1, column_max),
                                    (2, aggregate), (0, self_loop), (1, low_half), (-3, low_q)])

            @block.scalar
            def _(act):
                def high_half(t):
                    b = t.slot(R)
                    act.wait_ge(xT_ps, t.n + 1)
                    if t.base >= R:
                        act.wait_ge(qk_ps, t.n + 1 - R)
                    nc.scalar.activation(xT_hi[:, b, :], ps_x[:, b, :], ACT.Copy).then_inc(xT_hi_ok, 1)

                def exponent(t):
                    b = t.slot(X)
                    act.wait_ge(less_ok, t.n + 1)
                    nc.scalar.activation(qb[:, b, :], qb[:, b, :], ACT.Exp, scale=keep.unscale[:, 0:1]
                                         ).then_inc(exp_ok, 1)

                def high_q(t):
                    act.wait_ge(q_ps, t.n + 1)
                    nc.scalar.activation(keep.qT_hi[:, t.n, :], ps_q[:, t.slot(R), 0:QC], ACT.Copy,
                                         scale=ACT_SCALE).then_inc(qT_hi_ok, 1)

                def h_rows(t):
                    b = t.slot(R)
                    act.wait_ge(h_ps, t.n + 1)
                    if t.base >= R:
                        act.wait_ge(h_out[b], 16 * t.uses(R))
                        act.wait_ge(y_ok, t.n + 1 - R)
                    nc.scalar.activation(hb[:, b, :], ps_h[:, b, :], ACT.Identity,
                                         scale=keep.hcoef[:, bass.ds(t.n, 1)]).then_inc(h_ok, 1)

                over_tiles(act, X, [(0, h_rows), (-3, high_q), (1, high_half), (-1, exponent)])

            @block.tensor
            def _(pe):
                def parts(b):
                    return ((xT_hi, keep.w_hi), (xT_lo, keep.w_hi), (xT_hi, keep.w_lo))

                def h_product(t):
                    b = t.slot(R)
                    pe.wait_ge(xT_lo_ok, t.n + 1)
                    if t.base >= R:
                        pe.wait_ge(h_ok, t.n + 1 - R)
                    for k in range(KD):
                        for n, (xs, ws) in enumerate(parts(b)):
                            last = nc.tensor.matmul(ps_h[:, b, :], xs[:, b, k * P:(k + 1) * P], ws[:, k, D:2 * D],
                                                    start=(k == 0 and n == 0), stop=(k == KD - 1 and n == 2))
                    last.then_inc(h_ps, 1)

                def transposes(t):
                    b = t.slot(R)
                    pe.wait_ge(xn_ok, t.n + 1)
                    if t.base >= R:
                        pe.wait_ge(xT_lo_ok, t.n + 1 - R)
                    for k in range(KD):
                        last = nc.tensor.transpose(ps_x[:, b, k * P:(k + 1) * P], xn[:, b, k * P:(k + 1) * P],
                                                   keep.ident[:])
                    last.then_inc(xT_ps, 1)

                def qk_product(t):
                    b = t.slot(R)
                    if t.base >= R:
                        pe.wait_ge(q_in_ok, t.n + 1 - R)
                        pe.wait_ge(k_ok, t.n + 1 - R)
                    for k in range(KD):
                        for n, (xs, ws) in enumerate(parts(b)):
                            last = nc.tensor.matmul(ps_qk[:, b, :], xs[:, b, k * P:(k + 1) * P], ws[:, k, 0:D],
                                                    start=(k == 0 and n == 0), stop=(k == KD - 1 and n == 2))
                    last.then_inc(qk_ps, 1)

                def q_transposes(t):
                    b = t.slot(R)
                    pe.wait_ge(q_ok, t.n + 1)
                    if t.base == 0:
                        pe.wait_ge(bias_ok, 2)
                    if t.base >= R:
                        pe.wait_ge(qT_lo_ok, t.n + 1 - R)
                    for c in range(2):
                        last = nc.tensor.transpose(ps_q[:, b, c * P:(c + 1) * P], qb[:, t.slot(X), c * P:(c + 1) * P],
                                                   keep.ident[:])
                    last.then_inc(q_ps, 1)

                nc.tensor.matmul(ps_q[:, 0, :], keep.ones_b[:], keep.bias16[:], start=True, stop=True
                                 ).then_inc(bias_ps, 1)
                over_tiles(pe, X, [(0, h_product), (-3, q_transposes), (1, transposes), (0, qk_product)])


def second_pass(nc, keep, x, dst, h_table, y_table, dinv_table):
    with ExitStack() as st:
        m = Mem(nc, st, keep.lasting)
        X, R = 4, 2
        kmax_all = m.sb("b_kmax_all", [P, QC])
        xb = m.sb("b_x", [P, X, D])
        xs_hi = m.sb("b_x_hi", [P, X, D], F16)
        xs_lo = m.sb("b_x_lo", [P, R, D], F16)
        xn = m.sb("b_xn", [P, X, D])
        shift = m.sb("b_shift", [P, TILES])
        ones = m.sb("b_ones", [P, 1], F16)
        kb = m.sb("b_k", [P, X, QC])
        k_hi = m.sb("b_k_hi", [P, R, QC], F16)
        k_lo = m.sb("b_k_lo", [P, R, QC], F16)
        ln_act = m.sb("b_ln_act", [P, 1])
        dstrow = m.sb("b_dstrow", [P, P], I32)
        same = m.sb("b_same", [P, P])
        hsrc = m.sb("b_hsrc", [P, D])
        msg = m.sb("b_msg", [P, D])
        dst_dinv = m.sb("b_dst_dinv", [P, 1])
        index = m.sb("b_index", [P, 3], I32)
        ps_g = m.ps("bp_g", [P, 2, D])
        ps_e = m.ps("bp_e", [P, D])
        ps_s = m.ps("bp_s", [P, 2, D])

        x_in = m.sems("b_x_in", X)
        (kmax_in, dstrow_in, kmax_ready, ln_ok, xn_ok, less_ok, exp_ok, x_hi_ok, x_lo_ok, k_hi_ok, k_lo_ok, g_ps,
         shift_ok, ones_ok, same_ok, hsrc_in, dinv_in, sum_ps, msg_ok, added, g_ok, rk_ok, index_ok, target_ok) = (
            m.sem("b_" + n) for n in (
                "kmax_in", "dstrow_in", "kmax_ready", "ln_ok", "xn_ok", "less_ok", "exp_ok", "x_hi_ok", "x_lo_ok",
                "k_hi_ok", "k_lo_ok", "g_ps", "shift_ok", "ones_ok", "same_ok", "hsrc_in", "dinv_in", "sum_ps", "msg_ok",
                "added", "g_ok", "rk_ok", "index_ok", "target_ok"))

        def has_edges(t):
            return t.base % X == 0

        def etile(t):
            return t.uses(X)

        with nc.Block() as block:
            @block.sync
            def _(sp):
                def load(t):
                    if t.base >= X:
                        sp.wait_ge(xn_ok, t.n + 1 - X)
                    r = t.rows()
                    sp.dma_start(xb[0:r, t.slot(X), :], x[bass.ds(t.n * P, r), :]).then_inc(x_in[t.slot(X)], 16)

                def load_targets(t):
                    if not has_edges(t):
                        return
                    j = etile(t)
                    if t.base >= X:
                        sp.wait_ge(same_ok, j)
                    cols = ETAIL if t.j is None and t.base // X == ETILES - 1 else P
                    sp.dma_start(dstrow[:, 0:cols], dst.rearrange("(a e) -> a e", a=1)[:, bass.ds(j * P, cols)]
                                 .to_broadcast([P, cols])).then_inc(dstrow_in, 16)

                over_tiles(sp, X, [(2, load_targets), (5, load)])

            @block.gpsimd
            def _(pool):
                nc.gpsimd.memset(ones[:], 1.0).then_inc(ones_ok, 1)
                nc.gpsimd.partition_all_reduce(kmax_all[:], keep.kmax[:], P, ROP.max).then_inc(kmax_ready, 1)

                def gather(t):
                    if not has_edges(t):
                        return
                    j = etile(t)
                    if t.base >= X:
                        pool.wait_ge(sum_ps, j)
                        pool.wait_ge(msg_ok, j)
                    for n, table in enumerate((keep.src, keep.dst)):
                        nc.gpsimd.tensor_copy(index[:, n:n + 1], table[:, bass.ds(j, 1)]).then_inc(index_ok, 1)
                    pool.wait_ge(index_ok, j * 2 + 2)
                    stand_alone(pool)
                    pool.indirect_dma_start(hsrc[:], None, h_table, bass.IndirectOffsetOnAxis(
                        index[:, 0:1], 0)).then_inc(hsrc_in, 16)
                    stand_alone(pool)
                    pool.indirect_dma_start(dst_dinv[:], None, dinv_table, bass.IndirectOffsetOnAxis(
                        index[:, 1:2], 0)).then_inc(dinv_in, 16)

                def scatter(t):
                    if not has_edges(t):
                        return
                    j = etile(t)
                    pool.wait_ge(msg_ok, j + 1)
                    if t.base >= X:
                        pool.wait_ge(added, 16 * j)
                    nc.gpsimd.tensor_copy(index[:, 2:3], keep.target[:, bass.ds(j, 1)]).then_inc(target_ok, 1)
                    pool.wait_ge(target_ok, j + 1)
                    stand_alone(pool)
                    pool.indirect_dma_start(y_table, bass.IndirectOffsetOnAxis(index[:, 2:3], 0), msg[:], None,
                                            compute_op=ALU.add).then_inc(added, 16)

                over_tiles(pool, X, [(2, gather), (-2, scatter)])
                pool.wait_ge(added, 16 * ETILES)

            @block.vector
            def _(dve):
                nc.vector.memset(ln_act[:], 8.317766166719343).then_inc(ln_ok, 1)
                nc.vector.scalar_tensor_tensor(shift[:], keep.mean[:], -1.0, keep.rstd[:], ALU.mult, ALU.mult
                                               ).then_inc(shift_ok, 1)
                dve.wait_ge(kmax_ready, 1)

                def less_max(t):
                    if t.base >= X:
                        dve.wait_ge(k_lo_ok, t.n + 1 - X)
                    r = t.rows()
                    nc.vector.tensor_tensor(kb[0:r, t.slot(X), :], keep.k[0:r, t.n, :], kmax_all[0:r], ALU.subtract
                                            ).then_inc(less_ok, 1)

                def low_x(t):
                    b = t.slot(R)
                    dve.wait_ge(x_hi_ok, t.n + 1)
                    r = t.rows()
                    nc.vector.tensor_tensor(xs_lo[0:r, b, :], xn[0:r, t.slot(X), :], xs_hi[0:r, t.slot(X), :], ALU.subtract
                                            ).then_inc(x_lo_ok, 1)

                def high_k(t):
                    b = t.slot(R)
                    dve.wait_ge(exp_ok, t.n + 1)
                    if t.base >= R:
                        dve.wait_ge(g_ps, t.n + 1 - R)
                    r = t.rows()
                    nc.vector.tensor_copy(k_hi[0:r, b, :], kb[0:r, t.slot(X), :]).then_inc(k_hi_ok, 1)

                def low_k(t):
                    b = t.slot(R)
                    dve.wait_ge(k_hi_ok, t.n + 1)
                    r = t.rows()
                    nc.vector.tensor_tensor(k_lo[0:r, b, :], kb[0:r, t.slot(X), :], k_hi[0:r, b, :], ALU.subtract
                                            ).then_inc(k_lo_ok, 1)

                def same_target(t):
                    if not has_edges(t):
                        return
                    j = etile(t)
                    dve.wait_ge(dstrow_in, 16 * (j + 1))
                    if t.base >= X:
                        dve.wait_ge(sum_ps, j)
                    nc.vector.tensor_scalar(same[:], dstrow[:], keep.dstf[:, bass.ds(j, 1)],
                                            None, ALU.is_equal).then_inc(same_ok, 1)

                over_tiles(dve, X, [(0, high_k), (0, low_x), (0, low_k), (2, less_max), (1, same_target)])
                dve.wait_ge(g_ps, TILES)
                nc.vector.tensor_scalar(keep.rk[:], ps_s[:, :, 0], ACT_SCALE, None, ALU.mult).then_inc(rk_ok, 1)
                dve.wait_ge(rk_ok, 1)
                nc.vector.reciprocal(keep.rk[:], keep.rk[:]).then_inc(rk_ok, 1)
                dve.wait_ge(rk_ok, 2)
                for c in range(2):
                    nc.vector.tensor_scalar(keep.g[:, c, :], ps_g[:, c, :], keep.rk[:, c:c + 1], None, ALU.mult
                                            ).then_inc(g_ok, 1)
                dve.wait_ge(g_ok, 2)

            @block.scalar
            def _(act):
                act.wait_ge(ln_ok, 1)
                act.wait_ge(shift_ok, 1)

                def norm(t):
                    q, r = t.slot(X), t.rows()
                    act.wait_ge(x_in[q], 16 * (t.uses(X) + 1))
                    if t.base >= X:
                        act.wait_ge(x_lo_ok, t.n + 1 - X)
                    nc.scalar.activation(xn[0:r, q, :], xb[0:r, q, :], ACT.Identity,
                                         bias=shift[0:r, bass.ds(t.n, 1)], scale=keep.rstd[0:r, bass.ds(t.n, 1)]
                                         ).then_inc(xn_ok, 1)

                def exponent(t):
                    b = t.slot(X)
                    act.wait_ge(less_ok, t.n + 1)
                    r = t.rows()
                    nc.scalar.activation(kb[0:r, b, :], kb[0:r, b, :], ACT.Exp, bias=ln_act[0:r]).then_inc(exp_ok, 1)

                def high_x(t):
                    q = t.slot(X)
                    act.wait_ge(xn_ok, t.n + 1)
                    if t.base >= X:
                        act.wait_ge(g_ps, t.n + 1 - X)
                    r = t.rows()
                    nc.scalar.activation(xs_hi[0:r, q, :], xn[0:r, q, :], ACT.Copy).then_inc(x_hi_ok, 1)

                def message(t):
                    if not has_edges(t):
                        return
                    j = etile(t)
                    act.wait_ge(sum_ps, j + 1)
                    act.wait_ge(dinv_in, 16 * (j + 1))
                    if t.base >= X:
                        act.wait_ge(added, 16 * j)
                    nc.scalar.activation(msg[:], ps_e[:], ACT.Identity, scale=dst_dinv[:]).then_inc(msg_ok, 1)

                over_tiles(act, X, [(2, norm), (1, high_x), (1, exponent), (-1, message)])

            @block.tensor
            def _(pe):
                def products(t):
                    b, r = t.slot(R), t.rows()
                    pe.wait_ge(x_lo_ok, t.n + 1)
                    pe.wait_ge(k_lo_ok, t.n + 1)
                    hi, lo = xs_hi[0:r, t.slot(X), :], xs_lo[0:r, b, :]
                    for c in range(2):
                        cols = slice(c * P, (c + 1) * P)
                        for n, (ks, xs) in enumerate(((k_hi, hi), (k_hi, lo), (k_lo, hi))):
                            last = nc.tensor.matmul(ps_g[:, c, :], ks[0:r, b, cols], xs,
                                                    start=(t.j is None and t.base == 0 and n == 0),
                                                    stop=(t.j is None and t.base == TILES - 1 and n == 2))
                        for n, ks in enumerate((k_hi, k_lo)):
                            last = nc.tensor.matmul(ps_s[:, c, 0:1], ks[0:r, b, cols], ones[0:r],
                                                    start=(t.j is None and t.base == 0 and n == 0),
                                                    stop=(t.j is None and t.base == TILES - 1 and n == 1))
                    last.then_inc(g_ps, 1)

                def sum_edges(t):
                    if not has_edges(t):
                        return
                    j = etile(t)
                    pe.wait_ge(same_ok, j + 1)
                    pe.wait_ge(hsrc_in, 16 * (j + 1))
                    if t.base >= X:
                        pe.wait_ge(msg_ok, j)
                    nc.tensor.matmul(ps_e[:], same[:], hsrc[:], start=True, stop=True).then_inc(sum_ps, 1)

                pe.wait_ge(ones_ok, 1)
                over_tiles(pe, X, [(-1, products), (0, sum_edges)])



def fold(nc, keep, f, W_in, b_in, Wv, W_out, b_out, gnn_b, Wg, W1, b1, W2, b2, ln_g, ln_b, out_g, out_b):
    with ExitStack() as st:
        m = Mem(nc, st, st)
        win = m.sb("f_win", [P, KD, D])
        wout = m.sb("f_wout", [P, PAIRS, D])
        wv = m.sb("f_wv", [P, 2, HEAD])
        wvT = m.sb("f_wvT", [P, P])
        wvo = m.sb("f_wvo", [P, PAIRS, D])
        bcol = m.sb("f_bcol", [P, PAIRS])
        gT = m.sb("f_gT", [P, KD, QC])
        u = m.sb("f_u", [P, PAIRS, P])
        mm = m.sb("f_m", [P, 2, D])
        row = m.sb("f_row", [SLICE, 2, D])
        w1 = m.sb("f_w1", [P, KD, ZC])
        w1g = m.sb("f_w1g", [P, KD, ZC])
        w2 = m.sb("f_w2", [P, 2, D])
        gcol = m.sb("f_gcol", [P, KD])
        lbcol = m.sb("f_lbcol", [P, KD])
        lbB = m.sb("f_lbB", [P, KD, P])
        b2t = m.sb("f_b2t", [EXPERTS, D])
        b2_hi = m.sb("f_b2_hi", [EXPERTS, D], F16)
        b2_lo = m.sb("f_b2_lo", [EXPERTS, D], F16)
        peak = m.sb("f_peak", [P, 5])
        peak_all = m.sb("f_peak_all", [P, 5])
        bound = m.sb("f_bound", [P, 4])
        pow2 = m.sb("f_pow2", [P, 4])
        scale = m.sb("f_scale", [P, 4])
        b2scale = m.sb("f_b2scale", [P, 1])
        iota_i = m.sb("f_iota_i", [P, EXPERTS], I32)
        ps_t = m.ps("fp_t", [P, 2, D])
        ps_u = m.ps("fp_u", [P, D])
        ps_m = m.ps("fp_m", [P, 2, D])
        ps_v = m.ps("fp_v", [P, D])
        ps_z = m.ps("fp_z", [P, D])
        ps_w = m.ps("fp_w", [P, D])
        names = ("win_in", "wout_in", "wv_in", "col_in", "row_in", "w1_in", "w2_in", "b2_in", "b1_in", "out_in",
                 "b2_copied", "filled", "iota_ok", "wv_filled", "wvT_ps", "wvT_ok", "wvo_ps", "wvo_ok", "gT_ps", "gT_ok",
                 "u_ps", "u_ok", "m_ps", "m_ok", "lbB_ok", "z_ps", "peaks_ok", "peak_all_ok", "b2_ok", "own",
                 "ident_ok")
        sem = {n: m.sem("f_" + n) for n in names}

        with nc.Block() as block:
            @block.sync
            def _(sp):
                sp.dma_start(win[:], W_in.rearrange("(k p) n -> p k n", p=P)).then_inc(sem["win_in"], 16)
                sp.dma_start(wout[:], W_out.rearrange("(j p) n -> p j n", p=P)).then_inc(sem["wout_in"], 16)
                sp.wait_ge(sem["wv_filled"], 1)
                for h in range(2):
                    sp.dma_start(wv[h * HEAD:(h + 1) * HEAD, h, :], Wv).then_inc(sem["wv_in"], 16)
                for k in range(KD):
                    sp.dma_start(w1[:, k, 0:HC].rearrange("p (e j) -> p e j", e=EXPERTS),
                                 W1[:, k * P:(k + 1) * P, :].rearrange("e p j -> p e j")).then_inc(sem["w1_in"], 16)
                sp.dma_start(w1[:, :, HC:ZC], Wg.rearrange("(k p) e -> p k e", p=P)).then_inc(sem["w1_in"], 16)
                sp.wait_ge(sem["b2_ok"], 2)
                for n, part in enumerate((b2_hi, b2_hi, b2_lo)):
                    sp.dma_start(f.b2s[n * EXPERTS:(n + 1) * EXPERTS, :], part[:]).then_inc(sem["b2_copied"], 16)
                sp.wait_ge(sem["b2_copied"], 48)

            @block.scalar
            def _(act):
                act.dma_start(bcol[:], b_in.rearrange("(j p) -> p j", p=P),
                              allow_slow_non_contiguous=True).then_inc(sem["col_in"], 16)
                act.dma_start(gcol[:], ln_g.rearrange("(k p) -> p k", p=P),
                              allow_slow_non_contiguous=True).then_inc(sem["col_in"], 16)
                act.dma_start(lbcol[:], ln_b.rearrange("(k p) -> p k", p=P),
                              allow_slow_non_contiguous=True).then_inc(sem["col_in"], 16)
                for n, v in enumerate((gnn_b, b_out)):
                    act.dma_start(row[:, n, :], v.rearrange("(a n) -> a n", a=1).to_broadcast([SLICE, D])
                                  ).then_inc(sem["row_in"], 16)
                act.dma_start(w2[:], W2.rearrange("e j n -> (e j) n").rearrange("(c p) n -> p c n", p=P)
                              ).then_inc(sem["w2_in"], 16)
                act.dma_start(b2t[:], b2).then_inc(sem["b2_in"], 16)
                act.wait_ge(sem["filled"], 1)
                act.dma_start(f.zbias[:, 0:HC], b1.rearrange("e j -> (e j)").rearrange("(a n) -> a n", a=1)
                              .to_broadcast([P, HC])).then_inc(sem["b1_in"], 16)
                for v, tile in ((out_g, f.gain), (out_b, f.offset)):
                    act.dma_start(tile[:], v.rearrange("(a n) -> a n", a=1).to_broadcast([P, D])
                                  ).then_inc(sem["out_in"], 16)
                act.wait_ge(sem["wvT_ps"], 1)
                nc.scalar.activation(wvT[:], ps_v[:, 0:P], ACT.Copy).then_inc(sem["wvT_ok"], 1)
                for j in range(PAIRS):
                    act.wait_ge(sem["wvo_ps"], j + 1)
                    nc.scalar.activation(wvo[:, j, :], ps_w[:], ACT.Copy).then_inc(sem["wvo_ok"], 1)
                for c in range(2):
                    for k in range(0, KD, 2):
                        act.wait_ge(sem["gT_ps"], c * 2 + k // 2 + 1)
                        for kk in (k, k + 1):
                            nc.scalar.activation(gT[:, kk, c * P:(c + 1) * P],
                                                 ps_t[:, k // 2, (kk - k) * P:(kk - k + 1) * P],
                                                 ACT.Copy).then_inc(sem["gT_ok"], 1)
                act.wait_ge(sem["out_in"], 32)

            @block.gpsimd
            def _(pool):
                nc.gpsimd.memset(wv[:], 0.0).then_inc(sem["wv_filled"], 1)
                nc.gpsimd.memset(f.zbias[:], 0.0).then_inc(sem["filled"], 1)
                nc.gpsimd.iota(iota_i[:], [[1, EXPERTS]], base=0, channel_multiplier=0).then_inc(sem["iota_ok"], 1)
                nc.gpsimd.memset(f.ident16[:], 0.0).then_inc(sem["ident_ok"], 1)
                pool.wait_ge(sem["ident_ok"], 1)
                nc.gpsimd.affine_select(out=f.ident16[:], in_=f.ident16[:], compare_op=ALU.not_equal, fill=1.0,
                                        base=0, pattern=[[-1, P]], channel_multiplier=1
                                        ).then_inc(sem["ident_ok"], 1)
                pool.wait_ge(sem["peaks_ok"], 6)
                nc.gpsimd.partition_all_reduce(peak_all[:], peak[:], P, ROP.max).then_inc(sem["peak_all_ok"], 1)

            @block.tensor
            def _(pe):
                pe.wait_ge(sem["wv_in"], 32)
                nc.tensor.transpose(ps_v[:, 0:P], wv[:].rearrange("p h c -> p (h c)"), keep.ident[:]
                                    ).then_inc(sem["wvT_ps"], 1)
                pe.wait_ge(sem["wvT_ok"], 1)
                pe.wait_ge(sem["wout_in"], 16)
                for j in range(PAIRS):
                    if j:
                        pe.wait_ge(sem["wvo_ok"], j)
                    nc.tensor.matmul(ps_w[:], wvT[:], wout[:, j, :], start=True, stop=True
                                     ).then_inc(sem["wvo_ps"], 1)
                for c in range(2):
                    for k in range(0, KD, 2):
                        if c:
                            pe.wait_ge(sem["gT_ok"], k + 2)
                        for kk in (k, k + 1):
                            last = nc.tensor.transpose(ps_t[:, k // 2, (kk - k) * P:(kk - k + 1) * P],
                                                       keep.g[:, c, kk * P:(kk + 1) * P], keep.ident[:])
                        last.then_inc(sem["gT_ps"], 1)
                pe.wait_ge(sem["lbB_ok"], 1)
                pe.wait_ge(sem["w1_in"], 16 * (KD + 1))
                for k in range(KD):
                    last = nc.tensor.matmul(ps_z[:, 0:ZC], lbB[:, k, :], w1[:, k, :], start=(k == 0),
                                            stop=(k == KD - 1))
                last.then_inc(sem["z_ps"], 1)
                pe.wait_ge(sem["gT_ok"], 2 * KD)
                pe.wait_ge(sem["win_in"], 16)
                for j in range(PAIRS):
                    for k in range(KD):
                        last = nc.tensor.matmul(ps_u[:, j * 2 * SLICE:(j + 1) * 2 * SLICE],
                                                win[:, k, j * P:(j + 1) * P],
                                                gT[:, k, j * 2 * SLICE:(j + 1) * 2 * SLICE],
                                                start=(k == 0), stop=(k == KD - 1))
                last.then_inc(sem["u_ps"], 1)
                pe.wait_ge(sem["u_ok"], 2 * PAIRS + 1)
                pe.wait_ge(sem["wvo_ok"], PAIRS)
                for c in range(2):
                    for j in (2 * c, 2 * c + 1):
                        last = nc.tensor.matmul(ps_m[:, c, :], u[:, j, :], wvo[:, j, :], start=(j % 2 == 0),
                                                stop=(j % 2 == 1))
                last.then_inc(sem["m_ps"], 1)

            @block.vector
            def _(dve):
                own = Chain(dve, sem["own"])
                nc.vector.memset(u[:], 0.0).then_inc(sem["u_ok"], 1)
                own.do(nc.vector.memset(f.mhalf2[:], -0.5))
                own.do(nc.vector.memset(peak[:], 0.0))
                dve.wait_ge(sem["col_in"], 48)
                nc.vector.tensor_copy(lbB[:], lbcol[:].unsqueeze(2).to_broadcast([P, KD, P])
                                      ).then_inc(sem["lbB_ok"], 1)
                dve.wait_ge(sem["w1_in"], 16 * (KD + 1))
                for k in range(KD):
                    own.do(nc.vector.tensor_scalar(w1g[:, k, :], w1[:, k, :], gcol[:, k:k + 1], None, ALU.mult))
                dve.wait_ge(sem["iota_ok"], 1)
                own.do(nc.vector.tensor_copy(f.iota[:], iota_i[:]))
                dve.wait_ge(sem["w2_in"], 16)
                dve.wait_ge(sem["b2_in"], 16)
                own.settle()
                nc.vector.tensor_reduce(peak[:, 2:3], w2[:], AX.XY, ALU.max, apply_absolute_value=True
                                        ).then_inc(sem["peaks_ok"], 1)
                nc.vector.tensor_reduce(peak[0:EXPERTS, 3:4], b2t[:], AX.X, ALU.max, apply_absolute_value=True
                                        ).then_inc(sem["peaks_ok"], 1)
                nc.vector.tensor_reduce(peak[:, 1:2], w1g[:], AX.XY, ALU.max, apply_absolute_value=True
                                        ).then_inc(sem["peaks_ok"], 1)
                dve.wait_ge(sem["z_ps"], 1)
                dve.wait_ge(sem["b1_in"], 16)
                own.do(nc.vector.tensor_tensor(f.zbias[:], ps_z[:, 0:ZC], f.zbias[:], ALU.add))
                own.settle()
                nc.vector.tensor_reduce(peak[:, 4:5], f.zbias[:], AX.X, ALU.max, apply_absolute_value=True
                                        ).then_inc(sem["peaks_ok"], 1)
                dve.wait_ge(sem["u_ps"], 1)
                dve.wait_ge(sem["u_ok"], 1)
                for j in range(PAIRS):
                    for h in range(2):
                        rows = slice(h * HEAD, (h + 1) * HEAD)
                        at = (2 * (j % 2) + h) * SLICE
                        src_at = (2 * j + h) * SLICE
                        nc.vector.tensor_scalar(u[rows, j, at:at + SLICE], ps_u[rows, src_at:src_at + SLICE],
                                                bcol[rows, j:j + 1], None, ALU.add).then_inc(sem["u_ok"], 1)
                dve.wait_ge(sem["row_in"], 32)
                own.do(nc.vector.tensor_tensor(row[:, 0, :], row[:, 0, :], row[:, 1, :], ALU.add))
                dve.wait_ge(sem["m_ps"], 1)
                own.do(nc.vector.tensor_copy(mm[:], ps_m[:]))
                own.settle()
                own.do(nc.vector.tensor_tensor(mm[0:SLICE, 0, :], mm[0:SLICE, 0, :], row[:, 0, :], ALU.add))
                own.settle()
                nc.vector.tensor_reduce(peak[:, 0:1], mm[:], AX.XY, ALU.max, apply_absolute_value=True
                                        ).then_inc(sem["peaks_ok"], 1)
                dve.wait_ge(sem["peaks_ok"], 5)
                nc.vector.tensor_scalar(peak[:], peak[:], 1e-25, None, ALU.max).then_inc(sem["peaks_ok"], 1)
                dve.wait_ge(sem["peak_all_ok"], 1)
                own.do(nc.vector.tensor_copy(bound[:, 0:2], peak_all[:, 0:2]))
                own.do(nc.vector.scalar_tensor_tensor(bound[:, 2:3], peak_all[:, 1:2], float(D), peak_all[:, 4:5],
                                                      ALU.mult, ALU.add))
                own.settle()
                own.do(power_of_two(nc, pow2[:, 0:3], bound[:, 0:3]))
                own.settle()
                own.do(nc.vector.reciprocal(scale[:, 0:3], pow2[:, 0:3]))
                own.settle()
                own.do(nc.vector.tensor_scalar(scale[:, 0:3], scale[:, 0:3], W_TOP, None, ALU.mult))
                own.settle()
                own.do(nc.vector.tensor_scalar(bound[:, 3:4], peak_all[:, 3:4], scale[:, 2:3], 1.0 / ACT_SCALE,
                                               ALU.mult, ALU.mult))
                own.settle()
                own.do(nc.vector.tensor_tensor(bound[:, 3:4], bound[:, 3:4], peak_all[:, 2:3], ALU.max))
                own.settle()
                own.do(power_of_two(nc, pow2[:, 3:4], bound[:, 3:4]))
                own.settle()
                own.do(nc.vector.reciprocal(scale[:, 3:4], pow2[:, 3:4]))
                own.settle()
                own.do(nc.vector.tensor_scalar(scale[:, 3:4], scale[:, 3:4], W_TOP, None, ALU.mult))
                own.settle()
                own.do(nc.vector.tensor_scalar(b2scale[:], scale[:, 3:4], scale[:, 2:3], 1.0 / ACT_SCALE,
                                               ALU.mult, ALU.mult))
                own.do(nc.vector.tensor_scalar(f.hscale[:], scale[:, 2:3], 1.0 / ACT_SCALE, None, ALU.mult))
                own.do(nc.vector.tensor_scalar(f.m_unscale[:], pow2[:, 0:1], 1.0 / (W_TOP * ACT_SCALE), None,
                                               ALU.mult))
                own.do(nc.vector.tensor_scalar(f.z_unscale[:], pow2[:, 1:2], 1.0 / (W_TOP * ACT_SCALE), None,
                                               ALU.mult))
                own.do(nc.vector.tensor_scalar(f.o_unscale[:], pow2[:, 2:3], pow2[:, 3:4],
                                               ACT_SCALE / (W_TOP * W_TOP), ALU.mult, ALU.mult))
                own.settle()
                split(own, nc, [(f.m_hi[:, c, :], f.m_lo[:, c, :], mm[:, c, :], scale[:, 0:1]) for c in range(2)]
                      + [(f.w1_hi[:, k, :], f.w1_lo[:, k, :], w1g[:, k, :], scale[:, 1:2]) for k in range(KD)]
                      + [(f.w2_hi[:, c, :], f.w2_lo[:, c, :], w2[:, c, :], scale[:, 3:4]) for c in range(2)])
                own.settle()
                nc.vector.tensor_scalar(b2_hi[:], b2t[:], b2scale[0:EXPERTS], None, ALU.mult
                                        ).then_inc(sem["b2_ok"], 1)
                dve.wait_ge(sem["b2_ok"], 1)
                nc.vector.scalar_tensor_tensor(b2_lo[:], b2t[:], b2scale[0:EXPERTS], b2_hi[:], ALU.mult,
                                               ALU.subtract).then_inc(sem["b2_ok"], 1)
                dve.wait_ge(sem["b2_ok"], 2)
        m.clear_sems()


def third_pass(nc, keep, f, y_table, out):
    with ExitStack() as st:
        m = Mem(nc, st, keep.lasting)
        X, Y, R = 8, 4, 2
        yb = m.sb("c_y", [P, Y, D])
        x1 = m.sb("c_x1", [P, X, D])
        x2 = m.sb("c_x2", [P, X, D])
        ob = m.sb("c_o", [P, R, D])
        nb = m.sb("c_n", [P, R, D])
        square = m.sb("c_square", [P, 2, D])
        xT_hi = m.sb("c_xT_hi", [P, R, D], F16)
        xT_lo = m.sb("c_xT_lo", [P, R, D], F16)
        zb = m.sb("c_z", [P, R, ZC])
        hb = m.sb("c_h", [P, R, HC])
        hT_hi = m.sb("c_hT_hi", [P, R, HC], F16)
        hT_lo = m.sb("c_hT_lo", [P, R, HC], F16)
        conf3 = m.sb("c_conf3", [P, R, 3, EXPERTS], F16)
        confT = m.sb("c_confT", [3 * EXPERTS, R, P], F16)
        sum1 = m.sb("c_sum1", [P, Y, 1])
        sum2 = m.sb("c_sum2", [P, Y, 1])
        ssq1 = m.sb("c_ssq1", [P, R, 1])
        ssq2 = m.sb("c_ssq2", [P, R, 1])
        var1 = m.sb("c_var1", [P, R, 2])
        var2 = m.sb("c_var2", [P, R, 1])
        rs1 = m.sb("c_rs1", [P, R, 2])
        rs2 = m.sb("c_rs2", [P, R, 1])
        shift1 = m.sb("c_shift1", [P, R, 1])
        shift2 = m.sb("c_shift2", [P, R, 1])
        ratio = m.sb("c_ratio", [P, R, 1])
        rz = m.sb("c_rz", [P, Y, 1])
        best = m.sb("c_best", [P, R, 8])
        best_at = m.sb("c_best_at", [P, R, 8], U32)
        gate = m.sb("c_gate", [P, R, 8])
        conf = m.sb("c_conf", [P, R, 3, EXPERTS])
        hconf = m.sb("c_hconf", [P, R, EXPERTS])
        ps_a = m.ps("cp_a", [P, R, D])
        ps_x = m.ps("cp_x", [P, D])
        ps_z = m.ps("cp_z", [P, D])
        ps_h = m.ps("cp_h", [P, D])
        ps_c = m.ps("cp_c", [3 * EXPERTS, 2 * D], F16)
        ps_o = m.ps("cp_o", [P, R, D])

        y_in = m.sems("c_y_in", Y)
        out_done = m.sems("c_out", R)
        names = ("a_ps", "x1_ok", "ssq1_ok", "var1_ok", "rs1_ok", "shift1_ok", "ratio_ok", "rz_ok",
                 "x2_ok", "xT_ps", "xT_hi_ok", "xT_lo_ok", "z_ps", "z_ok", "best_ok", "best_at_ok", "gelu_ok",
                 "gap_ok", "tanh_ok", "share_ok", "picked_ok", "conf_ok", "hconf_ok", "conf_hi_ok", "conf3_ok",
                 "h_ok", "hT_ps", "hT_hi_ok", "hT_lo_ok", "confT_ok", "o_ps", "t_ok", "ssq2_ok",
                 "var2_ok", "rs2_ok", "shift2_ok", "n_ok", "gained_ok", "offset_ok", "o_ok")
        sem = {n: m.sem("c_" + n) for n in names}

        with nc.Block() as block:
            @block.sync
            def _(sp):
                def load(t):
                    if t.base >= Y:
                        sp.wait_ge(sem["x1_ok"], t.n + 1 - Y)
                    r = t.rows()
                    sp.dma_start(yb[0:r, t.slot(Y), :], y_table[bass.ds(t.n * P, r), :]
                                 ).then_inc(y_in[t.slot(Y)], 16)

                def store(t):
                    r = t.rows()
                    sp.wait_ge(sem["o_ok"], t.n + 1)
                    sp.dma_start(out[bass.ds(t.n * P, r), :], ob[0:r, t.slot(R), :]
                                 ).then_inc(out_done[t.slot(R)], 16)

                over_tiles(sp, X, [(6, load), (-5, store)])
                for q in range(R):
                    sp.wait_ge(out_done[q], 16 * len(range(q, TILES, R)))

            @block.tensor
            def _(pe):
                def attention(t):
                    b = t.slot(R)
                    if t.base >= R:
                        pe.wait_ge(sem["x1_ok"], t.n + 1 - R)
                    for c in range(2):
                        for n, (qs, ms) in enumerate(((keep.qT_hi, f.m_hi), (keep.qT_lo, f.m_hi),
                                                      (keep.qT_hi, f.m_lo))):
                            last = nc.tensor.matmul(ps_a[:, b, :], qs[:, t.n, c * P:(c + 1) * P], ms[:, c, :],
                                                    start=(c == 0 and n == 0), stop=(c == 1 and n == 2))
                    last.then_inc(sem["a_ps"], 1)

                def x2_transposes(t):
                    pe.wait_ge(sem["x2_ok"], t.n + 1)
                    if t.base >= 1:
                        pe.wait_ge(sem["xT_lo_ok"], t.n)
                    for k in range(KD):
                        last = nc.tensor.transpose(ps_x[:, k * P:(k + 1) * P],
                                                   x2[:, t.slot(X), k * P:(k + 1) * P], keep.ident[:])
                    last.then_inc(sem["xT_ps"], 1)

                def first_layer(t):
                    b = t.slot(R)
                    pe.wait_ge(sem["xT_lo_ok"], t.n + 1)
                    if t.base >= 1:
                        pe.wait_ge(sem["z_ok"], t.n)
                    for k in range(KD):
                        for n, (xs, ws) in enumerate(((xT_hi, f.w1_hi), (xT_lo, f.w1_hi), (xT_hi, f.w1_lo))):
                            last = nc.tensor.matmul(ps_z[:, 0:ZC], xs[:, b, k * P:(k + 1) * P], ws[:, k, :],
                                                    start=(k == 0 and n == 0), stop=(k == KD - 1 and n == 2))
                    last.then_inc(sem["z_ps"], 1)

                def h_transposes(t):
                    b = t.slot(R)
                    pe.wait_ge(sem["conf3_ok"], t.n + 1)
                    if t.base >= 1:
                        pe.wait_ge(sem["hT_lo_ok"], t.n)
                        pe.wait_ge(sem["confT_ok"], t.n)
                    nc.tensor.transpose(ps_c[:, 0:P], conf3[:, b].rearrange("p a e -> p (a e)"), f.ident16[:])
                    pe.wait_ge(sem["h_ok"], t.n + 1)
                    for c in range(2):
                        last = nc.tensor.transpose(ps_h[:, c * P:(c + 1) * P], hb[:, b, c * P:(c + 1) * P],
                                                   keep.ident[:])
                    last.then_inc(sem["hT_ps"], 1)

                def second_layer(t):
                    b = t.slot(R)
                    pe.wait_ge(sem["hT_lo_ok"], t.n + 1)
                    pe.wait_ge(sem["confT_ok"], t.n + 1)
                    if t.base >= R:
                        pe.wait_ge(sem["t_ok"], t.n + 1 - R)
                    nc.tensor.matmul(ps_o[:, b, :], confT[:, b, :], f.b2s[:], start=True, stop=False)
                    for c in range(2):
                        for n, (hs, ws) in enumerate(((hT_hi, f.w2_hi), (hT_lo, f.w2_hi), (hT_hi, f.w2_lo))):
                            last = nc.tensor.matmul(ps_o[:, b, :], hs[:, b, c * P:(c + 1) * P], ws[:, c, :],
                                                    start=False, stop=(c == 1 and n == 2))
                    last.then_inc(sem["o_ps"], 1)

                over_tiles(pe, X, [(-2, h_transposes), (0, first_layer), (1, x2_transposes), (4, attention),
                                   (-2, second_layer)])

            @block.vector
            def _(dve):
                def add_attention(t):
                    q, b = t.slot(X), t.slot(R)
                    dve.wait_ge(sem["a_ps"], t.n + 1)
                    dve.wait_ge(y_in[t.slot(Y)], 16 * (t.uses(Y) + 1))
                    if t.base >= X:
                        dve.wait_ge(sem["o_ok"], t.n + 1 - X)
                    if t.base >= Y:
                        dve.wait_ge(sem["shift1_ok"], t.n + 1 - Y)
                    nc.vector.scalar_tensor_tensor(x1[:, q, :], ps_a[:, b, :], f.m_unscale[:], yb[:, t.slot(Y), :],
                                                   ALU.mult, ALU.add, accum_out=sum1[:, t.slot(Y)]
                                                   ).then_inc(sem["x1_ok"], 1)

                def low_x2(t):
                    b = t.slot(R)
                    dve.wait_ge(sem["xT_hi_ok"], t.n + 1)
                    nc.vector.tensor_tensor(xT_lo[:, b, :], ps_x[:], xT_hi[:, b, :], ALU.subtract
                                            ).then_inc(sem["xT_lo_ok"], 1)

                def hidden(t):
                    b = t.slot(R)
                    dve.wait_ge(sem["z_ps"], t.n + 1)
                    dve.wait_ge(sem["rz_ok"], t.n + 1)
                    if t.base >= R:
                        dve.wait_ge(sem["gelu_ok"], t.n + 1 - R)
                    nc.vector.scalar_tensor_tensor(zb[:, b, :], ps_z[:, 0:ZC], rz[:, t.slot(Y)], f.zbias[:], ALU.mult,
                                                   ALU.add).then_inc(sem["z_ok"], 1)

                def best_two(t):
                    b = t.slot(R)
                    dve.wait_ge(sem["z_ok"], t.n + 1)
                    stand_alone(dve)
                    nc.vector.max(best[:, b, :], zb[:, b, HC:ZC]).then_inc(sem["best_ok"], 1)

                def best_places(t):
                    b = t.slot(R)
                    dve.wait_ge(sem["best_ok"], t.n + 1)
                    stand_alone(dve)
                    nc.vector.max_index(best_at[:, b, :], best[:, b, :], zb[:, b, HC:ZC]
                                        ).then_inc(sem["best_at_ok"], 1)

                def pick(t):
                    b = t.slot(R)
                    dve.wait_ge(sem["share_ok"], t.n * 3 + 3)
                    for n in range(2):
                        nc.vector.tensor_scalar(conf[:, b, n, :], f.iota[:], gate[:, b, n:n + 1],
                                                gate[:, b, 4 + n:5 + n], ALU.is_equal, ALU.mult
                                                ).then_inc(sem["picked_ok"], 1)

                def add_picked(t):
                    b = t.slot(R)
                    dve.wait_ge(sem["picked_ok"], t.n * 2 + 2)
                    nc.vector.tensor_tensor(conf[:, b, 2, :], conf[:, b, 0, :], conf[:, b, 1, :], ALU.add
                                            ).then_inc(sem["conf_ok"], 1)

                def low_confidence(t):
                    b = t.slot(R)
                    dve.wait_ge(sem["conf_hi_ok"], t.n + 1)
                    nc.vector.tensor_tensor(conf3[:, b, 1, :], conf[:, b, 2, :], conf3[:, b, 0, :], ALU.subtract
                                            ).then_inc(sem["conf3_ok"], 1)

                def weigh(t):
                    b = t.slot(R)
                    dve.wait_ge(sem["gelu_ok"], t.n + 1)
                    dve.wait_ge(sem["hconf_ok"], t.n + 1)
                    nc.vector.tensor_tensor(hb[:, b, :].rearrange("p (e j) -> p e j", e=EXPERTS),
                                            hb[:, b, :].rearrange("p (e j) -> p e j", e=EXPERTS),
                                            hconf[:, b, :].unsqueeze(2).to_broadcast([P, EXPERTS, HID]),
                                            ALU.mult).then_inc(sem["h_ok"], 1)

                def low_h(t):
                    b = t.slot(R)
                    dve.wait_ge(sem["hT_hi_ok"], t.n + 1)
                    nc.vector.tensor_tensor(hT_lo[:, b, :], ps_h[:, 0:HC], hT_hi[:, b, :], ALU.subtract
                                            ).then_inc(sem["hT_lo_ok"], 1)

                def add_experts(t):
                    q, b = t.slot(X), t.slot(R)
                    dve.wait_ge(sem["o_ps"], t.n + 1)
                    if t.base >= Y:
                        dve.wait_ge(sem["shift2_ok"], t.n + 1 - Y)
                    nc.vector.scalar_tensor_tensor(x2[:, q, :], ps_o[:, b, :], f.o_unscale[:], x2[:, q, :],
                                                   ALU.mult, ALU.add, accum_out=sum2[:, t.slot(Y)]
                                                   ).then_inc(sem["t_ok"], 1)

                def gain(t):
                    b = t.slot(R)
                    dve.wait_ge(sem["n_ok"], t.n + 1)
                    nc.vector.tensor_tensor(nb[:, b, :], nb[:, b, :], f.gain[:], ALU.mult
                                            ).then_inc(sem["gained_ok"], 1)

                def finish(t):
                    b, q = t.slot(R), t.slot(X)
                    dve.wait_ge(sem["gained_ok"], t.n + 1)
                    dve.wait_ge(sem["offset_ok"], t.n + 1)
                    if t.base >= R:
                        dve.wait_ge(out_done[b], 16 * t.uses(R))
                    nc.vector.tensor_tensor(ob[:, b, :], x1[:, q, :], nb[:, b, :], ALU.add
                                            ).then_inc(sem["o_ok"], 1)

                over_tiles(dve, X, [(-3, add_experts), (-1, pick), (-2, low_h), (-1, add_picked), (0, hidden),
                                    (-5, gain), (0, best_two), (1, low_x2), (0, best_places),
                                    (-1, low_confidence), (-5, finish), (-1, weigh), (3, add_attention)])

            @block.scalar
            def _(act):
                def norm1(t):
                    b, q = t.slot(R), t.slot(X)
                    act.wait_ge(sem["shift1_ok"], t.n + 1)
                    if t.base >= X:
                        act.wait_ge(sem["n_ok"], t.n + 1 - X)
                    nc.scalar.activation(x2[:, q, :], x1[:, q, :], ACT.Identity, bias=shift1[:, b],
                                         scale=rs1[:, b, 0:1]).then_inc(sem["x2_ok"], 1)

                def norm2(t):
                    b, q = t.slot(R), t.slot(X)
                    act.wait_ge(sem["shift2_ok"], t.n + 1)
                    if t.base >= R:
                        act.wait_ge(sem["o_ok"], t.n + 1 - R)
                    nc.scalar.activation(nb[:, b, :], x2[:, q, :], ACT.Identity, bias=shift2[:, b],
                                         scale=rs2[:, b]).then_inc(sem["n_ok"], 1)

                def square1(t):
                    b, q = t.slot(R), t.slot(X)
                    act.wait_ge(sem["x1_ok"], t.n + 1)
                    if t.base >= R:
                        act.wait_ge(sem["var1_ok"], (t.n + 1 - R) * 2)
                    if t.base >= 1:
                        act.wait_ge(sem["ssq1_ok"], t.n)
                    nc.scalar.activation(square[:, 0], x1[:, q, :], ACT.Square, bias=sum1[:, t.slot(Y)], scale=-float(D),
                                         accum_out=ssq1[:, b]).then_inc(sem["ssq1_ok"], 1)

                def square2(t):
                    b, q = t.slot(R), t.slot(X)
                    act.wait_ge(sem["t_ok"], t.n + 1)
                    if t.base >= R:
                        act.wait_ge(sem["var2_ok"], t.n + 1 - R)
                    if t.base >= 1:
                        act.wait_ge(sem["ssq2_ok"], t.n)
                    nc.scalar.activation(square[:, 1], x2[:, q, :], ACT.Square, bias=sum2[:, t.slot(Y)], scale=-float(D),
                                         accum_out=ssq2[:, b]).then_inc(sem["ssq2_ok"], 1)

                def high_x2(t):
                    b = t.slot(R)
                    act.wait_ge(sem["xT_ps"], t.n + 1)
                    if t.base >= R:
                        act.wait_ge(sem["z_ps"], t.n + 1 - R)
                    nc.scalar.activation(xT_hi[:, b, :], ps_x[:], ACT.Copy).then_inc(sem["xT_hi_ok"], 1)

                def gelu(t):
                    b = t.slot(R)
                    act.wait_ge(sem["z_ok"], t.n + 1)
                    if t.base >= R:
                        act.wait_ge(sem["hT_ps"], t.n + 1 - R)
                    nc.scalar.activation(hb[:, b, :], zb[:, b, 0:HC], ACT.Gelu_apprx_tanh
                                         ).then_inc(sem["gelu_ok"], 1)

                def scale_confidence(t):
                    b = t.slot(R)
                    act.wait_ge(sem["conf_ok"], t.n + 1)
                    if t.base >= R:
                        act.wait_ge(sem["h_ok"], t.n + 1 - R)
                    nc.scalar.activation(hconf[:, b, :], conf[:, b, 2, :], ACT.Copy, scale=f.hscale[:]
                                         ).then_inc(sem["hconf_ok"], 1)
                    if t.base >= R:
                        act.wait_ge(sem["hT_ps"], t.n + 1 - R)
                    nc.scalar.activation(conf3[:, b, 0:3:2, :],
                                         conf[:, b, 2, :].unsqueeze(1).to_broadcast([P, 2, EXPERTS]), ACT.Copy
                                         ).then_inc(sem["conf_hi_ok"], 1)

                def tanh(t):
                    b = t.slot(R)
                    act.wait_ge(sem["gap_ok"], t.n + 1)
                    nc.scalar.activation(gate[:, b, 3:4], gate[:, b, 2:3], ACT.Tanh, scale=0.5
                                         ).then_inc(sem["tanh_ok"], 1)

                def high_h(t):
                    b = t.slot(R)
                    act.wait_ge(sem["hT_ps"], t.n + 1)
                    if t.base >= R:
                        act.wait_ge(sem["o_ps"], t.n + 1 - R)
                    nc.scalar.activation(hT_hi[:, b, :], ps_h[:, 0:HC], ACT.Copy).then_inc(sem["hT_hi_ok"], 1)
                    nc.scalar.activation(confT[:, b, :], ps_c[:, 0:P], ACT.Copy).then_inc(sem["confT_ok"], 1)

                over_tiles(act, X, [(-2, high_h), (1, norm1), (2, square1), (1, high_x2),
                                    (-1, scale_confidence), (0, gelu), (-4, norm2), (-3, square2), (0, tanh)])

            @block.gpsimd
            def _(pool):
                def rstd1(t):
                    b = t.slot(R)
                    pool.wait_ge(sem["ssq1_ok"], t.n + 1)
                    if t.base >= R:
                        pool.wait_ge(sem["x2_ok"], t.n + 1 - R)
                    if t.base >= Y:
                        pool.wait_ge(sem["z_ok"], t.n + 1 - Y)
                    stand_alone(pool)
                    small = ACT_SCALE ** -2
                    nc.gpsimd.tensor_scalar(var1[:, b, 0:1], ssq1[:, b], small / D ** 3, EPS * small, ALU.mult, ALU.add
                                            ).then_inc(sem["var1_ok"], 1)
                    nc.gpsimd.tensor_scalar(var1[:, b, 1:2], ssq1[:, b], (1 + EPS) * small / D ** 3, EPS * EPS * small,
                                            ALU.mult, ALU.add).then_inc(sem["var1_ok"], 1)
                    pool.wait_ge(sem["var1_ok"], t.n * 2 + 2)
                    nc.gpsimd.tensor_tensor(rs1[:, b, :], var1[:, b, :], f.mhalf2[:], ALU.pow
                                            ).then_inc(sem["rs1_ok"], 1)
                    pool.wait_ge(sem["rs1_ok"], t.n + 1)
                    stand_alone(pool)
                    nc.gpsimd.tensor_scalar(shift1[:, b], sum1[:, t.slot(Y)], rs1[:, b, 0:1], -1.0 / D, ALU.mult, ALU.mult
                                            ).then_inc(sem["shift1_ok"], 1)
                    nc.gpsimd.tensor_scalar(ratio[:, b], rs1[:, b, 1:2], rs1[:, b, 0:1], var1[:, b, 0:1],
                                            ALU.mult, ALU.mult).then_inc(sem["ratio_ok"], 1)
                    pool.wait_ge(sem["ratio_ok"], t.n + 1)
                    nc.gpsimd.tensor_tensor(rz[:, t.slot(Y)], ratio[:, b], f.z_unscale[:], ALU.mult
                                            ).then_inc(sem["rz_ok"], 1)

                def shares(t):
                    b = t.slot(R)
                    g = gate[:, b, :]
                    pool.wait_ge(sem["best_ok"], t.n + 1)
                    nc.gpsimd.tensor_tensor(g[:, 2:3], best[:, b, 0:1], best[:, b, 1:2], ALU.subtract
                                            ).then_inc(sem["gap_ok"], 1)
                    pool.wait_ge(sem["best_at_ok"], t.n + 1)
                    stand_alone(pool)
                    nc.gpsimd.tensor_copy(g[:, 0:2], best_at[:, b, 0:2]).then_inc(sem["share_ok"], 1)
                    pool.wait_ge(sem["tanh_ok"], t.n + 1)
                    half = ACT_SCALE / 2
                    stand_alone(pool)
                    nc.gpsimd.tensor_scalar(g[:, 4:5], g[:, 3:4], half, half, ALU.mult, ALU.add
                                            ).then_inc(sem["share_ok"], 1)
                    nc.gpsimd.tensor_scalar(g[:, 5:6], g[:, 3:4], -half, half, ALU.mult, ALU.add
                                            ).then_inc(sem["share_ok"], 1)

                def rstd2(t):
                    b = t.slot(R)
                    pool.wait_ge(sem["ssq2_ok"], t.n + 1)
                    if t.base >= R:
                        pool.wait_ge(sem["n_ok"], t.n + 1 - R)
                    stand_alone(pool)
                    nc.gpsimd.tensor_scalar(var2[:, b], ssq2[:, b], 1.0 / D ** 3, EPS * ACT_SCALE ** 2, ALU.mult,
                                            ALU.add).then_inc(sem["var2_ok"], 1)
                    pool.wait_ge(sem["var2_ok"], t.n + 1)
                    nc.gpsimd.tensor_tensor(rs2[:, b], var2[:, b], keep.mhalf[:], ALU.pow
                                            ).then_inc(sem["rs2_ok"], 1)
                    pool.wait_ge(sem["rs2_ok"], t.n + 1)
                    stand_alone(pool)
                    nc.gpsimd.tensor_scalar(shift2[:, b], sum2[:, t.slot(Y)], rs2[:, b], -1.0 / D, ALU.mult, ALU.mult
                                            ).then_inc(sem["shift2_ok"], 1)

                def offset(t):
                    q = t.slot(X)
                    pool.wait_ge(sem["x2_ok"], t.n + 1)
                    nc.gpsimd.tensor_tensor(x1[:, q, :], x1[:, q, :], f.offset[:], ALU.add
                                            ).then_inc(sem["offset_ok"], 1)

                over_tiles(pool, X, [(-4, rstd2), (0, offset), (2, rstd1), (0, shares)])


class Namespace:
    pass


def program(nc, x, src, dst, gnn_W, gnn_b, W_in, b_in, Wq, Wk, Wv, W_out, b_out, Wg, W1, b1, W2, b2, ln_g, ln_b,
            out_g, out_b, out):
    h_table = nc.dram_tensor("h_table", [N, D], F32).ap()
    y_table = nc.dram_tensor("y_table", [N + SPARE, D], F32).ap()
    dinv_table = nc.dram_tensor("dinv_table", [TILES * P, 1], F32).ap()
    keep, f = Namespace(), Namespace()
    with ExitStack() as st:
        keep.lasting = st.enter_context(ExitStack())
        m = Mem(nc, st, keep.lasting)
        keep.ident = m.sb("ident", [P, P])
        keep.mhalf = m.sb("mhalf", [P, 1])
        keep.one = m.sb("one", [P, 1])
        keep.src = m.sb("src_t", [P, ETILES], I32)
        keep.dst = m.sb("dst_t", [P, ETILES], I32)
        keep.dstf = m.sb("dst_f", [P, ETILES])
        keep.target = m.sb("target", [P, ETILES], I32)
        keep.mean = m.sb("mean", [P, TILES])
        keep.rstd = m.sb("rstd", [P, TILES])
        keep.dinv = m.sb("dinv", [P, TILES])
        keep.hcoef = m.sb("hcoef", [P, TILES])
        keep.unscale = m.sb("unscale", [P, 2])
        keep.kmax = m.sb("kmax", [P, QC])
        keep.rk = m.sb("rk", [P, 2])
        keep.qT_hi = m.sb("qT_hi", [P, TILES, QC], F16)
        keep.qT_lo = m.sb("qT_lo", [P, TILES, QC], F16)
        keep.g = m.sb("g", [P, 2, D])
        with ExitStack() as st2:
            keep.k = Mem(nc, st2, keep.lasting).sb("k_logits", [P, TILES, QC])
            with ExitStack() as st3:
                w3 = Mem(nc, st3, keep.lasting)
                keep.w_hi = w3.sb("w_hi", [P, KD, 2 * D], F16)
                keep.w_lo = w3.sb("w_lo", [P, KD, 2 * D], F16)
                keep.ones_b = w3.sb("ones_b", [64, P], F16)
                keep.bias16 = w3.sb("bias16", [64, D], F16)
                prepare(nc, keep, src, dst, gnn_W, W_in, b_in, Wq, Wk, dinv_table, y_table)
                first_pass(nc, keep, x, h_table, y_table)
            second_pass(nc, keep, x, dst, h_table, y_table, dinv_table)
        f.zbias = m.sb("zbias", [P, ZC])
        f.gain = m.sb("gain", [P, D])
        f.offset = m.sb("offset", [P, D])
        f.b2s = m.sb("b2s", [3 * EXPERTS, D], F16)
        f.ident16 = m.sb("ident16", [P, P], F16)
        f.iota = m.sb("iota8", [P, EXPERTS])
        f.hscale = m.sb("hscale", [P, 1])
        f.mhalf2 = m.sb("mhalf2", [P, 2])
        f.m_unscale = m.sb("m_unscale", [P, 1])
        f.z_unscale = m.sb("z_unscale", [P, 1])
        f.o_unscale = m.sb("o_unscale", [P, 1])
        f.m_hi = m.sb("m_hi", [P, 2, D], F16)
        f.m_lo = m.sb("m_lo", [P, 2, D], F16)
        f.w1_hi = m.sb("w1_hi", [P, KD, ZC], F16)
        f.w1_lo = m.sb("w1_lo", [P, KD, ZC], F16)
        f.w2_hi = m.sb("w2_hi", [P, 2, D], F16)
        f.w2_lo = m.sb("w2_lo", [P, 2, D], F16)
        fold(nc, keep, f, W_in, b_in, Wv, W_out, b_out, gnn_b, Wg, W1, b1, W2, b2, ln_g, ln_b, out_g, out_b)
        third_pass(nc, keep, f, y_table, out)


_INS = ["x", "src", "dst", "L0_gnn_W", "L0_gnn_b", "L0_mix_W_in", "L0_mix_b_in", "L0_mix_Wq", "L0_mix_Wk",
        "L0_mix_Wv", "L0_mix_W_out", "L0_mix_b_out", "L0_ffn_Wg", "L0_ffn_W1", "L0_ffn_b1", "L0_ffn_W2",
        "L0_ffn_b2", "L0_ffn_ln_g", "L0_ffn_ln_b", "L0_ffn_out_g", "L0_ffn_out_b"]


def kernel(**inputs):
    import numpy as np
    import concourse.bacc as bacc
    from concourse.bass_utils import run_bass_kernel_spmd

    nc = bacc.Bacc("TRN2", target_bir_lowering=False, num_devices=1)
    arrays, args = {}, []
    for name in _INS:
        array = np.ascontiguousarray(inputs[name])
        arrays[f"in_{name}"] = array
        args.append(nc.dram_tensor(f"in_{name}", array.shape, mybir.dt.from_np(array.dtype),
                                   kind="ExternalInput").ap())
    out = nc.dram_tensor("out_x", (N, D), F32, kind="ExternalOutput").ap()
    program(nc, *args, out)
    result = run_bass_kernel_spmd(nc, [arrays], core_ids=[0])
    return result.results[0]["out_x"]
```

```python
from contextlib import ExitStack

import concourse.bass as bass
from concourse import mybir

ALU = mybir.AluOpType
ACT = mybir.ActivationFunctionType
AX = mybir.AxisListType
F32 = mybir.dt.float32
F16 = mybir.dt.float16
I32 = mybir.dt.int32
U32 = mybir.dt.uint32
ROP = bass.bass_isa.ReduceOp

P = 128
N, D = 10000, 512
EDGES = 2500
HEADS, HEAD, SLICE = 8, 64, 32
QC = HEADS * SLICE
EXPERTS, HID = 8, 32
HC = EXPERTS * HID
ZC = HC + EXPERTS
KD = D // P
PAIRS = HEADS // 2
TILES = -(-N // P)
TAIL = N - (TILES - 1) * P
ETILES = -(-EDGES // P)
ETAIL = EDGES - (ETILES - 1) * P
EPS = 1e-5
ACT_SCALE = 1024.0
W_TOP = 2.0 ** 14
EXP_MASK = 0x7F800000
SPARE = P
Y_SLOTS = 4


class Tile:

    def __init__(self, base, unroll=1, j=None):
        self.base, self.unroll, self.j = base, unroll, j
        self.n = base if j is None else j * unroll + base

    def slot(self, ring):
        return self.base % ring

    def uses(self, ring):
        if self.j is None:
            return self.base // ring
        return self.j * (self.unroll // ring) + self.base // ring

    def rows(self):
        return TAIL if self.j is None and self.base == TILES - 1 else P


def over_tiles(eng, unroll, stages):
    ahead, behind = max(o for o, _ in stages), min(o for o, _ in stages)
    start = unroll * -(-(unroll - behind) // unroll)
    count = (TILES - 1 - ahead - start) // unroll

    def peeled(lo, hi):
        for s in range(lo, hi):
            for o, body in stages:
                if 0 <= s + o < TILES:
                    body(Tile(s + o))

    peeled(-ahead, start)
    with eng.Fori(0, count) as j:
        for c in range(unroll):
            for o, body in stages:
                body(Tile(start + c + o, unroll, j))
    peeled(start + count * unroll, TILES - behind)


def stand_alone(eng):
    eng.nop(nofuse=True)


class Mem:

    def __init__(self, nc, stack, lasting):
        self.nc, self.stack, self.lasting, self.own = nc, stack, lasting, []

    def sb(self, name, shape, dt=F32):
        return self.stack.enter_context(self.nc.sbuf_tensor(name, shape, dt))

    def ps(self, name, shape, dt=F32):
        return self.stack.enter_context(self.nc.psum_tensor(name, shape, dt))

    def sem(self, name):
        handle = self.lasting.enter_context(self.nc.semaphore(name))
        self.own.append(handle)
        return handle

    def sems(self, name, n):
        return [self.sem(f"{name}{i}") for i in range(n)]


class Arena(Mem):

    def __init__(self, nc, stack, lasting, tensor):
        super().__init__(nc, stack, lasting)
        self.flat, self.at = tensor[:].rearrange("p a b -> p (a b)"), 0

    def sb(self, name, shape, dt=F32):
        count = 1
        for n in shape[1:]:
            count *= n
        words = -(-count * (2 if dt == F16 else 4) // 4)
        view = self.flat[0:shape[0], self.at:self.at + words]
        self.at += words
        if dt != F32:
            view = view.bitcast(dt)
        if len(shape) == 3:
            view = view.rearrange("p (a b) -> p a b", a=shape[1])
        if len(shape) == 4:
            view = view.rearrange("p (a b c) -> p a b c", a=shape[1], b=shape[2])
        return view


class Chain:

    def __init__(self, eng, sem):
        self.eng, self.sem, self.n = eng, sem, 0

    def do(self, ins):
        self.n += 1
        return ins.then_inc(self.sem, 1)

    def settle(self):
        self.eng.wait_ge(self.sem, self.n)


def load_target_row(sp, j, dst, row, row_in, reused, row_used, last):
    if reused:
        sp.wait_ge(row_used, j)
    cols = ETAIL if last else P
    sp.dma_start(row[:, 0:cols], dst.rearrange("(a e) -> a e", a=1)[:, bass.ds(j * P, cols)]
                 .to_broadcast([P, cols])).then_inc(row_in, 16)


def power_of_two(nc, out, value):
    return nc.vector.tensor_scalar(out.bitcast(I32), value.bitcast(I32), EXP_MASK, None, ALU.bitwise_and)


def prepare(nc, keep, src, dst, W_gnn, W_in, b_in, Wq, Wk, dinv_table, y_table):
    with ExitStack() as st:
        m = Arena(nc, st, st, keep.k)
        win = m.sb("p_win", [P, KD, D])
        wg = m.sb("p_wg", [P, KD, D])
        winT = m.sb("p_winT", [P, PAIRS, D])
        wqk = m.sb("p_wqk", [P, KD, D])
        bd = m.sb("p_bd", [P, 2, 2, SLICE])
        bcol = m.sb("p_bcol", [P, PAIRS])
        bcolB = m.sb("p_bcolB", [P, PAIRS, 64])
        brow = m.sb("p_brow", [64, D])
        brow_hi = m.sb("p_brow_hi", [64, D], F16)
        peak = m.sb("p_peak", [P, 2])
        peakb = m.sb("p_peakb", [P, 1])
        peak_all = m.sb("p_peak_all", [P, 2])
        pow2 = m.sb("p_pow2", [P, 2])
        wscale = m.sb("p_wscale", [P, 2])
        iota_i = m.sb("p_iota_i", [P, P], I32)
        iota = m.sb("p_iota", [P, P])
        spare_i = m.sb("p_spare_i", [P, 1], I32)
        part = m.sb("p_part", [P, 2, ETILES], I32)
        partf = m.sb("p_partf", [P, 2, ETILES])
        hot_lo = m.sb("p_hot_lo", [P, ETILES, P], F16)
        hot_hi = m.sb("p_hot_hi", [P, ETILES, TILES], F16)
        deg = m.sb("p_deg", [P, TILES])
        root = m.sb("p_root", [P, TILES])
        error = m.sb("p_error", [P, TILES])
        dinvT = m.sb("p_dinvT", [TILES, P])
        zero = m.sb("p_zero", [P, D])
        ps_t = m.ps("pp_t", [P, 2, D])
        ps_w = m.ps("pp_w", [P, 2, D])
        ps_b = m.ps("pp_b", [64, D])
        ps_d = m.ps("pp_d", [P, D])
        ps_i = m.ps("pp_i", [P, D])

        (win_in, wg_in, bd_in, bcol_in, edges_in, dinv_out, spare_out) = (
            m.sem("p_" + n) for n in ("win_in", "wg_in", "bd_in", "bcol_in", "edges_in",
                                      "dinv_out", "spare_out"))
        (filled, ident_ok, earlier_ok, iota_ok, pool_own, peaks_ok, peak_all_ok, deg_ok, dinv_ok, dve_own,
         winT_ps, winT_ok, wqk_ps, wqk_ok, bcolB_ok, brow_ps, hot_ok, deg_ps, dinvT_ps, dinvT_ok,
         codes_ok, wscale_ok, w_hi_ok, root_ok) = (
            m.sem("p_" + n) for n in (
                "filled", "ident_ok", "earlier_ok", "iota_ok", "pool_own", "peaks_ok", "peak_all_ok", "deg_ok",
                "dinv_ok", "dve_own", "winT_ps", "winT_ok", "wqk_ps", "wqk_ok", "bcolB_ok", "brow_ps", "hot_ok",
                "deg_ps", "dinvT_ps", "dinvT_ok", "codes_ok", "wscale_ok", "w_hi_ok", "root_ok"))

        with nc.Block() as block:
            @block.gpsimd
            def _(pool):
                own = Chain(pool, pool_own)
                own.do(nc.gpsimd.memset(keep.ident[:], 0.0))
                own.do(nc.gpsimd.memset(keep.earlier[:], 1.0))
                nc.gpsimd.memset(bd[:], 0.0).then_inc(filled, 1)
                nc.gpsimd.memset(keep.src[:], 0).then_inc(filled, 1)
                nc.gpsimd.memset(keep.dst[:], N).then_inc(filled, 1)
                nc.gpsimd.memset(zero[:], 0.0).then_inc(filled, 1)
                own.do(nc.gpsimd.memset(keep.mhalf[:], -0.5))
                own.settle()
                nc.gpsimd.affine_select(out=keep.ident[:], in_=keep.ident[:], compare_op=ALU.not_equal,
                                        fill=1.0, base=0, pattern=[[-1, P]],
                                        channel_multiplier=1).then_inc(ident_ok, 1)
                nc.gpsimd.affine_select(out=keep.earlier[:], in_=keep.earlier[:], compare_op=ALU.is_gt,
                                        fill=0.0, base=0, pattern=[[-1, P]], channel_multiplier=1
                                        ).then_inc(earlier_ok, 1)
                nc.gpsimd.iota(iota_i[:], [[1, P]], base=0, channel_multiplier=0).then_inc(iota_ok, 1)
                nc.gpsimd.iota(spare_i[:], [[1, 1]], base=N, channel_multiplier=1).then_inc(iota_ok, 1)
                pool.wait_ge(codes_ok, 1)
                stand_alone(pool)
                for j in range(ETILES):
                    nc.gpsimd.tensor_scalar(hot_hi[:, j, :], iota[:, 0:TILES], partf[:, 1, j:j + 1], None,
                                            ALU.is_equal).then_inc(hot_ok, 1)
                pool.wait_ge(peaks_ok, 3)
                nc.gpsimd.partition_all_reduce(peak_all[:], peak[:], P, ROP.max).then_inc(peak_all_ok, 1)

            @block.sync
            def _(sp):
                sp.dma_start(win[:], W_in.rearrange("(k p) n -> p k n", p=P)).then_inc(win_in, 16)
                sp.dma_start(wg[:], W_gnn.rearrange("(k p) n -> p k n", p=P)).then_inc(wg_in, 16)
                sp.wait_ge(filled, 4)
                for h in range(2):
                    rows = slice(h * HEAD, (h + 1) * HEAD)
                    sp.dma_start(bd[rows, 0, h, :], Wq).then_inc(bd_in, 16)
                    sp.dma_start(bd[rows, 1, h, :], Wk).then_inc(bd_in, 16)
                sp.dma_start(y_table[N:N + SPARE, :], zero[:]).then_inc(spare_out, 16)
                sp.wait_ge(dinvT_ok, 1)
                sp.dma_start(dinv_table.rearrange("(t p) o -> t (p o)", p=P), dinvT[:]).then_inc(dinv_out, 16)
                sp.wait_ge(dinv_out, 16)
                sp.wait_ge(spare_out, 16)

            @block.scalar
            def _(act):
                act.wait_ge(filled, 4)
                full = (ETILES - 1) * P
                for vec, tile in ((src, keep.src), (dst, keep.dst)):
                    act.dma_start(tile[:, 0:ETILES - 1],
                                  vec[0:full].rearrange("(j p) -> p j", p=P),
                                  allow_slow_non_contiguous=True).then_inc(edges_in, 16)
                    act.dma_start(tile[0:ETAIL, ETILES - 1:ETILES],
                                  vec[full:EDGES].rearrange("(p o) -> p o", o=1)).then_inc(edges_in, 16)
                act.dma_start(bcol[:], b_in.rearrange("(j p) -> p j", p=P),
                              allow_slow_non_contiguous=True).then_inc(bcol_in, 16)
                for j in range(PAIRS):
                    act.wait_ge(winT_ps, j + 1)
                    nc.scalar.activation(winT[:, j, :], ps_t[:, j % 2, :], ACT.Copy).then_inc(winT_ok, 1)
                for k in range(KD):
                    act.wait_ge(wqk_ps, k + 1)
                    for qk in range(2):
                        nc.scalar.activation(
                            wqk[:, k, qk * QC:(qk + 1) * QC].rearrange("p (j c) -> p j c", j=PAIRS),
                            ps_w[:, k % 2, :].rearrange("p (j q c) -> p q j c", j=PAIRS, q=2)[:, qk],
                            ACT.Copy).then_inc(wqk_ok, 1)
                act.wait_ge(deg_ok, 1)
                nc.scalar.activation(root[:], deg[:], ACT.Sqrt).then_inc(root_ok, 1)
                act.wait_ge(dinvT_ps, 1)
                nc.scalar.activation(dinvT[:], ps_i[0:TILES, 0:P], ACT.Copy).then_inc(dinvT_ok, 1)
                act.wait_ge(wscale_ok, 1)
                for w, col, c in ((wqk, 0, 0), (wg, D, 1)):
                    for k in range(KD):
                        nc.scalar.activation(keep.w_hi[:, k, col:col + D], w[:, k, :], ACT.Copy,
                                             scale=wscale[:, c:c + 1]).then_inc(w_hi_ok, 1)

            @block.tensor
            def _(pe):
                pe.wait_ge(ident_ok, 1)
                pe.wait_ge(win_in, 16)
                for j in range(PAIRS):
                    if j >= 2:
                        pe.wait_ge(winT_ok, j - 1)
                    for k in range(KD):
                        last = nc.tensor.transpose(ps_t[:, j % 2, k * P:(k + 1) * P],
                                                   win[:, k, j * P:(j + 1) * P], keep.ident[:])
                    last.then_inc(winT_ps, 1)
                pe.wait_ge(winT_ok, PAIRS)
                pe.wait_ge(bd_in, 64)
                for k in range(KD):
                    if k >= 2:
                        pe.wait_ge(wqk_ok, 2 * (k - 1))
                    for j in range(PAIRS):
                        last = nc.tensor.matmul(ps_w[:, k % 2, j * P:(j + 1) * P],
                                                winT[:, j, k * P:(k + 1) * P],
                                                bd[:].rearrange("p q h s -> p (q h s)"), start=True, stop=True)
                    last.then_inc(wqk_ps, 1)
                pe.wait_ge(bcolB_ok, 1)
                for j in range(PAIRS):
                    last = nc.tensor.matmul(ps_b[:, j * P:(j + 1) * P], bcolB[:, j, :],
                                            bd[:].rearrange("p q h s -> p (q h s)"), start=True, stop=True)
                last.then_inc(brow_ps, 1)
                pe.wait_ge(hot_ok, 2 * ETILES)
                for j in range(ETILES):
                    last = nc.tensor.matmul(ps_d[:, 0:TILES], hot_lo[:, j, :], hot_hi[:, j, :],
                                            start=(j == 0), stop=(j == ETILES - 1))
                last.then_inc(deg_ps, 1)
                pe.wait_ge(dinv_ok, 1)
                nc.tensor.transpose(ps_i[0:TILES, 0:P], keep.dinv[:], keep.ident[:]).then_inc(dinvT_ps, 1)

            @block.vector
            def _(dve):
                own = Chain(dve, dve_own)
                own.do(nc.vector.memset(keep.bias16[:], 0.0))
                own.do(nc.vector.memset(keep.ones_b[:], ACT_SCALE))
                own.do(nc.vector.memset(keep.one[:], 1.0))
                dve.wait_ge(wg_in, 16)
                nc.vector.tensor_reduce(peak[:, 1:2], wg[:], AX.XY, ALU.max,
                                        apply_absolute_value=True).then_inc(peaks_ok, 1)
                dve.wait_ge(edges_in, 64)
                dve.wait_ge(iota_ok, 2)
                own.do(nc.vector.tensor_scalar(part[:, 0, :], keep.dst[:], P - 1, None, ALU.bitwise_and))
                own.do(nc.vector.tensor_scalar(part[:, 1, :], keep.dst[:], 7, None, ALU.logical_shift_right))
                own.do(nc.vector.tensor_copy(iota[:], iota_i[:]))
                own.do(nc.vector.tensor_copy(keep.spare[:], spare_i[:]))
                own.do(nc.vector.tensor_copy(keep.dstf[:], keep.dst[:]))
                own.settle()
                own.do(nc.vector.tensor_scalar(keep.padding[:], keep.dstf[:], float(N), None, ALU.is_equal))
                nc.vector.tensor_copy(partf[:], part[:]).then_inc(codes_ok, 1)
                dve.wait_ge(codes_ok, 1)
                for j in range(ETILES):
                    nc.vector.tensor_scalar(hot_lo[:, j, :], iota[:], partf[:, 0, j:j + 1], None,
                                            ALU.is_equal).then_inc(hot_ok, 1)
                dve.wait_ge(bcol_in, 16)
                nc.vector.tensor_copy(bcolB[:], bcol[:].unsqueeze(2).to_broadcast([P, PAIRS, 64])
                                      ).then_inc(bcolB_ok, 1)
                dve.wait_ge(brow_ps, 1)
                for qk in range(2):
                    own.do(nc.vector.tensor_copy(
                        brow[:, qk * QC:(qk + 1) * QC].rearrange("p (j c) -> p j c", j=PAIRS),
                        ps_b[:].rearrange("p (j q c) -> p q j c", j=PAIRS, q=2)[:, qk]))
                own.do(nc.vector.memset(peakb[:], 1e-30))
                own.settle()
                own.do(nc.vector.tensor_reduce(peakb[0:64], brow[:], AX.X, ALU.max, apply_absolute_value=True))
                dve.wait_ge(wqk_ok, 2 * KD)
                own.do(nc.vector.tensor_reduce(peak[:, 0:1], wqk[:], AX.XY, ALU.max, apply_absolute_value=True))
                own.settle()
                nc.vector.tensor_tensor(peak[:, 0:1], peak[:, 0:1], peakb[:], ALU.max).then_inc(peaks_ok, 1)
                dve.wait_ge(peaks_ok, 2)
                nc.vector.tensor_scalar(peak[:, 1:2], peak[:, 1:2], 1e-30, None, ALU.max).then_inc(peaks_ok, 1)
                dve.wait_ge(deg_ps, 1)
                nc.vector.tensor_scalar(deg[:], ps_d[:, 0:TILES], 1.0, None, ALU.add).then_inc(deg_ok, 1)
                dve.wait_ge(peak_all_ok, 1)
                own.do(power_of_two(nc, pow2[:], peak_all[:]))
                own.settle()
                own.do(nc.vector.reciprocal(wscale[:], pow2[:]))
                own.settle()
                nc.vector.tensor_scalar(wscale[:], wscale[:], W_TOP, None, ALU.mult).then_inc(wscale_ok, 1)
                own.do(nc.vector.tensor_scalar(keep.unscale[:], pow2[:], 1.0 / (W_TOP * ACT_SCALE), None, ALU.mult))
                dve.wait_ge(root_ok, 1)
                own.do(nc.vector.reciprocal(root[:], root[:]))
                own.settle()
                own.do(nc.vector.tensor_tensor(error[:], root[:], root[:], ALU.mult))
                own.settle()
                own.do(nc.vector.tensor_tensor(error[:], error[:], deg[:], ALU.mult))
                own.settle()
                own.do(nc.vector.tensor_scalar(error[:], error[:], -0.5, 1.5, ALU.mult, ALU.add))
                own.settle()
                nc.vector.tensor_tensor(keep.dinv[:], root[:], error[:], ALU.mult).then_inc(dinv_ok, 1)
                dve.wait_ge(wscale_ok, 1)
                own.do(nc.vector.tensor_scalar(brow_hi[:], brow[:], wscale[0:64, 0:1], None, ALU.mult))
                for n, (w, col, c, k) in enumerate([(w, col, c, k) for w, col, c in ((wqk, 0, 0), (wg, D, 1))
                                                    for k in range(KD)]):
                    dve.wait_ge(w_hi_ok, n + 1)
                    own.do(nc.vector.scalar_tensor_tensor(keep.w_lo[:, k, col:col + D], w[:, k, :],
                                                          wscale[:, c:c + 1], keep.w_hi[:, k, col:col + D],
                                                          ALU.mult, ALU.subtract))
                own.settle()
                dve.wait_ge(dinv_ok, 1)
                own.do(nc.vector.tensor_scalar(keep.hcoef[:], keep.dinv[:], keep.unscale[:, 1:2], None, ALU.mult))
                own.do(nc.vector.tensor_copy(keep.bias16[0:1, :], brow_hi[0:1, :]))
                own.do(nc.vector.scalar_tensor_tensor(keep.bias16[32:33, :], brow[32:33, :], wscale[32:33, 0:1],
                                                      brow_hi[32:33, :], ALU.mult, ALU.subtract))
                own.settle()
    return m.own



def first_pass(nc, keep, x, dst, h_table, y_table, dinv_table):
    with ExitStack() as st:
        m = Mem(nc, st, keep.lasting)
        X, R = 4, 2
        xb = m.sb("a_x", [P, X, D])
        xn = m.sb("a_xn", [P, R, D])
        xT_hi = m.sb("a_xT_hi", [P, R, D], F16)
        xT_lo = m.sb("a_xT_lo", [P, R, D], F16)
        hb = m.sb("a_h", [P, R, D])
        qb = m.sb("a_q", [P, X, QC])
        bias = keep.g[:, 0, :]
        stats = m.sb("a_stats", [P, R, 6])
        mv = m.sb("a_mv", [P, R, 2])
        var = m.sb("a_var", [P, R, 1])
        top = m.sb("a_top", [P, R, HEADS])
        total = m.sb("a_total", [P, R, HEADS])
        index = m.sb("a_index", [P, 1], I32)
        dinv_rows = m.sb("a_dinv_rows", [P, 1])
        ps_x = m.ps("ap_x", [P, R, D])
        ps_qk = m.ps("ap_qk", [P, R, D])
        ps_h = m.ps("ap_h", [P, R, D])
        ps_q = m.ps("ap_q", [P, R, D])

        x_in = m.sems("a_x_in", X)
        y_out = m.sems("a_y_out", X)
        h_out = m.sems("a_h_out", R)
        (stats_ok, mv_ok, var_ok, rstd_ok, mean_ok, xn_ok, xT_ps, xT_hi_ok, xT_lo_ok, qk_ps, h_ps, k_ok, kmax_ok,
         q_in_ok, bias_ps, bias_ok, top_ok, less_ok, exp_ok, total_ok, recip_ok, q_ok, q_ps, qT_hi_ok, qT_lo_ok,
         h_ok, y_ok) = (
            m.sem("a_" + n) for n in (
                "stats_ok", "mv_ok", "var_ok", "rstd_ok", "mean_ok", "xn_ok", "xT_ps", "xT_hi_ok", "xT_lo_ok",
                "qk_ps", "h_ps", "k_ok", "kmax_ok", "q_in_ok", "bias_ps", "bias_ok", "top_ok", "less_ok",
                "exp_ok", "total_ok", "recip_ok", "q_ok",
                "q_ps", "qT_hi_ok", "qT_lo_ok", "h_ok", "y_ok"))

        dstrow = keep.g[:, 1, P:2 * P].bitcast(I32)
        before = keep.g[:, 1, 2 * P:2 * P + P // 2].bitcast(F16)
        prev = m.sb("a_prev", [P, 1])
        move = m.sb("a_move", [P, 1])
        dstrow_in, before_ok, prev_ok, moved_ok, target_ok = (
            m.sem("a_" + n) for n in ("dstrow_in", "before_ok", "prev_ok", "moved_ok", "target_ok"))
        index_ok, dinv_in, dinv_kept = m.sem("a_index_ok"), m.sem("a_dinv_in"), m.sem("a_dinv_kept")

        def heads(ap):
            return ap.rearrange("p (h s) -> p h s", h=HEADS)

        with nc.Block() as block:
            @block.sync
            def _(sp):
                def load(t):
                    if t.base >= X:
                        sp.wait_ge(y_out[t.slot(X)], 16 * t.uses(X))
                    r = t.rows()
                    sp.dma_start(xb[0:r, t.slot(X), :], x[bass.ds(t.n * P, r), :]).then_inc(x_in[t.slot(X)], 16)

                def store(t):
                    r = t.rows()
                    sp.wait_ge(h_ok, t.n + 1)
                    sp.dma_start(h_table[bass.ds(t.n * P, r), :], hb[0:r, t.slot(R), :]
                                 ).then_inc(h_out[t.slot(R)], 16)
                    sp.wait_ge(y_ok, t.n + 1)
                    sp.dma_start(y_table[bass.ds(t.n * P, r), :], xb[0:r, t.slot(X), :]
                                 ).then_inc(y_out[t.slot(X)], 16)

                def load_targets(t):
                    if t.base % X == 0:
                        load_target_row(sp, t.uses(X), dst, dstrow, dstrow_in, t.base >= X, before_ok,
                                        t.j is None and t.base // X == ETILES - 1)

                over_tiles(sp, X, [(3, load), (1, load_targets), (0, store)])
                for q in range(X):
                    sp.wait_ge(y_out[q], 16 * len(range(q, TILES, X)))
                for q in range(R):
                    sp.wait_ge(h_out[q], 16 * len(range(q, TILES, R)))

            @block.gpsimd
            def _(pool):
                def rstd(t):
                    b = t.slot(R)
                    pool.wait_ge(mv_ok, t.n + 1)
                    stand_alone(pool)
                    nc.gpsimd.tensor_scalar(var[:, b], mv[:, b, 1:2], EPS, ACT_SCALE ** -2, ALU.add, ALU.mult
                                            ).then_inc(var_ok, 1)
                    nc.gpsimd.tensor_copy(keep.mean[:, bass.ds(t.n, 1)], mv[:, b, 0:1]).then_inc(mean_ok, 1)
                    pool.wait_ge(var_ok, t.n + 1)
                    nc.gpsimd.tensor_tensor(keep.rstd[:, bass.ds(t.n, 1)], var[:, b], keep.mhalf[:], ALU.pow
                                            ).then_inc(rstd_ok, 1)

                def normalise_q(t):
                    q = t.slot(X)
                    pool.wait_ge(recip_ok, t.n + 1)
                    nc.gpsimd.tensor_tensor(heads(qb[:, q, :]), heads(qb[:, q, :]),
                                            total[:, t.slot(R), :].unsqueeze(2).to_broadcast([P, HEADS, SLICE]),
                                            ALU.mult).then_inc(q_ok, 1)

                def gather_dinv(t):
                    if t.base % X:
                        return
                    j = t.uses(X)
                    if t.base >= X:
                        pool.wait_ge(dinv_kept, j)
                    stand_alone(pool)
                    nc.gpsimd.tensor_copy(index[:], keep.dst[:, bass.ds(j, 1)]).then_inc(index_ok, 1)
                    pool.wait_ge(index_ok, j + 1)
                    stand_alone(pool)
                    pool.indirect_dma_start(dinv_rows[:], None, dinv_table, bass.IndirectOffsetOnAxis(
                        index[:], 0)).then_inc(dinv_in, 16)

                def keep_dinv(t):
                    if t.base % X != 2:
                        return
                    j = t.uses(X)
                    pool.wait_ge(dinv_in, 16 * (j + 1))
                    stand_alone(pool)
                    nc.gpsimd.tensor_copy(keep.dst_dinv[:, bass.ds(j, 1)], dinv_rows[:]).then_inc(dinv_kept, 1)

                over_tiles(pool, X, [(-2, normalise_q), (2, rstd), (0, gather_dinv), (0, keep_dinv)])

            @block.vector
            def _(dve):
                def norm(t):
                    dve.wait_ge(rstd_ok, t.n + 1)
                    dve.wait_ge(mean_ok, t.n + 1)
                    if t.base >= R:
                        dve.wait_ge(xT_ps, t.n + 1 - R)
                    nc.vector.tensor_scalar(xn[:, t.slot(R), :], xb[:, t.slot(X), :],
                                            keep.mean[:, bass.ds(t.n, 1)], keep.rstd[:, bass.ds(t.n, 1)],
                                            ALU.subtract, ALU.mult).then_inc(xn_ok, 1)

                def statistics(t):
                    dve.wait_ge(x_in[t.slot(X)], 16 * (t.uses(X) + 1))
                    nc.vector.bn_stats(stats[:, t.slot(R), :], xb[:, t.slot(X), :]).then_inc(stats_ok, 1)

                def aggregate(t):
                    dve.wait_ge(stats_ok, t.n + 1)
                    if t.base >= R:
                        dve.wait_ge(mean_ok, t.n + 1 - R)
                    stand_alone(dve)
                    nc.vector.bn_aggr(mv[:, t.slot(R), :], stats[:, t.slot(R), :]).then_inc(mv_ok, 1)

                def low_half(t):
                    dve.wait_ge(xT_hi_ok, t.n + 1)
                    b = t.slot(R)
                    nc.vector.tensor_tensor(xT_lo[:, b, :], ps_x[:, b, :], xT_hi[:, b, :], ALU.subtract
                                            ).then_inc(xT_lo_ok, 1)

                def bias_q(t):
                    b, q = t.slot(R), t.slot(X)
                    dve.wait_ge(qk_ps, t.n + 1)
                    if t.base >= X:
                        dve.wait_ge(q_ps, t.n + 1 - X)
                    nc.vector.tensor_tensor(qb[:, q, :], ps_qk[:, b, 0:QC], bias[:, 0:QC], ALU.add
                                            ).then_inc(q_in_ok, 1)

                def bias_k(t):
                    nc.vector.scalar_tensor_tensor(keep.k[:, t.n, :], ps_qk[:, t.slot(R), QC:2 * QC],
                                                   keep.unscale[:, 0:1], bias[:, QC:2 * QC], ALU.mult, ALU.add
                                                   ).then_inc(k_ok, 1)

                def row_max(t):
                    dve.wait_ge(q_in_ok, t.n + 1)
                    nc.vector.tensor_reduce(top[:, t.slot(R), :], heads(qb[:, t.slot(X), :]), AX.X, ALU.max
                                            ).then_inc(top_ok, 1)

                def column_max(t):
                    dve.wait_ge(k_ok, t.n + 1)
                    if t.base == 0 and t.j is None:
                        nc.vector.tensor_copy(keep.kmax[:], keep.k[:, 0, :]).then_inc(kmax_ok, 1)
                    else:
                        dve.wait_ge(kmax_ok, t.n)
                        r = t.rows()
                        nc.vector.tensor_tensor(keep.kmax[0:r], keep.kmax[0:r], keep.k[0:r, t.n, :], ALU.max
                                                ).then_inc(kmax_ok, 1)

                def less_max(t):
                    q = t.slot(X)
                    dve.wait_ge(top_ok, t.n + 1)
                    nc.vector.tensor_tensor(heads(qb[:, q, :]), heads(qb[:, q, :]),
                                            top[:, t.slot(R), :].unsqueeze(2).to_broadcast([P, HEADS, SLICE]),
                                            ALU.subtract).then_inc(less_ok, 1)

                def totals(t):
                    dve.wait_ge(exp_ok, t.n + 1)
                    if t.base >= R:
                        dve.wait_ge(q_ok, t.n + 1 - R)
                    nc.vector.tensor_reduce(total[:, t.slot(R), :], heads(qb[:, t.slot(X), :]), AX.X, ALU.add
                                            ).then_inc(total_ok, 1)

                def reciprocals(t):
                    dve.wait_ge(total_ok, t.n + 1)
                    nc.vector.reciprocal(total[:, t.slot(R), :], total[:, t.slot(R), :]).then_inc(recip_ok, 1)

                def low_q(t):
                    dve.wait_ge(qT_hi_ok, t.n + 1)
                    nc.vector.scalar_tensor_tensor(keep.qT_lo[:, t.n, :], ps_q[:, t.slot(R), 0:QC], ACT_SCALE,
                                                   keep.qT_hi[:, t.n, :], ALU.mult, ALU.subtract
                                                   ).then_inc(qT_lo_ok, 1)

                def find_earlier(t):
                    if t.base % X:
                        return
                    j = t.uses(X)
                    dve.wait_ge(dstrow_in, 16 * (j + 1))
                    if t.base >= X:
                        dve.wait_ge(moved_ok, 3 * j)
                    nc.vector.scalar_tensor_tensor(before[:], dstrow[:], keep.dstf[:, bass.ds(j, 1)],
                                                   keep.earlier[:], ALU.is_equal, ALU.mult, accum_out=prev[:]
                                                   ).then_inc(before_ok, 1)

                def distance_to_spare(t):
                    if t.base % X:
                        return
                    j = t.uses(X)
                    dve.wait_ge(before_ok, j + 1)
                    nc.vector.tensor_scalar(prev[:], prev[:], keep.padding[:, bass.ds(j, 1)], 0.0, ALU.add,
                                            ALU.is_gt).then_inc(prev_ok, 1)
                    nc.vector.tensor_scalar(move[:], keep.spare[:], keep.dstf[:, bass.ds(j, 1)], None,
                                            ALU.subtract).then_inc(moved_ok, 1)

                def distance_if_before(t):
                    if t.base % X:
                        return
                    j = t.uses(X)
                    dve.wait_ge(prev_ok, j + 1)
                    dve.wait_ge(moved_ok, 3 * j + 1)
                    nc.vector.tensor_tensor(move[:], move[:], prev[:], ALU.mult).then_inc(moved_ok, 1)

                def target_or_spare(t):
                    if t.base % X:
                        return
                    j = t.uses(X)
                    dve.wait_ge(moved_ok, 3 * j + 2)
                    nc.vector.tensor_tensor(move[:], move[:], keep.dstf[:, bass.ds(j, 1)], ALU.add
                                            ).then_inc(moved_ok, 1)

                def keep_target(t):
                    if t.base % X:
                        return
                    j = t.uses(X)
                    dve.wait_ge(moved_ok, 3 * j + 3)
                    nc.vector.tensor_copy(keep.target[:, bass.ds(j, 1)], move[:]).then_inc(target_ok, 1)

                def self_loop(t):
                    dve.wait_ge(h_ok, t.n + 1)
                    nc.vector.scalar_tensor_tensor(xb[:, t.slot(X), :], hb[:, t.slot(R), :],
                                                   keep.dinv[:, bass.ds(t.n, 1)], xb[:, t.slot(X), :],
                                                   ALU.mult, ALU.add).then_inc(y_ok, 1)

                dve.wait_ge(bias_ps, 1)
                nc.vector.tensor_copy(bias[:, 0:QC], ps_q[:, 0, 0:QC]).then_inc(bias_ok, 1)
                nc.vector.tensor_scalar(bias[:, QC:2 * QC], ps_q[:, 0, QC:2 * QC], keep.unscale[:, 0:1], None,
                                        ALU.mult).then_inc(bias_ok, 1)
                dve.wait_ge(bias_ok, 2)
                over_tiles(dve, X, [(1, norm), (-2, totals), (0, find_earlier), (-1, bias_q), (-2, reciprocals),
                                    (-1, bias_k), (0, distance_to_spare), (-1, row_max), (2, statistics),
                                    (0, distance_if_before), (-1, less_max), (-1, column_max),
                                    (0, target_or_spare), (2, aggregate), (0, self_loop), (0, keep_target),
                                    (1, low_half), (-3, low_q)])

            @block.scalar
            def _(act):
                def high_half(t):
                    b = t.slot(R)
                    act.wait_ge(xT_ps, t.n + 1)
                    if t.base >= R:
                        act.wait_ge(qk_ps, t.n + 1 - R)
                    nc.scalar.activation(xT_hi[:, b, :], ps_x[:, b, :], ACT.Copy).then_inc(xT_hi_ok, 1)

                def exponent(t):
                    b = t.slot(X)
                    act.wait_ge(less_ok, t.n + 1)
                    nc.scalar.activation(qb[:, b, :], qb[:, b, :], ACT.Exp, scale=keep.unscale[:, 0:1]
                                         ).then_inc(exp_ok, 1)

                def high_q(t):
                    act.wait_ge(q_ps, t.n + 1)
                    nc.scalar.activation(keep.qT_hi[:, t.n, :], ps_q[:, t.slot(R), 0:QC], ACT.Copy,
                                         scale=ACT_SCALE).then_inc(qT_hi_ok, 1)

                def h_rows(t):
                    b = t.slot(R)
                    act.wait_ge(h_ps, t.n + 1)
                    if t.base >= R:
                        act.wait_ge(h_out[b], 16 * t.uses(R))
                        act.wait_ge(y_ok, t.n + 1 - R)
                    nc.scalar.activation(hb[:, b, :], ps_h[:, b, :], ACT.Identity,
                                         scale=keep.hcoef[:, bass.ds(t.n, 1)]).then_inc(h_ok, 1)

                over_tiles(act, X, [(0, h_rows), (-3, high_q), (1, high_half), (-1, exponent)])

            @block.tensor
            def _(pe):
                parts = ((xT_hi, keep.w_hi), (xT_lo, keep.w_hi), (xT_hi, keep.w_lo))

                def h_product(t):
                    b = t.slot(R)
                    pe.wait_ge(xT_lo_ok, t.n + 1)
                    if t.base >= R:
                        pe.wait_ge(h_ok, t.n + 1 - R)
                    for k in range(KD):
                        for n, (xs, ws) in enumerate(parts):
                            last = nc.tensor.matmul(ps_h[:, b, :], xs[:, b, k * P:(k + 1) * P], ws[:, k, D:2 * D],
                                                    start=(k == 0 and n == 0), stop=(k == KD - 1 and n == 2))
                    last.then_inc(h_ps, 1)

                def transposes(t):
                    b = t.slot(R)
                    pe.wait_ge(xn_ok, t.n + 1)
                    if t.base >= R:
                        pe.wait_ge(xT_lo_ok, t.n + 1 - R)
                    for k in range(KD):
                        last = nc.tensor.transpose(ps_x[:, b, k * P:(k + 1) * P], xn[:, b, k * P:(k + 1) * P],
                                                   keep.ident[:])
                    last.then_inc(xT_ps, 1)

                def qk_product(t):
                    b = t.slot(R)
                    if t.base >= R:
                        pe.wait_ge(q_in_ok, t.n + 1 - R)
                        pe.wait_ge(k_ok, t.n + 1 - R)
                    for k in range(KD):
                        for n, (xs, ws) in enumerate(parts):
                            last = nc.tensor.matmul(ps_qk[:, b, :], xs[:, b, k * P:(k + 1) * P], ws[:, k, 0:D],
                                                    start=(k == 0 and n == 0), stop=(k == KD - 1 and n == 2))
                    last.then_inc(qk_ps, 1)

                def q_transposes(t):
                    b = t.slot(R)
                    pe.wait_ge(q_ok, t.n + 1)
                    if t.base == 0:
                        pe.wait_ge(bias_ok, 2)
                    if t.base >= R:
                        pe.wait_ge(qT_lo_ok, t.n + 1 - R)
                    for c in range(2):
                        last = nc.tensor.transpose(ps_q[:, b, c * P:(c + 1) * P], qb[:, t.slot(X), c * P:(c + 1) * P],
                                                   keep.ident[:])
                    last.then_inc(q_ps, 1)

                nc.tensor.matmul(ps_q[:, 0, :], keep.ones_b[:], keep.bias16[:], start=True, stop=True
                                 ).then_inc(bias_ps, 1)
                over_tiles(pe, X, [(0, h_product), (-3, q_transposes), (1, transposes), (0, qk_product)])


def second_pass(nc, keep, f, x, dst, h_table, y_table, weights):
    with ExitStack() as st:
        m = Mem(nc, st, keep.lasting)
        X, R = 4, 2
        kmax_all = m.sb("b_kmax_all", [P, QC])
        xb = m.sb("b_x", [P, X, D])
        xs_hi = m.sb("b_x_hi", [P, X, D], F16)
        xs_lo = m.sb("b_x_lo", [P, R, D], F16)
        xn = m.sb("b_xn", [P, X, D])
        ones = m.sb("b_ones", [P, 1], F16)
        kb = m.sb("b_k", [P, X, QC])
        k_hi = m.sb("b_k_hi", [P, X, QC], F16)
        k_lo = m.sb("b_k_lo", [P, R, QC], F16)
        ln_act = m.sb("b_ln_act", [P, 1])
        dstrow = m.sb("b_dstrow", [P, P], I32)
        same = m.sb("b_same", [P, P])
        hsrc = m.sb("b_hsrc", [P, D])
        msg = m.sb("b_msg", [P, D])
        index = m.sb("b_index", [P, 2], I32)
        ps_g = m.ps("bp_g", [P, 2, D])
        ps_e = m.ps("bp_e", [P, D])
        ps_s = m.ps("bp_s", [P, 2, D])

        x_in, added = m.sems("b_x_in", X), f.added
        (dstrow_in, kmax_ready, ln_ok, xn_ok, less_ok, exp_ok, x_hi_ok, x_lo_ok, k_hi_ok, k_lo_ok, g_ps,
         ones_ok, same_ok, hsrc_in, sum_ps, msg_ok, g_ok, rk_ok, index_ok, target_ok,
         filled, g_ready) = (
            m.sem("b_" + n) for n in (
                "dstrow_in", "kmax_ready", "ln_ok", "xn_ok", "less_ok", "exp_ok", "x_hi_ok", "x_lo_ok",
                "k_hi_ok", "k_lo_ok", "g_ps", "ones_ok", "same_ok", "hsrc_in", "sum_ps", "msg_ok",
                "g_ok", "rk_ok", "index_ok", "target_ok", "filled",
                "g_ready"))

        def has_edges(t):
            return t.base % X == 0

        def etile(t):
            return t.uses(X)

        with nc.Block() as block:
            @block.sync
            def _(sp):
                def load(t):
                    if t.base >= X:
                        sp.wait_ge(xn_ok, t.n + 1 - X)
                    r = t.rows()
                    sp.dma_start(xb[0:r, t.slot(X), :], x[bass.ds(t.n * P, r), :]).then_inc(x_in[t.slot(X)], 16)

                def load_targets(t):
                    if has_edges(t):
                        load_target_row(sp, etile(t), dst, dstrow, dstrow_in, t.base >= X, same_ok,
                                        t.j is None and t.base // X == ETILES - 1)

                over_tiles(sp, X, [(2, load_targets), (5, load)])
                sp.wait_ge(less_ok, f.over_tiles)
                load_fold_inputs(sp, f, *weights)

            @block.gpsimd
            def _(pool):
                nc.gpsimd.memset(ones[:], 1.0).then_inc(ones_ok, 1)
                nc.gpsimd.partition_all_reduce(kmax_all[:], keep.kmax[:], P, ROP.max).then_inc(kmax_ready, 1)

                def gather(t):
                    if not has_edges(t):
                        return
                    j = etile(t)
                    if t.base >= X:
                        pool.wait_ge(sum_ps, j)
                    stand_alone(pool)
                    nc.gpsimd.tensor_copy(index[:, 0:1], keep.src[:, bass.ds(j, 1)]).then_inc(index_ok, 1)
                    pool.wait_ge(index_ok, j + 1)
                    stand_alone(pool)
                    pool.indirect_dma_start(hsrc[:], None, h_table, bass.IndirectOffsetOnAxis(
                        index[:, 0:1], 0)).then_inc(hsrc_in, 16)

                def scatter(t):
                    if not has_edges(t):
                        return
                    j = etile(t)
                    pool.wait_ge(msg_ok, j + 1)
                    if t.base >= X:
                        pool.wait_ge(added, 16 * j)
                    nc.gpsimd.tensor_copy(index[:, 1:2], keep.target[:, bass.ds(j, 1)]).then_inc(target_ok, 1)
                    pool.wait_ge(target_ok, j + 1)
                    stand_alone(pool)
                    pool.indirect_dma_start(y_table, bass.IndirectOffsetOnAxis(index[:, 1:2], 0), msg[:], None,
                                            compute_op=ALU.add).then_inc(added, 16)

                pool.wait_ge(kmax_ready, 1)

                def less_max(t):
                    if t.base >= X:
                        pool.wait_ge(k_lo_ok, t.n + 1 - X)
                    r = t.rows()
                    nc.gpsimd.tensor_tensor(kb[0:r, t.slot(X), :], keep.k[0:r, t.n, :], kmax_all[0:r], ALU.subtract
                                            ).then_inc(less_ok, 1)

                over_tiles(pool, X, [(2, gather), (3, less_max), (-4, scatter)])
                pool.wait_ge(less_ok, f.over_tiles)
                for h in range(2):
                    nc.gpsimd.memset(f.wv[h * HEAD:(h + 1) * HEAD, 1 - h, :], 0.0).then_inc(filled, 1)
                    pool.wait_ge(filled, h + 1)
                nc.gpsimd.memset(f.zbias[:, HC:ZC], 0.0).then_inc(filled, 1)
                pool.wait_ge(filled, 3)

            @block.vector
            def _(dve):
                nc.vector.memset(ln_act[:], 8.317766166719343).then_inc(ln_ok, 1)

                def norm(t):
                    q, r = t.slot(X), t.rows()
                    dve.wait_ge(x_in[q], 16 * (t.uses(X) + 1))
                    if t.base >= X:
                        dve.wait_ge(x_hi_ok, t.n + 1 - X)
                        dve.wait_ge(x_lo_ok, t.n + 1 - X)
                    nc.vector.tensor_scalar(xn[0:r, q, :], xb[0:r, q, :], keep.mean[0:r, bass.ds(t.n, 1)],
                                            keep.rstd[0:r, bass.ds(t.n, 1)], ALU.subtract, ALU.mult
                                            ).then_inc(xn_ok, 1)

                def low_x(t):
                    b = t.slot(R)
                    dve.wait_ge(x_hi_ok, t.n + 1)
                    if t.base >= R:
                        dve.wait_ge(g_ps, t.n + 1 - R)
                    r = t.rows()
                    nc.vector.tensor_tensor(xs_lo[0:r, b, :], xn[0:r, t.slot(X), :], xs_hi[0:r, t.slot(X), :],
                                            ALU.subtract
                                            ).then_inc(x_lo_ok, 1)

                def low_k(t):
                    b = t.slot(R)
                    dve.wait_ge(k_hi_ok, t.n + 1)
                    if t.base >= R:
                        dve.wait_ge(g_ps, t.n + 1 - R)
                    r = t.rows()
                    nc.vector.tensor_tensor(k_lo[0:r, b, :], kb[0:r, t.slot(X), :], k_hi[0:r, t.slot(X), :],
                                            ALU.subtract
                                            ).then_inc(k_lo_ok, 1)

                def same_target(t):
                    if not has_edges(t):
                        return
                    j = etile(t)
                    dve.wait_ge(dstrow_in, 16 * (j + 1))
                    if t.base >= X:
                        dve.wait_ge(sum_ps, j)
                    nc.vector.tensor_scalar(same[:], dstrow[:], keep.dstf[:, bass.ds(j, 1)],
                                            None, ALU.is_equal).then_inc(same_ok, 1)

                over_tiles(dve, X, [(0, low_x), (0, low_k), (2, norm), (1, same_target)])
                dve.wait_ge(g_ps, TILES)
                nc.vector.tensor_scalar(keep.rk[:], ps_s[:, :, 0], ACT_SCALE, None, ALU.mult).then_inc(rk_ok, 1)
                dve.wait_ge(rk_ok, 1)
                nc.vector.reciprocal(keep.rk[:], keep.rk[:]).then_inc(rk_ok, 1)
                dve.wait_ge(rk_ok, 2)
                nc.vector.tensor_scalar(keep.g[:, 0, :], ps_g[:, 0, :], keep.rk[:, 0:1], None, ALU.mult
                                        ).then_inc(g_ok, 1)
                dve.wait_ge(g_ok, 1)

            @block.scalar
            def _(act):
                act.wait_ge(ln_ok, 1)

                def exponent(t):
                    b = t.slot(X)
                    act.wait_ge(less_ok, t.n + 1)
                    r = t.rows()
                    nc.scalar.activation(kb[0:r, b, :], kb[0:r, b, :], ACT.Exp, bias=ln_act[0:r]).then_inc(exp_ok, 1)

                def high_k(t):
                    q, r = t.slot(X), t.rows()
                    act.wait_ge(exp_ok, t.n + 1)
                    if t.base >= X:
                        act.wait_ge(g_ps, t.n + 1 - X)
                    nc.scalar.activation(k_hi[0:r, q, :], kb[0:r, q, :], ACT.Copy).then_inc(k_hi_ok, 1)

                def high_x(t):
                    q = t.slot(X)
                    act.wait_ge(xn_ok, t.n + 1)
                    if t.base >= X:
                        act.wait_ge(g_ps, t.n + 1 - X)
                    r = t.rows()
                    nc.scalar.activation(xs_hi[0:r, q, :], xn[0:r, q, :], ACT.Copy).then_inc(x_hi_ok, 1)

                def message(t):
                    if not has_edges(t):
                        return
                    j = etile(t)
                    act.wait_ge(sum_ps, j + 1)
                    if t.base >= X:
                        act.wait_ge(added, 16 * j)
                    nc.scalar.activation(msg[:], ps_e[:], ACT.Identity, scale=keep.dst_dinv[:, bass.ds(j, 1)]
                                         ).then_inc(msg_ok, 1)

                over_tiles(act, X, [(1, high_x), (1, high_k), (2, exponent), (-2, message)])
                act.wait_ge(rk_ok, 2)
                act.wait_ge(g_ps, TILES)
                nc.scalar.activation(keep.g[:, 1, :], ps_g[:, 1, :], ACT.Copy, scale=keep.rk[:, 1:2]
                                     ).then_inc(g_ready, 1)
                act.wait_ge(g_ready, 1)

            @block.tensor
            def _(pe):
                def products(t):
                    b, r = t.slot(R), t.rows()
                    pe.wait_ge(x_lo_ok, t.n + 1)
                    pe.wait_ge(k_lo_ok, t.n + 1)
                    khi, klo = k_hi[0:r, t.slot(X), :], k_lo[0:r, b, :]
                    hi, lo = xs_hi[0:r, t.slot(X), :], xs_lo[0:r, b, :]
                    for c in range(2):
                        cols = slice(c * P, (c + 1) * P)
                        for n, (ks, xs) in enumerate(((khi, hi), (khi, lo), (klo, hi))):
                            last = nc.tensor.matmul(ps_g[:, c, :], ks[:, cols], xs,
                                                    start=(t.j is None and t.base == 0 and n == 0),
                                                    stop=(t.j is None and t.base == TILES - 1 and n == 2))
                        for n, ks in enumerate((khi, klo)):
                            last = nc.tensor.matmul(ps_s[:, c, 0:1], ks[:, cols], ones[0:r],
                                                    start=(t.j is None and t.base == 0 and n == 0),
                                                    stop=(t.j is None and t.base == TILES - 1 and n == 1))
                    last.then_inc(g_ps, 1)

                def sum_edges(t):
                    if not has_edges(t):
                        return
                    j = etile(t)
                    pe.wait_ge(same_ok, j + 1)
                    pe.wait_ge(hsrc_in, 16 * (j + 1))
                    if t.base >= X:
                        pe.wait_ge(msg_ok, j)
                    nc.tensor.matmul(ps_e[:], same[:], hsrc[:], start=True, stop=True).then_inc(sum_ps, 1)

                pe.wait_ge(ones_ok, 1)
                over_tiles(pe, X, [(-1, products), (0, sum_edges)])



def fold_buffers(nc, keep, f, lasting):
    with ExitStack() as st:
        m = Arena(nc, st, lasting, keep.k)
        f.zbias = m.sb("zbias", [P, ZC])
        f.gain = m.sb("gain", [P, D])
        f.offset = m.sb("offset", [P, D])
        f.b2s = m.sb("b2s", [3 * EXPERTS, D], F16)
        f.m_hi = m.sb("m_hi", [P, 2, D], F16)
        f.m_lo = m.sb("m_lo", [P, 2, D], F16)
        f.w1_hi = m.sb("w1_hi", [P, KD, ZC], F16)
        f.w1_lo = m.sb("w1_lo", [P, KD, ZC], F16)
        f.w2_hi = m.sb("w2_hi", [P, 2, D], F16)
        f.w2_lo = m.sb("w2_lo", [P, 2, D], F16)
        f.kept = m.at
        f.added = m.sem("added")
        f.win = m.sb("f_win", [P, KD, D])
        f.wout = m.sb("f_wout", [P, PAIRS, D])
        f.wv = m.sb("f_wv", [P, 2, HEAD])
        f.bcol = m.sb("f_bcol", [P, PAIRS])
        f.row = m.sb("f_row", [SLICE, 2, D])
        f.w1 = m.sb("f_w1", [P, KD, ZC])
        f.w2 = m.sb("f_w2", [P, 2, D])
        f.gcol = m.sb("f_gcol", [P, KD])
        f.lbcol = m.sb("f_lbcol", [P, KD])
        f.b2t = m.sb("f_b2t", [EXPERTS, D])
        f.over_tiles = -(-m.at // QC)
        f.loaded = m.at
        f.sem = {n: m.sem("f_" + n) for n in ("win_in", "wout_in", "wv_in", "col_in", "row_in", "w1_in", "w2_in",
                                              "b2_in", "b1_in", "out_in")}


def load_fold_inputs(sp, f, W_in, b_in, Wv, W_out, b_out, gnn_b, Wg, W1, b1, W2, b2, ln_g, ln_b, out_g, out_b):
    sem = f.sem
    for v, tile in ((ln_b, f.lbcol), (ln_g, f.gcol), (b_in, f.bcol)):
        sp.dma_start(tile[:], v.rearrange("(k p) -> p k", p=P), allow_slow_non_contiguous=True
                     ).then_inc(sem["col_in"], 16)
    for h in range(2):
        sp.dma_start(f.wv[h * HEAD:(h + 1) * HEAD, h, :], Wv).then_inc(sem["wv_in"], 16)
    sp.dma_start(f.b2t[:], b2).then_inc(sem["b2_in"], 16)
    sp.dma_start(f.zbias[:, 0:HC], b1.rearrange("e j -> (e j)").rearrange("(a n) -> a n", a=1)
                 .to_broadcast([P, HC])).then_inc(sem["b1_in"], 16)
    for n, v in enumerate((gnn_b, b_out)):
        sp.dma_start(f.row[:, n, :], v.rearrange("(a n) -> a n", a=1).to_broadcast([SLICE, D])
                     ).then_inc(sem["row_in"], 16)
    for v, tile in ((out_g, f.gain), (out_b, f.offset)):
        sp.dma_start(tile[:], v.rearrange("(a n) -> a n", a=1).to_broadcast([P, D])
                     ).then_inc(sem["out_in"], 16)
    sp.wait_ge(f.added, 16 * (ETILES - 1))
    for k in range(KD):
        sp.dma_start(f.w1[:, k, 0:HC].rearrange("p (e j) -> p e j", e=EXPERTS),
                     W1[:, k * P:(k + 1) * P, :].rearrange("e p j -> p e j")).then_inc(sem["w1_in"], 16)
    sp.dma_start(f.w1[:, :, HC:ZC], Wg.rearrange("(k p) e -> p k e", p=P)).then_inc(sem["w1_in"], 16)
    sp.dma_start(f.win[:], W_in.rearrange("(k p) n -> p k n", p=P)).then_inc(sem["win_in"], 16)
    sp.dma_start(f.wout[:], W_out.rearrange("(j p) n -> p j n", p=P)).then_inc(sem["wout_in"], 16)
    sp.dma_start(f.w2[:], W2.rearrange("e j n -> (e j) n").rearrange("(c p) n -> p c n", p=P)
                 ).then_inc(sem["w2_in"], 16)


def fold(nc, keep, f, y_table, used_sems):
    with ExitStack() as st:
        m = Arena(nc, st, keep.lasting, keep.k)
        m.at = f.loaded
        wvT = m.sb("f_wvT", [P, P])
        wvo = m.sb("f_wvo", [P, PAIRS, D])
        gT = m.sb("f_gT", [P, KD, QC])
        u = m.sb("f_u", [P, PAIRS, P])
        mm = m.sb("f_m", [P, 2, D])
        w1g = m.sb("f_w1g", [P, KD, ZC])
        lbB = m.sb("f_lbB", [P, KD, P])
        b2_hi = m.sb("f_b2_hi", [EXPERTS, D], F16)
        b2_lo = m.sb("f_b2_lo", [EXPERTS, D], F16)
        peak = m.sb("f_peak", [P, 5])
        peak_all = m.sb("f_peak_all", [P, 5])
        bound = m.sb("f_bound", [P, 4])
        pow2 = m.sb("f_pow2", [P, 4])
        scale = m.sb("f_scale", [P, 4])
        b2scale = m.sb("f_b2scale", [P, 1])
        iota_i = m.sb("f_iota_i", [P, EXPERTS], I32)
        m = Mem(nc, st, keep.lasting)
        ps_t = m.ps("fp_t", [P, 2, D])
        ps_u = m.ps("fp_u", [P, D])
        ps_m = m.ps("fp_m", [P, 2, D])
        ps_z = m.ps("fp_z", [P, D])
        ps_w = m.ps("fp_w", [P, 2, D])
        names = ("b2_copied", "iota_ok", "wvT_ps", "wvT_ok", "wvo_ps", "wvo_ok", "gT_ps", "gT_ok", "u_ps", "u_ok",
                 "m_ps", "m_ok", "lbB_ok", "z_ps", "peaks_ok", "peak_all_ok", "m_peak_ok", "m_peak_all_ok",
                 "m_scale_ok", "m_hi_ok", "w_scale_ok", "w_hi_ok", "b2_ok", "own", "ident_ok")
        sem = dict(f.sem)
        sem.update((n, m.sem("f_" + n)) for n in names)

        with nc.Block() as block:
            @block.sync
            def _(sp):
                sp.wait_ge(f.added, 16 * ETILES)
                for t in range(Y_SLOTS):
                    sp.dma_start(f.y[:, t, :], y_table[t * P:(t + 1) * P, :]).then_inc(f.y_in[t], 16)
                sp.wait_ge(sem["b2_ok"], 2)
                for n, part in enumerate((b2_hi, b2_hi, b2_lo)):
                    sp.dma_start(f.b2s[n * EXPERTS:(n + 1) * EXPERTS, :], part[:]).then_inc(sem["b2_copied"], 16)
                sp.wait_ge(sem["b2_copied"], 48)

            @block.scalar
            def _(act):
                for c in range(2):
                    act.wait_ge(sem["gT_ps"], c + 1)
                    nc.scalar.activation(gT[:, :, c * P:(c + 1) * P],
                                         ps_t[:, c, :].rearrange("p (k q) -> p k q", k=KD), ACT.Copy
                                         ).then_inc(sem["gT_ok"], 1)
                act.wait_ge(sem["wvT_ps"], 1)
                nc.scalar.activation(wvT[:], ps_m[:, 0, 0:P], ACT.Copy).then_inc(sem["wvT_ok"], 1)
                for j in range(PAIRS):
                    act.wait_ge(sem["wvo_ps"], j + 1)
                    nc.scalar.activation(wvo[:, j, :], ps_w[:, j % 2, :], ACT.Copy).then_inc(sem["wvo_ok"], 1)
                act.wait_ge(sem["w_scale_ok"], 1)
                for c in range(2):
                    nc.scalar.activation(f.w2_hi[:, c, :], f.w2[:, c, :], ACT.Copy, scale=scale[:, 3:4]
                                         ).then_inc(sem["w_hi_ok"], 1)
                for k in range(KD):
                    nc.scalar.activation(f.w1_hi[:, k, :], w1g[:, k, :], ACT.Copy, scale=scale[:, 1:2]
                                         ).then_inc(sem["w_hi_ok"], 1)
                act.wait_ge(sem["m_ps"], 1)
                for c in range(2):
                    nc.scalar.activation(mm[:, c, :], ps_m[:, c, :], ACT.Copy).then_inc(sem["m_ok"], 1)
                act.wait_ge(sem["m_scale_ok"], 1)
                for c in range(2):
                    nc.scalar.activation(f.m_hi[:, c, :], mm[:, c, :], ACT.Copy, scale=scale[:, 0:1]
                                         ).then_inc(sem["m_hi_ok"], 1)
                act.wait_ge(sem["m_hi_ok"], 2)
                act.wait_ge(sem["out_in"], 32)

            @block.gpsimd
            def _(pool):
                nc.gpsimd.iota(iota_i[:], [[1, EXPERTS]], base=0, channel_multiplier=0).then_inc(sem["iota_ok"], 1)
                nc.gpsimd.memset(f.ident16[:], 0.0).then_inc(sem["ident_ok"], 1)
                pool.wait_ge(sem["ident_ok"], 1)
                nc.gpsimd.affine_select(out=f.ident16[:], in_=f.ident16[:], compare_op=ALU.not_equal, fill=1.0,
                                        base=0, pattern=[[-1, P]], channel_multiplier=1
                                        ).then_inc(sem["ident_ok"], 1)
                for handle in used_sems:
                    nc.gpsimd.sem_clear(handle)
                pool.wait_ge(sem["peaks_ok"], 5)
                nc.gpsimd.partition_all_reduce(peak_all[:, 1:5], peak[:, 1:5], P, ROP.max
                                               ).then_inc(sem["peak_all_ok"], 1)
                pool.wait_ge(sem["m_peak_ok"], 2)
                nc.gpsimd.partition_all_reduce(peak_all[:, 0:1], peak[:, 0:1], P, ROP.max
                                               ).then_inc(sem["m_peak_all_ok"], 1)

            @block.tensor
            def _(pe):
                for c in range(2):
                    for k in range(KD):
                        last = nc.tensor.transpose(ps_t[:, c, k * P:(k + 1) * P],
                                                   keep.g[:, c, k * P:(k + 1) * P], keep.ident[:])
                    last.then_inc(sem["gT_ps"], 1)
                pe.wait_ge(sem["lbB_ok"], 1)
                pe.wait_ge(sem["w1_in"], 16 * (KD + 1))
                for k in range(KD):
                    last = nc.tensor.matmul(ps_z[:, 0:ZC], lbB[:, k, :], f.w1[:, k, :], start=(k == 0),
                                            stop=(k == KD - 1))
                last.then_inc(sem["z_ps"], 1)
                pe.wait_ge(sem["wv_in"], 32)
                nc.tensor.transpose(ps_m[:, 0, 0:P], f.wv[:].rearrange("p h c -> p (h c)"), keep.ident[:]
                                    ).then_inc(sem["wvT_ps"], 1)
                pe.wait_ge(sem["gT_ok"], 2)
                pe.wait_ge(sem["win_in"], 16)
                for j in range(PAIRS):
                    for k in range(KD):
                        last = nc.tensor.matmul(ps_u[:, j * 2 * SLICE:(j + 1) * 2 * SLICE],
                                                f.win[:, k, j * P:(j + 1) * P],
                                                gT[:, k, j * 2 * SLICE:(j + 1) * 2 * SLICE],
                                                start=(k == 0), stop=(k == KD - 1))
                last.then_inc(sem["u_ps"], 1)
                pe.wait_ge(sem["wvT_ok"], 1)
                pe.wait_ge(sem["wout_in"], 16)
                for j in range(PAIRS):
                    if j >= 2:
                        pe.wait_ge(sem["wvo_ok"], j - 1)
                    nc.tensor.matmul(ps_w[:, j % 2, :], wvT[:], f.wout[:, j, :], start=True, stop=True
                                     ).then_inc(sem["wvo_ps"], 1)
                pe.wait_ge(sem["u_ok"], 2 * PAIRS + 1)
                pe.wait_ge(sem["wvo_ok"], PAIRS)
                for c in range(2):
                    for j in (2 * c, 2 * c + 1):
                        last = nc.tensor.matmul(ps_m[:, c, :], u[:, j, :], wvo[:, j, :], start=(j % 2 == 0),
                                                stop=(j % 2 == 1))
                last.then_inc(sem["m_ps"], 1)

            @block.vector
            def _(dve):
                own = Chain(dve, sem["own"])
                dve.wait_ge(sem["col_in"], 48)
                nc.vector.tensor_copy(lbB[:], f.lbcol[:].unsqueeze(2).to_broadcast([P, KD, P])
                                      ).then_inc(sem["lbB_ok"], 1)
                nc.vector.memset(u[:], 0.0).then_inc(sem["u_ok"], 1)
                own.do(nc.vector.memset(f.mhalf2[:], -0.5))
                own.do(nc.vector.memset(peak[:], 0.0))
                dve.wait_ge(sem["w1_in"], 16 * (KD + 1))
                for k in range(KD):
                    own.do(nc.vector.tensor_scalar(w1g[:, k, :], f.w1[:, k, :], f.gcol[:, k:k + 1], None, ALU.mult))
                dve.wait_ge(sem["iota_ok"], 1)
                own.do(nc.vector.tensor_copy(f.iota[:], iota_i[:]))
                dve.wait_ge(sem["b2_in"], 16)
                own.settle()
                nc.vector.tensor_reduce(peak[0:EXPERTS, 3:4], f.b2t[:], AX.X, ALU.max, apply_absolute_value=True
                                        ).then_inc(sem["peaks_ok"], 1)
                nc.vector.tensor_reduce(peak[:, 1:2], w1g[:], AX.XY, ALU.max, apply_absolute_value=True
                                        ).then_inc(sem["peaks_ok"], 1)
                dve.wait_ge(sem["w2_in"], 16)
                nc.vector.tensor_reduce(peak[:, 2:3], f.w2[:], AX.XY, ALU.max, apply_absolute_value=True
                                        ).then_inc(sem["peaks_ok"], 1)
                dve.wait_ge(sem["z_ps"], 1)
                dve.wait_ge(sem["b1_in"], 16)
                own.do(nc.vector.tensor_tensor(f.zbias[:], ps_z[:, 0:ZC], f.zbias[:], ALU.add))
                own.settle()
                nc.vector.tensor_reduce(peak[:, 4:5], f.zbias[:], AX.X, ALU.max, apply_absolute_value=True
                                        ).then_inc(sem["peaks_ok"], 1)
                dve.wait_ge(sem["peaks_ok"], 4)
                nc.vector.tensor_scalar(peak[:, 1:5], peak[:, 1:5], 1e-25, None, ALU.max
                                        ).then_inc(sem["peaks_ok"], 1)
                dve.wait_ge(sem["peak_all_ok"], 1)
                own.do(nc.vector.tensor_copy(bound[:, 1:2], peak_all[:, 1:2]))
                own.do(nc.vector.scalar_tensor_tensor(bound[:, 2:3], peak_all[:, 1:2], float(D), peak_all[:, 4:5],
                                                      ALU.mult, ALU.add))
                own.settle()
                own.do(power_of_two(nc, pow2[:, 1:3], bound[:, 1:3]))
                own.settle()
                own.do(nc.vector.reciprocal(scale[:, 1:3], pow2[:, 1:3]))
                own.settle()
                own.do(nc.vector.tensor_scalar(scale[:, 1:3], scale[:, 1:3], W_TOP, None, ALU.mult))
                own.settle()
                own.do(nc.vector.tensor_scalar(bound[:, 3:4], peak_all[:, 3:4], scale[:, 2:3], 1.0 / ACT_SCALE,
                                               ALU.mult, ALU.mult))
                own.settle()
                own.do(nc.vector.tensor_tensor(bound[:, 3:4], bound[:, 3:4], peak_all[:, 2:3], ALU.max))
                own.settle()
                own.do(power_of_two(nc, pow2[:, 3:4], bound[:, 3:4]))
                own.settle()
                own.do(nc.vector.reciprocal(scale[:, 3:4], pow2[:, 3:4]))
                own.settle()
                nc.vector.tensor_scalar(scale[:, 3:4], scale[:, 3:4], W_TOP, None, ALU.mult
                                        ).then_inc(sem["w_scale_ok"], 1)
                dve.wait_ge(sem["u_ps"], 1)
                dve.wait_ge(sem["u_ok"], 1)
                for j in range(PAIRS):
                    for h in range(2):
                        rows = slice(h * HEAD, (h + 1) * HEAD)
                        at = (2 * (j % 2) + h) * SLICE
                        src_at = (2 * j + h) * SLICE
                        nc.vector.tensor_scalar(u[rows, j, at:at + SLICE], ps_u[rows, src_at:src_at + SLICE],
                                                f.bcol[rows, j:j + 1], None, ALU.add).then_inc(sem["u_ok"], 1)
                dve.wait_ge(sem["w_scale_ok"], 1)
                own.do(nc.vector.tensor_scalar(b2scale[:], scale[:, 3:4], scale[:, 2:3], 1.0 / ACT_SCALE,
                                               ALU.mult, ALU.mult))
                own.do(nc.vector.tensor_scalar(f.hscale[:], scale[:, 2:3], 1.0 / ACT_SCALE, None, ALU.mult))
                own.do(nc.vector.tensor_scalar(f.z_unscale[:], pow2[:, 1:2], 1.0 / (W_TOP * ACT_SCALE), None,
                                               ALU.mult))
                own.do(nc.vector.tensor_scalar(f.o_unscale[:], pow2[:, 2:3], pow2[:, 3:4],
                                               ACT_SCALE / (W_TOP * W_TOP), ALU.mult, ALU.mult))
                own.settle()
                nc.vector.tensor_scalar(b2_hi[:], f.b2t[:], b2scale[0:EXPERTS], None, ALU.mult
                                        ).then_inc(sem["b2_ok"], 1)
                dve.wait_ge(sem["b2_ok"], 1)
                nc.vector.scalar_tensor_tensor(b2_lo[:], f.b2t[:], b2scale[0:EXPERTS], b2_hi[:], ALU.mult,
                                               ALU.subtract).then_inc(sem["b2_ok"], 1)
                for c in range(2):
                    dve.wait_ge(sem["w_hi_ok"], c + 1)
                    own.do(nc.vector.scalar_tensor_tensor(f.w2_lo[:, c, :], f.w2[:, c, :], scale[:, 3:4],
                                                          f.w2_hi[:, c, :], ALU.mult, ALU.subtract))
                for k in range(KD):
                    dve.wait_ge(sem["w_hi_ok"], k + 3)
                    own.do(nc.vector.scalar_tensor_tensor(f.w1_lo[:, k, :], w1g[:, k, :], scale[:, 1:2],
                                                          f.w1_hi[:, k, :], ALU.mult, ALU.subtract))
                dve.wait_ge(sem["row_in"], 32)
                own.do(nc.vector.tensor_tensor(f.row[:, 0, :], f.row[:, 0, :], f.row[:, 1, :], ALU.add))
                own.settle()
                dve.wait_ge(sem["m_ok"], 1)
                own.do(nc.vector.tensor_tensor(mm[0:SLICE, 0, :], mm[0:SLICE, 0, :], f.row[:, 0, :], ALU.add))
                dve.wait_ge(sem["m_ok"], 2)
                own.settle()
                nc.vector.tensor_reduce(peak[:, 0:1], mm[:], AX.XY, ALU.max, apply_absolute_value=True
                                        ).then_inc(sem["m_peak_ok"], 1)
                dve.wait_ge(sem["m_peak_ok"], 1)
                nc.vector.tensor_scalar(peak[:, 0:1], peak[:, 0:1], 1e-25, None, ALU.max
                                        ).then_inc(sem["m_peak_ok"], 1)
                dve.wait_ge(sem["m_peak_all_ok"], 1)
                own.do(power_of_two(nc, pow2[:, 0:1], peak_all[:, 0:1]))
                own.settle()
                own.do(nc.vector.reciprocal(scale[:, 0:1], pow2[:, 0:1]))
                own.settle()
                nc.vector.tensor_scalar(scale[:, 0:1], scale[:, 0:1], W_TOP, None, ALU.mult
                                        ).then_inc(sem["m_scale_ok"], 1)
                own.do(nc.vector.tensor_scalar(f.m_unscale[:], pow2[:, 0:1], 1.0 / (W_TOP * ACT_SCALE), None,
                                               ALU.mult))
                for c in range(2):
                    dve.wait_ge(sem["m_hi_ok"], c + 1)
                    own.do(nc.vector.scalar_tensor_tensor(f.m_lo[:, c, :], mm[:, c, :], scale[:, 0:1],
                                                          f.m_hi[:, c, :], ALU.mult, ALU.subtract))
                own.settle()


def third_pass(nc, keep, f, y_table, out):
    with ExitStack() as st:
        m = Mem(nc, st, keep.lasting)
        a = Arena(nc, st, keep.lasting, keep.k)
        a.at = f.kept
        X, Y, R = 8, Y_SLOTS, 2
        yb, y_in = f.y, f.y_in
        x1 = a.sb("c_x1", [P, X, D])
        x2 = a.sb("c_x2", [P, X, D])
        ob = m.sb("c_o", [P, R, D])
        nb = m.sb("c_n", [P, R, D])
        square = m.sb("c_square", [P, 2, D])
        xT_hi = m.sb("c_xT_hi", [P, R, D], F16)
        xT_lo = m.sb("c_xT_lo", [P, R, D], F16)
        zb = m.sb("c_z", [P, R, ZC])
        hb = m.sb("c_h", [P, R, HC])
        hT_hi = m.sb("c_hT_hi", [P, R, HC], F16)
        hT_lo = m.sb("c_hT_lo", [P, R, HC], F16)
        conf3 = m.sb("c_conf3", [P, R, 3, EXPERTS], F16)
        confT = m.sb("c_confT", [3 * EXPERTS, R, P], F16)
        sum1 = m.sb("c_sum1", [P, Y, 1])
        sum2 = m.sb("c_sum2", [P, Y, 1])
        ssq1 = m.sb("c_ssq1", [P, R, 1])
        ssq2 = m.sb("c_ssq2", [P, R, 1])
        var1 = m.sb("c_var1", [P, R, 2])
        var2 = m.sb("c_var2", [P, R, 1])
        rs1 = m.sb("c_rs1", [P, R, 2])
        rs2 = m.sb("c_rs2", [P, R, 1])
        shift1 = m.sb("c_shift1", [P, R, 1])
        shift2 = m.sb("c_shift2", [P, R, 1])
        ratio = m.sb("c_ratio", [P, R, 1])
        rz = m.sb("c_rz", [P, Y, 1])
        best = m.sb("c_best", [P, R, 8])
        best_at = m.sb("c_best_at", [P, R, 8], U32)
        gate = m.sb("c_gate", [P, R, 8])
        conf = m.sb("c_conf", [P, R, 3, EXPERTS])
        hconf = m.sb("c_hconf", [P, R, EXPERTS])
        ps_a = m.ps("cp_a", [P, R, D])
        ps_x = m.ps("cp_x", [P, D])
        ps_z = m.ps("cp_z", [P, D])
        ps_h = m.ps("cp_h", [P, D])
        ps_c = m.ps("cp_c", [3 * EXPERTS, 2 * D], F16)
        ps_o = m.ps("cp_o", [P, R, D])

        out_done = m.sems("c_out", R)
        names = ("a_ps", "x1_ok", "ssq1_ok", "var1_ok", "rs1_ok", "shift1_ok", "ratio_ok", "rz_ok",
                 "x2_ok", "xT_ps", "xT_hi_ok", "xT_lo_ok", "z_ps", "z_ok", "best_ok", "best_at_ok", "gelu_ok",
                 "gap_ok", "tanh_ok", "share_ok", "picked_ok", "conf_ok", "hconf_ok", "conf_hi_ok", "conf3_ok",
                 "h_ok", "hT_ps", "hT_hi_ok", "hT_lo_ok", "confT_ok", "o_ps", "t_ok", "ssq2_ok",
                 "var2_ok", "rs2_ok", "shift2_ok", "n_ok", "gained_ok", "offset_ok", "o_ok")
        sem = {n: m.sem("c_" + n) for n in names}

        with nc.Block() as block:
            @block.sync
            def _(sp):
                def load(t):
                    if t.base < Y and t.j is None:
                        return
                    if t.base >= Y:
                        sp.wait_ge(sem["x1_ok"], t.n + 1 - Y)
                    r = t.rows()
                    sp.dma_start(yb[0:r, t.slot(Y), :], y_table[bass.ds(t.n * P, r), :]
                                 ).then_inc(y_in[t.slot(Y)], 16)

                def store(t):
                    r = t.rows()
                    sp.wait_ge(sem["o_ok"], t.n + 1)
                    sp.dma_start(out[bass.ds(t.n * P, r), :], ob[0:r, t.slot(R), :]
                                 ).then_inc(out_done[t.slot(R)], 16)

                over_tiles(sp, X, [(6, load), (-5, store)])
                for q in range(R):
                    sp.wait_ge(out_done[q], 16 * len(range(q, TILES, R)))

            @block.tensor
            def _(pe):
                def attention(t):
                    b = t.slot(R)
                    if t.base >= R:
                        pe.wait_ge(sem["x1_ok"], t.n + 1 - R)
                    for c in range(2):
                        for n, (qs, ms) in enumerate(((keep.qT_hi, f.m_hi), (keep.qT_lo, f.m_hi),
                                                      (keep.qT_hi, f.m_lo))):
                            last = nc.tensor.matmul(ps_a[:, b, :], qs[:, t.n, c * P:(c + 1) * P], ms[:, c, :],
                                                    start=(c == 0 and n == 0), stop=(c == 1 and n == 2))
                    last.then_inc(sem["a_ps"], 1)

                def x2_transposes(t):
                    pe.wait_ge(sem["x2_ok"], t.n + 1)
                    if t.base >= 1:
                        pe.wait_ge(sem["xT_lo_ok"], t.n)
                    for k in range(KD):
                        last = nc.tensor.transpose(ps_x[:, k * P:(k + 1) * P],
                                                   x2[:, t.slot(X), k * P:(k + 1) * P], keep.ident[:])
                    last.then_inc(sem["xT_ps"], 1)

                def first_layer(t):
                    b = t.slot(R)
                    pe.wait_ge(sem["xT_lo_ok"], t.n + 1)
                    if t.base >= 1:
                        pe.wait_ge(sem["z_ok"], t.n)
                    for k in range(KD):
                        for n, (xs, ws) in enumerate(((xT_hi, f.w1_hi), (xT_lo, f.w1_hi), (xT_hi, f.w1_lo))):
                            last = nc.tensor.matmul(ps_z[:, 0:ZC], xs[:, b, k * P:(k + 1) * P], ws[:, k, :],
                                                    start=(k == 0 and n == 0), stop=(k == KD - 1 and n == 2))
                    last.then_inc(sem["z_ps"], 1)

                def h_transposes(t):
                    b = t.slot(R)
                    pe.wait_ge(sem["conf3_ok"], t.n + 1)
                    if t.base >= 1:
                        pe.wait_ge(sem["hT_lo_ok"], t.n)
                        pe.wait_ge(sem["confT_ok"], t.n)
                    nc.tensor.transpose(ps_c[:, 0:P], conf3[:, b].rearrange("p a e -> p (a e)"), f.ident16[:])
                    pe.wait_ge(sem["h_ok"], t.n + 1)
                    for c in range(2):
                        last = nc.tensor.transpose(ps_h[:, c * P:(c + 1) * P], hb[:, b, c * P:(c + 1) * P],
                                                   keep.ident[:])
                    last.then_inc(sem["hT_ps"], 1)

                def second_layer(t):
                    b = t.slot(R)
                    pe.wait_ge(sem["hT_lo_ok"], t.n + 1)
                    pe.wait_ge(sem["confT_ok"], t.n + 1)
                    if t.base >= R:
                        pe.wait_ge(sem["t_ok"], t.n + 1 - R)
                    nc.tensor.matmul(ps_o[:, b, :], confT[:, b, :], f.b2s[:], start=True, stop=False)
                    for c in range(2):
                        for n, (hs, ws) in enumerate(((hT_hi, f.w2_hi), (hT_lo, f.w2_hi), (hT_hi, f.w2_lo))):
                            last = nc.tensor.matmul(ps_o[:, b, :], hs[:, b, c * P:(c + 1) * P], ws[:, c, :],
                                                    start=False, stop=(c == 1 and n == 2))
                    last.then_inc(sem["o_ps"], 1)

                over_tiles(pe, X, [(-2, h_transposes), (0, first_layer), (1, x2_transposes), (4, attention),
                                   (-2, second_layer)])

            @block.vector
            def _(dve):
                def add_attention(t):
                    q, b = t.slot(X), t.slot(R)
                    dve.wait_ge(sem["a_ps"], t.n + 1)
                    dve.wait_ge(y_in[t.slot(Y)], 16 * (t.uses(Y) + 1))
                    if t.base >= X:
                        dve.wait_ge(sem["o_ok"], t.n + 1 - X)
                    if t.base >= Y:
                        dve.wait_ge(sem["shift1_ok"], t.n + 1 - Y)
                    nc.vector.scalar_tensor_tensor(x1[:, q, :], ps_a[:, b, :], f.m_unscale[:], yb[:, t.slot(Y), :],
                                                   ALU.mult, ALU.add, accum_out=sum1[:, t.slot(Y)]
                                                   ).then_inc(sem["x1_ok"], 1)

                def low_x2(t):
                    b = t.slot(R)
                    dve.wait_ge(sem["xT_hi_ok"], t.n + 1)
                    nc.vector.tensor_tensor(xT_lo[:, b, :], ps_x[:], xT_hi[:, b, :], ALU.subtract
                                            ).then_inc(sem["xT_lo_ok"], 1)

                def hidden(t):
                    b = t.slot(R)
                    dve.wait_ge(sem["z_ps"], t.n + 1)
                    dve.wait_ge(sem["rz_ok"], t.n + 1)
                    if t.base >= R:
                        dve.wait_ge(sem["gelu_ok"], t.n + 1 - R)
                    nc.vector.scalar_tensor_tensor(zb[:, b, :], ps_z[:, 0:ZC], rz[:, t.slot(Y)], f.zbias[:], ALU.mult,
                                                   ALU.add).then_inc(sem["z_ok"], 1)

                def best_two(t):
                    b = t.slot(R)
                    dve.wait_ge(sem["z_ok"], t.n + 1)
                    stand_alone(dve)
                    nc.vector.max(best[:, b, :], zb[:, b, HC:ZC]).then_inc(sem["best_ok"], 1)

                def best_places(t):
                    b = t.slot(R)
                    dve.wait_ge(sem["best_ok"], t.n + 1)
                    stand_alone(dve)
                    nc.vector.max_index(best_at[:, b, :], best[:, b, :], zb[:, b, HC:ZC]
                                        ).then_inc(sem["best_at_ok"], 1)

                def pick(t):
                    b = t.slot(R)
                    dve.wait_ge(sem["share_ok"], t.n * 3 + 3)
                    for n in range(2):
                        nc.vector.tensor_scalar(conf[:, b, n, :], f.iota[:], gate[:, b, n:n + 1],
                                                gate[:, b, 4 + n:5 + n], ALU.is_equal, ALU.mult
                                                ).then_inc(sem["picked_ok"], 1)

                def add_picked(t):
                    b = t.slot(R)
                    dve.wait_ge(sem["picked_ok"], t.n * 2 + 2)
                    nc.vector.tensor_tensor(conf[:, b, 2, :], conf[:, b, 0, :], conf[:, b, 1, :], ALU.add
                                            ).then_inc(sem["conf_ok"], 1)

                def low_confidence(t):
                    b = t.slot(R)
                    dve.wait_ge(sem["conf_hi_ok"], t.n + 1)
                    nc.vector.tensor_tensor(conf3[:, b, 1, :], conf[:, b, 2, :], conf3[:, b, 0, :], ALU.subtract
                                            ).then_inc(sem["conf3_ok"], 1)

                def weigh(t):
                    b = t.slot(R)
                    dve.wait_ge(sem["gelu_ok"], t.n + 1)
                    dve.wait_ge(sem["hconf_ok"], t.n + 1)
                    nc.vector.tensor_tensor(hb[:, b, :].rearrange("p (e j) -> p e j", e=EXPERTS),
                                            hb[:, b, :].rearrange("p (e j) -> p e j", e=EXPERTS),
                                            hconf[:, b, :].unsqueeze(2).to_broadcast([P, EXPERTS, HID]),
                                            ALU.mult).then_inc(sem["h_ok"], 1)

                def low_h(t):
                    b = t.slot(R)
                    dve.wait_ge(sem["hT_hi_ok"], t.n + 1)
                    nc.vector.tensor_tensor(hT_lo[:, b, :], ps_h[:, 0:HC], hT_hi[:, b, :], ALU.subtract
                                            ).then_inc(sem["hT_lo_ok"], 1)

                def add_experts(t):
                    q, b = t.slot(X), t.slot(R)
                    dve.wait_ge(sem["o_ps"], t.n + 1)
                    if t.base >= Y:
                        dve.wait_ge(sem["shift2_ok"], t.n + 1 - Y)
                    nc.vector.scalar_tensor_tensor(x2[:, q, :], ps_o[:, b, :], f.o_unscale[:], x2[:, q, :],
                                                   ALU.mult, ALU.add, accum_out=sum2[:, t.slot(Y)]
                                                   ).then_inc(sem["t_ok"], 1)

                def gain(t):
                    b = t.slot(R)
                    dve.wait_ge(sem["n_ok"], t.n + 1)
                    nc.vector.tensor_tensor(nb[:, b, :], nb[:, b, :], f.gain[:], ALU.mult
                                            ).then_inc(sem["gained_ok"], 1)

                def finish(t):
                    b, q = t.slot(R), t.slot(X)
                    dve.wait_ge(sem["gained_ok"], t.n + 1)
                    dve.wait_ge(sem["offset_ok"], t.n + 1)
                    if t.base >= R:
                        dve.wait_ge(out_done[b], 16 * t.uses(R))
                    nc.vector.tensor_tensor(ob[:, b, :], x1[:, q, :], nb[:, b, :], ALU.add
                                            ).then_inc(sem["o_ok"], 1)

                over_tiles(dve, X, [(-3, add_experts), (-1, pick), (-2, low_h), (-1, add_picked), (0, hidden),
                                    (-5, gain), (0, best_two), (1, low_x2), (0, best_places),
                                    (-1, low_confidence), (-5, finish), (-1, weigh), (3, add_attention)])

            @block.scalar
            def _(act):
                def norm1(t):
                    b, q = t.slot(R), t.slot(X)
                    act.wait_ge(sem["shift1_ok"], t.n + 1)
                    if t.base >= X:
                        act.wait_ge(sem["n_ok"], t.n + 1 - X)
                    nc.scalar.activation(x2[:, q, :], x1[:, q, :], ACT.Identity, bias=shift1[:, b],
                                         scale=rs1[:, b, 0:1]).then_inc(sem["x2_ok"], 1)

                def norm2(t):
                    b, q = t.slot(R), t.slot(X)
                    act.wait_ge(sem["shift2_ok"], t.n + 1)
                    if t.base >= R:
                        act.wait_ge(sem["o_ok"], t.n + 1 - R)
                    nc.scalar.activation(nb[:, b, :], x2[:, q, :], ACT.Identity, bias=shift2[:, b],
                                         scale=rs2[:, b]).then_inc(sem["n_ok"], 1)

                def square1(t):
                    b, q = t.slot(R), t.slot(X)
                    act.wait_ge(sem["x1_ok"], t.n + 1)
                    if t.base >= R:
                        act.wait_ge(sem["var1_ok"], (t.n + 1 - R) * 2)
                    if t.base >= 1:
                        act.wait_ge(sem["ssq1_ok"], t.n)
                    nc.scalar.activation(square[:, 0], x1[:, q, :], ACT.Square, bias=sum1[:, t.slot(Y)],
                                         scale=-float(D), accum_out=ssq1[:, b]).then_inc(sem["ssq1_ok"], 1)

                def square2(t):
                    b, q = t.slot(R), t.slot(X)
                    act.wait_ge(sem["t_ok"], t.n + 1)
                    if t.base >= R:
                        act.wait_ge(sem["var2_ok"], t.n + 1 - R)
                    if t.base >= 1:
                        act.wait_ge(sem["ssq2_ok"], t.n)
                    nc.scalar.activation(square[:, 1], x2[:, q, :], ACT.Square, bias=sum2[:, t.slot(Y)],
                                         scale=-float(D), accum_out=ssq2[:, b]).then_inc(sem["ssq2_ok"], 1)

                def high_x2(t):
                    b = t.slot(R)
                    act.wait_ge(sem["xT_ps"], t.n + 1)
                    if t.base >= R:
                        act.wait_ge(sem["z_ps"], t.n + 1 - R)
                    nc.scalar.activation(xT_hi[:, b, :], ps_x[:], ACT.Copy).then_inc(sem["xT_hi_ok"], 1)

                def gelu(t):
                    b = t.slot(R)
                    act.wait_ge(sem["z_ok"], t.n + 1)
                    if t.base >= R:
                        act.wait_ge(sem["hT_ps"], t.n + 1 - R)
                    nc.scalar.activation(hb[:, b, :], zb[:, b, 0:HC], ACT.Gelu_apprx_tanh
                                         ).then_inc(sem["gelu_ok"], 1)

                def scale_confidence(t):
                    b = t.slot(R)
                    act.wait_ge(sem["conf_ok"], t.n + 1)
                    if t.base >= R:
                        act.wait_ge(sem["h_ok"], t.n + 1 - R)
                    nc.scalar.activation(hconf[:, b, :], conf[:, b, 2, :], ACT.Copy, scale=f.hscale[:]
                                         ).then_inc(sem["hconf_ok"], 1)
                    if t.base >= R:
                        act.wait_ge(sem["hT_ps"], t.n + 1 - R)
                    nc.scalar.activation(conf3[:, b, 0:3:2, :],
                                         conf[:, b, 2, :].unsqueeze(1).to_broadcast([P, 2, EXPERTS]), ACT.Copy
                                         ).then_inc(sem["conf_hi_ok"], 1)

                def tanh(t):
                    b = t.slot(R)
                    act.wait_ge(sem["gap_ok"], t.n + 1)
                    nc.scalar.activation(gate[:, b, 3:4], gate[:, b, 2:3], ACT.Tanh, scale=0.5
                                         ).then_inc(sem["tanh_ok"], 1)

                def high_h(t):
                    b = t.slot(R)
                    act.wait_ge(sem["hT_ps"], t.n + 1)
                    if t.base >= R:
                        act.wait_ge(sem["o_ps"], t.n + 1 - R)
                    nc.scalar.activation(hT_hi[:, b, :], ps_h[:, 0:HC], ACT.Copy).then_inc(sem["hT_hi_ok"], 1)
                    nc.scalar.activation(confT[:, b, :], ps_c[:, 0:P], ACT.Copy).then_inc(sem["confT_ok"], 1)

                over_tiles(act, X, [(-2, high_h), (1, norm1), (2, square1), (1, high_x2),
                                    (-1, scale_confidence), (0, gelu), (-4, norm2), (-3, square2), (0, tanh)])

            @block.gpsimd
            def _(pool):
                def rstd1(t):
                    b = t.slot(R)
                    pool.wait_ge(sem["ssq1_ok"], t.n + 1)
                    if t.base >= R:
                        pool.wait_ge(sem["x2_ok"], t.n + 1 - R)
                    if t.base >= Y:
                        pool.wait_ge(sem["z_ok"], t.n + 1 - Y)
                    stand_alone(pool)
                    small = ACT_SCALE ** -2
                    nc.gpsimd.tensor_scalar(var1[:, b, 0:1], ssq1[:, b], small / D ** 3, EPS * small,
                                            ALU.mult, ALU.add).then_inc(sem["var1_ok"], 1)
                    nc.gpsimd.tensor_scalar(var1[:, b, 1:2], ssq1[:, b], (1 + EPS) * small / D ** 3,
                                            EPS * EPS * small, ALU.mult, ALU.add).then_inc(sem["var1_ok"], 1)
                    pool.wait_ge(sem["var1_ok"], t.n * 2 + 2)
                    nc.gpsimd.tensor_tensor(rs1[:, b, :], var1[:, b, :], f.mhalf2[:], ALU.pow
                                            ).then_inc(sem["rs1_ok"], 1)
                    pool.wait_ge(sem["rs1_ok"], t.n + 1)
                    stand_alone(pool)
                    nc.gpsimd.tensor_scalar(shift1[:, b], sum1[:, t.slot(Y)], rs1[:, b, 0:1], -1.0 / D,
                                            ALU.mult, ALU.mult).then_inc(sem["shift1_ok"], 1)
                    nc.gpsimd.tensor_scalar(ratio[:, b], rs1[:, b, 1:2], rs1[:, b, 0:1], var1[:, b, 0:1],
                                            ALU.mult, ALU.mult).then_inc(sem["ratio_ok"], 1)
                    pool.wait_ge(sem["ratio_ok"], t.n + 1)
                    nc.gpsimd.tensor_tensor(rz[:, t.slot(Y)], ratio[:, b], f.z_unscale[:], ALU.mult
                                            ).then_inc(sem["rz_ok"], 1)

                def shares(t):
                    b = t.slot(R)
                    g = gate[:, b, :]
                    pool.wait_ge(sem["best_ok"], t.n + 1)
                    nc.gpsimd.tensor_tensor(g[:, 2:3], best[:, b, 0:1], best[:, b, 1:2], ALU.subtract
                                            ).then_inc(sem["gap_ok"], 1)
                    pool.wait_ge(sem["best_at_ok"], t.n + 1)
                    stand_alone(pool)
                    nc.gpsimd.tensor_copy(g[:, 0:2], best_at[:, b, 0:2]).then_inc(sem["share_ok"], 1)
                    pool.wait_ge(sem["tanh_ok"], t.n + 1)
                    half = ACT_SCALE / 2
                    stand_alone(pool)
                    nc.gpsimd.tensor_scalar(g[:, 4:5], g[:, 3:4], half, half, ALU.mult, ALU.add
                                            ).then_inc(sem["share_ok"], 1)
                    nc.gpsimd.tensor_scalar(g[:, 5:6], g[:, 3:4], -half, half, ALU.mult, ALU.add
                                            ).then_inc(sem["share_ok"], 1)

                def rstd2(t):
                    b = t.slot(R)
                    pool.wait_ge(sem["ssq2_ok"], t.n + 1)
                    if t.base >= R:
                        pool.wait_ge(sem["n_ok"], t.n + 1 - R)
                    stand_alone(pool)
                    nc.gpsimd.tensor_scalar(var2[:, b], ssq2[:, b], 1.0 / D ** 3, EPS * ACT_SCALE ** 2, ALU.mult,
                                            ALU.add).then_inc(sem["var2_ok"], 1)
                    pool.wait_ge(sem["var2_ok"], t.n + 1)
                    nc.gpsimd.tensor_tensor(rs2[:, b], var2[:, b], keep.mhalf[:], ALU.pow
                                            ).then_inc(sem["rs2_ok"], 1)
                    pool.wait_ge(sem["rs2_ok"], t.n + 1)
                    stand_alone(pool)
                    nc.gpsimd.tensor_scalar(shift2[:, b], sum2[:, t.slot(Y)], rs2[:, b], -1.0 / D, ALU.mult, ALU.mult
                                            ).then_inc(sem["shift2_ok"], 1)

                def offset(t):
                    q = t.slot(X)
                    pool.wait_ge(sem["x2_ok"], t.n + 1)
                    nc.gpsimd.tensor_tensor(x1[:, q, :], x1[:, q, :], f.offset[:], ALU.add
                                            ).then_inc(sem["offset_ok"], 1)

                over_tiles(pool, X, [(-4, rstd2), (0, offset), (2, rstd1), (0, shares)])


class Namespace:
    pass


def program(nc, x, src, dst, gnn_W, gnn_b, W_in, b_in, Wq, Wk, Wv, W_out, b_out, Wg, W1, b1, W2, b2, ln_g, ln_b,
            out_g, out_b, out):
    h_table = nc.dram_tensor("h_table", [N, D], F32).ap()
    y_table = nc.dram_tensor("y_table", [N + SPARE, D], F32).ap()
    dinv_table = nc.dram_tensor("dinv_table", [TILES * P, 1], F32).ap()
    keep, f = Namespace(), Namespace()
    with ExitStack() as st:
        keep.lasting = st.enter_context(ExitStack())
        m = Mem(nc, st, keep.lasting)
        keep.ident = m.sb("ident", [P, P])
        keep.mhalf = m.sb("mhalf", [P, 1])
        keep.one = m.sb("one", [P, 1])
        keep.src = m.sb("src_t", [P, ETILES], I32)
        keep.dst = m.sb("dst_t", [P, ETILES], I32)
        keep.dstf = m.sb("dst_f", [P, ETILES])
        keep.dst_dinv = m.sb("dst_dinv", [P, ETILES])
        keep.padding = m.sb("padding", [P, ETILES])
        keep.target = m.sb("target", [P, ETILES], I32)
        keep.mean = m.sb("mean", [P, TILES])
        keep.rstd = m.sb("rstd", [P, TILES])
        keep.dinv = m.sb("dinv", [P, TILES])
        keep.hcoef = m.sb("hcoef", [P, TILES])
        keep.unscale = m.sb("unscale", [P, 2])
        keep.kmax = m.sb("kmax", [P, QC])
        keep.spare = m.sb("spare", [P, 1])
        keep.rk = m.sb("rk", [P, 2])
        keep.qT_hi = m.sb("qT_hi", [P, TILES, QC], F16)
        keep.qT_lo = m.sb("qT_lo", [P, TILES, QC], F16)
        keep.g = m.sb("g", [P, 2, D])
        keep.earlier = keep.g[:, 1, 0:P]
        f.ident16 = m.sb("ident16", [P, P], F16)
        f.iota = m.sb("iota8", [P, EXPERTS])
        f.hscale = m.sb("hscale", [P, 1])
        f.mhalf2 = m.sb("mhalf2", [P, 2])
        f.m_unscale = m.sb("m_unscale", [P, 1])
        f.z_unscale = m.sb("z_unscale", [P, 1])
        f.o_unscale = m.sb("o_unscale", [P, 1])
        keep.k = m.sb("k_logits", [P, TILES, QC])
        fold_buffers(nc, keep, f, keep.lasting)
        with ExitStack() as st2:
            w2 = Mem(nc, st2, keep.lasting)
            keep.w_hi = w2.sb("w_hi", [P, KD, 2 * D], F16)
            keep.w_lo = w2.sb("w_lo", [P, KD, 2 * D], F16)
            keep.ones_b = w2.sb("ones_b", [64, P], F16)
            keep.bias16 = w2.sb("bias16", [64, D], F16)
            used_sems = prepare(nc, keep, src, dst, gnn_W, W_in, b_in, Wq, Wk, dinv_table, y_table)
            first_pass(nc, keep, x, dst, h_table, y_table, dinv_table)
        second_pass(nc, keep, f, x, dst, h_table, y_table,
                    (W_in, b_in, Wv, W_out, b_out, gnn_b, Wg, W1, b1, W2, b2, ln_g, ln_b, out_g, out_b))
        f.y = m.sb("c_y", [P, Y_SLOTS, D])
        f.y_in = m.sems("c_y_in", Y_SLOTS)
        fold(nc, keep, f, y_table, used_sems)
        third_pass(nc, keep, f, y_table, out)


_INS = ["x", "src", "dst", "L0_gnn_W", "L0_gnn_b", "L0_mix_W_in", "L0_mix_b_in", "L0_mix_Wq", "L0_mix_Wk",
        "L0_mix_Wv", "L0_mix_W_out", "L0_mix_b_out", "L0_ffn_Wg", "L0_ffn_W1", "L0_ffn_b1", "L0_ffn_W2",
        "L0_ffn_b2", "L0_ffn_ln_g", "L0_ffn_ln_b", "L0_ffn_out_g", "L0_ffn_out_b"]


def kernel(**inputs):
    import numpy as np
    import concourse.bacc as bacc
    from concourse.bass_utils import run_bass_kernel_spmd

    nc = bacc.Bacc("TRN2", target_bir_lowering=False, num_devices=1)
    arrays, args = {}, []
    for name in _INS:
        array = np.ascontiguousarray(inputs[name])
        arrays[f"in_{name}"] = array
        args.append(nc.dram_tensor(f"in_{name}", array.shape, mybir.dt.from_np(array.dtype),
                                   kind="ExternalInput").ap())
    out = nc.dram_tensor("out_x", (N, D), F32, kind="ExternalOutput").ap()
    program(nc, *args, out)
    result = run_bass_kernel_spmd(nc, [arrays], core_ids=[0])
    return result.results[0]["out_x"]
```
